# Optimizing a Trainium2 kernel written in Bass

```python
import numpy as np
import jax
import jax.numpy as jnp

def _softmax(x, axis=-1):
    return jax.nn.softmax(x, axis=axis)

def _gelu(x):
    return jax.nn.gelu(x, approximate=True)

def _silu(x):
    return jax.nn.silu(x)

def _sigmoid(x):
    return jax.nn.sigmoid(x)

def _layernorm(x, axis=-1, eps=1e-05):
    m = jnp.mean(x, axis=axis, keepdims=True)
    v = jnp.var(x, axis=axis, keepdims=True)
    return (x - m) / jnp.sqrt(v + eps)

def _scatter_add(tgt, idx, src, axis=0):
    return tgt.at[idx].add(src)

def _segment_sum(src, seg, n):
    return jax.ops.segment_sum(src, seg, n)
kernel_name = 'mk_vit_tower_d2_tok_img256_r4_8f6474'

def setup_inputs(seed: int=0):
    np.random.seed(seed)
    _w = jnp.asarray

    def _rec_inputs():
        import jax
        import jax.numpy as jnp
        _rk = jax.random.key(seed)
        x = -0.0003702 + 0.999946 * jax.random.normal(jax.random.fold_in(_rk, 1), (128, 1, 64, 1000), jnp.float32)
        return x
    x = _rec_inputs()

    def _L0_tok_setup():
        import jax, jax.numpy as jnp
        import numpy as np
        PH, PW = (64, 25)
        SH, SW = (64, 12)

        def _unfold(x, ph, pw, sh, sw):
            B, C, H, W = x.shape
            nh = (H - ph) // sh + 1
            nw = (W - pw) // sw + 1
            rows = jnp.arange(nh)[:, None] * sh + jnp.arange(ph)[None, :]
            cols = jnp.arange(nw)[:, None] * sw + jnp.arange(pw)[None, :]
            p = x[:, :, rows, :]
            p = p[:, :, :, :, cols]
            p = jnp.transpose(p, (0, 2, 4, 1, 3, 5))
            return p.reshape(B, nh * nw, C * ph * pw)
        key = jax.random.key(seed)
        kx, kw = jax.random.split(key, 2)
        x = jax.random.normal(kx, (64, 1, 64, 1000), dtype=jnp.float32)
        in_dim = 1 * PH * PW
        weight = jax.random.normal(kw, (in_dim, 64), dtype=jnp.float32) / np.sqrt(in_dim).astype(np.float32)
        bias = jnp.zeros((64,), dtype=jnp.float32)
        return {'x': x, 'weight': weight, 'bias': bias}
    _L0_tok_all = _L0_tok_setup()
    _L0_tok_in = {k: v for k, v in _L0_tok_all.items() if k in ('weight', 'bias')}
    del _L0_tok_all

    def _L0_attn_setup():
        import jax, jax.numpy as jnp
        import numpy as np
        B, L, D = (4, 1024, 64)
        key = jax.random.key(seed)
        kx, kq, kk, kv, ko = jax.random.split(key, 5)
        std = 0.02
        return {'x': jax.random.normal(kx, (B, L, D), dtype=jnp.float32), 'Wq': std * jax.random.normal(kq, (D, D), dtype=jnp.float32), 'Wk': std * jax.random.normal(kk, (D, D), dtype=jnp.float32), 'Wv': std * jax.random.normal(kv, (D, D), dtype=jnp.float32), 'Wo': std * jax.random.normal(ko, (D, D), dtype=jnp.float32)}
    _L0_attn_all = _L0_attn_setup()
    _L0_attn_in = {k: v for k, v in _L0_attn_all.items() if k in ('Wq', 'Wk', 'Wv', 'Wo')}
    del _L0_attn_all

    def _L0_ffn_setup():
        import jax, jax.numpy as jnp
        import numpy as np
        E, D, H, TOP_K = (6, 64, 64, 2)
        ROUTER_H = D // 2
        key = jax.random.key(seed)
        ks = jax.random.split(key, 12)
        s = 1.0 / np.sqrt(D)
        sh = 1.0 / np.sqrt(H)
        sr = 1.0 / np.sqrt(ROUTER_H)
        return {'features': jax.random.normal(ks[0], (8, 1024, D), dtype=jnp.float32), 'router_w1': jax.random.uniform(ks[1], (D, ROUTER_H), jnp.float32, -s, s), 'router_b1': jnp.zeros((ROUTER_H,), jnp.float32), 'router_w2': jax.random.uniform(ks[2], (ROUTER_H, E), jnp.float32, -sr, sr), 'router_b2': jnp.zeros((E,), jnp.float32), 'expert_w1': jax.random.uniform(ks[3], (E, D, H), jnp.float32, -s, s), 'expert_b1': jnp.zeros((E, H), jnp.float32), 'expert_w2': jax.random.uniform(ks[4], (E, H, H), jnp.float32, -sh, sh), 'expert_b2': jnp.zeros((E, H), jnp.float32), 'expert_w3': jax.random.uniform(ks[5], (E, H, D), jnp.float32, -sh, sh), 'expert_b3': jnp.zeros((E, D), jnp.float32)}
    _L0_ffn_all = _L0_ffn_setup()
    _L0_ffn_in = {k: v for k, v in _L0_ffn_all.items() if k in ('router_w1', 'router_b1', 'router_w2', 'router_b2', 'expert_w1', 'expert_b1', 'expert_w2', 'expert_b2', 'expert_w3', 'expert_b3')}
    del _L0_ffn_all

    def _L1_attn_setup():
        import jax, jax.numpy as jnp
        import numpy as np
        HEAD_SIZE = 64
        HEAD_SIZE_R = HEAD_SIZE // 4
        HEAD_SIZE_C = HEAD_SIZE - HEAD_SIZE_R
        N_EMBD = 64

        def rope(x, start_pos=0):
            B, T, d = x.shape
            half = d // 2
            theta = 1.0 / 10000.0 ** (jnp.arange(half, dtype=x.dtype) / half)
            idx = jnp.arange(start_pos, start_pos + T, dtype=x.dtype)[:, None] * theta[None, :]
            sin, cos = (jnp.sin(idx), jnp.cos(idx))
            xs = x.reshape(B, T, half, 2)
            x1, x2 = (xs[..., 0], xs[..., 1])
            rot = jnp.stack([x1 * cos - x2 * sin, x1 * sin + x2 * cos], axis=-1)
            return rot.reshape(B, T, d)

        def _reference_tuple_inner(x, Wq_comp, Wkv_comp, Wqc, Wqr, Wkc, Wkr, Wv):
            c_q = x @ Wq_comp
            c_kv = x @ Wkv_comp
            q_c = c_q @ Wqc
            q_r = rope(c_q @ Wqr, start_pos=0)
            q = jnp.concatenate([q_c, q_r], axis=-1)
            k_c = c_kv @ Wkc
            k_r = rope(c_kv @ Wkr, start_pos=0)
            k = jnp.concatenate([k_c, k_r], axis=-1)
            v = c_kv @ Wv
            scale = 1.0 / jnp.sqrt(jnp.asarray(HEAD_SIZE, dtype=x.dtype))
            wei = jnp.einsum('bqd,bkd->bqk', q, k) * scale
            T_q = q.shape[1]
            mask = jnp.tril(jnp.ones((T_q, T_q), dtype=bool))
            wei = jnp.where(mask, wei, jnp.asarray(-jnp.inf, dtype=wei.dtype))
            wei = jax.nn.softmax(wei, axis=-1)
            out = jnp.einsum('bqk,bkd->bqd', wei, v)
            return (out, (k, v))
        key = jax.random.key(seed)
        ks = jax.random.split(key, 8)
        B, T = (32, 512)
        s = 0.05
        return {'x': jax.random.normal(ks[0], (B, T, N_EMBD), dtype=jnp.float32), 'Wq_comp': jax.random.normal(ks[1], (N_EMBD, N_EMBD), dtype=jnp.float32) * s, 'Wkv_comp': jax.random.normal(ks[2], (N_EMBD, N_EMBD), dtype=jnp.float32) * s, 'Wqc': jax.random.normal(ks[3], (N_EMBD, HEAD_SIZE_C), dtype=jnp.float32) * s, 'Wqr': jax.random.normal(ks[4], (N_EMBD, HEAD_SIZE_R), dtype=jnp.float32) * s, 'Wkc': jax.random.normal(ks[5], (N_EMBD, HEAD_SIZE_C), dtype=jnp.float32) * s, 'Wkr': jax.random.normal(ks[6], (N_EMBD, HEAD_SIZE_R), dtype=jnp.float32) * s, 'Wv': jax.random.normal(ks[7], (N_EMBD, HEAD_SIZE), dtype=jnp.float32) * s}
    _L1_attn_all = _L1_attn_setup()
    _L1_attn_in = {k: v for k, v in _L1_attn_all.items() if k in ('Wq_comp', 'Wkv_comp', 'Wqc', 'Wqr', 'Wkc', 'Wkr', 'Wv')}
    del _L1_attn_all

    def _L1_ffn_setup():
        import jax, jax.numpy as jnp
        import numpy as np
        NUM_EXPERTS = 8
        TOP_K = 2
        B, S, D = (8, 2048, 64)

        def _moe(tokens, router_w, w1, b1, w2, b2):
            N = tokens.shape[0]
            E = router_w.shape[0]
            logits = tokens.astype(jnp.float32) @ router_w.astype(jnp.float32).T
            probs = jax.nn.softmax(logits, axis=-1)
            rw, re = jax.lax.top_k(probs, TOP_K)
            if TOP_K > 1:
                rw = rw / jnp.maximum(rw.sum(-1, keepdims=True), 1e-12)
            rw = rw.astype(tokens.dtype)
            combine = jnp.zeros((N, E), tokens.dtype).at[jnp.arange(N)[:, None], re].set(rw)
            out = tokens
            for e in range(E):
                h = jax.nn.gelu(tokens @ w1[e] + b1[e], approximate=False)
                y = h @ w2[e] + b2[e]
                out = out + combine[:, e:e + 1] * y
            return out
        key = jax.random.key(seed)
        ks = jax.random.split(key, 4)
        scale = 1.0 / np.sqrt(D).astype(np.float32)
        return {'input_embeddings': jax.random.normal(ks[0], (B, S, D), jnp.float32), 'router_w': jax.random.normal(ks[1], (NUM_EXPERTS, D), jnp.float32) * scale, 'w1': jax.random.normal(ks[2], (NUM_EXPERTS, D, D), jnp.float32) * scale, 'b1': jnp.zeros((NUM_EXPERTS, D), jnp.float32), 'w2': jax.random.normal(ks[3], (NUM_EXPERTS, D, D), jnp.float32) * scale, 'b2': jnp.zeros((NUM_EXPERTS, D), jnp.float32)}
    _L1_ffn_all = _L1_ffn_setup()
    _L1_ffn_in = {k: v for k, v in _L1_ffn_all.items() if k in ('router_w', 'w1', 'b1', 'w2', 'b2')}
    del _L1_ffn_all
    return {'x': x, 'L0_tok_weight': _L0_tok_in['weight'], 'L0_tok_bias': _L0_tok_in['bias'], 'L0_attn_Wq': _L0_attn_in['Wq'], 'L0_attn_Wk': _L0_attn_in['Wk'], 'L0_attn_Wv': _L0_attn_in['Wv'], 'L0_attn_Wo': _L0_attn_in['Wo'], 'L0_ffn_router_w1': _L0_ffn_in['router_w1'], 'L0_ffn_router_b1': _L0_ffn_in['router_b1'], 'L0_ffn_router_w2': _L0_ffn_in['router_w2'], 'L0_ffn_router_b2': _L0_ffn_in['router_b2'], 'L0_ffn_expert_w1': _L0_ffn_in['expert_w1'], 'L0_ffn_expert_b1': _L0_ffn_in['expert_b1'], 'L0_ffn_expert_w2': _L0_ffn_in['expert_w2'], 'L0_ffn_expert_b2': _L0_ffn_in['expert_b2'], 'L0_ffn_expert_w3': _L0_ffn_in['expert_w3'], 'L0_ffn_expert_b3': _L0_ffn_in['expert_b3'], 'L1_attn_Wq_comp': _L1_attn_in['Wq_comp'], 'L1_attn_Wkv_comp': _L1_attn_in['Wkv_comp'], 'L1_attn_Wqc': _L1_attn_in['Wqc'], 'L1_attn_Wqr': _L1_attn_in['Wqr'], 'L1_attn_Wkc': _L1_attn_in['Wkc'], 'L1_attn_Wkr': _L1_attn_in['Wkr'], 'L1_attn_Wv': _L1_attn_in['Wv'], 'L1_ffn_router_w': _L1_ffn_in['router_w'], 'L1_ffn_w1': _L1_ffn_in['w1'], 'L1_ffn_b1': _L1_ffn_in['b1'], 'L1_ffn_w2': _L1_ffn_in['w2'], 'L1_ffn_b2': _L1_ffn_in['b2']}

def reference(x, L0_tok_weight, L0_tok_bias, L0_attn_Wq, L0_attn_Wk, L0_attn_Wv, L0_attn_Wo, L0_ffn_router_w1, L0_ffn_router_b1, L0_ffn_router_w2, L0_ffn_router_b2, L0_ffn_expert_w1, L0_ffn_expert_b1, L0_ffn_expert_w2, L0_ffn_expert_b2, L0_ffn_expert_w3, L0_ffn_expert_b3, L1_attn_Wq_comp, L1_attn_Wkv_comp, L1_attn_Wqc, L1_attn_Wqr, L1_attn_Wkc, L1_attn_Wkr, L1_attn_Wv, L1_ffn_router_w, L1_ffn_w1, L1_ffn_b1, L1_ffn_w2, L1_ffn_b2):
    import jax
    import jax.numpy as jnp

    def _L0_tok_ref(x, weight, bias):
        import jax, jax.numpy as jnp
        import numpy as np
        PH, PW = (64, 25)
        SH, SW = (64, 12)

        def _unfold(x, ph, pw, sh, sw):
            B, C, H, W = x.shape
            nh = (H - ph) // sh + 1
            nw = (W - pw) // sw + 1
            rows = jnp.arange(nh)[:, None] * sh + jnp.arange(ph)[None, :]
            cols = jnp.arange(nw)[:, None] * sw + jnp.arange(pw)[None, :]
            p = x[:, :, rows, :]
            p = p[:, :, :, :, cols]
            p = jnp.transpose(p, (0, 2, 4, 1, 3, 5))
            return p.reshape(B, nh * nw, C * ph * pw)
        p = _unfold(x, PH, PW, SH, SW)
        return jax.nn.gelu(jnp.einsum('bnk,kd->bnd', p, weight) + bias, approximate=False)

    def _L0_attn_ref(x, Wq, Wk, Wv, Wo):
        import jax, jax.numpy as jnp
        import numpy as np
        B, L, D = (4, 1024, 64)
        q = x @ Wq.T
        k = x @ Wk.T
        v = x @ Wv.T
        logits = jnp.einsum('bld,bmd->blm', q, k)
        Lq = x.shape[1]
        causal_mask = jnp.triu(jnp.ones((Lq, Lq), dtype=bool), k=1)
        logits = jnp.where(causal_mask[None], jnp.asarray(0.0, logits.dtype), logits)
        attn = jax.nn.relu(logits)
        row_counts = jnp.maximum(jnp.arange(Lq, dtype=attn.dtype), 1.0)
        attn = attn / row_counts[None, :, None]
        ctx = jnp.einsum('blm,bmd->bld', attn, v)
        return ctx @ Wo.T

    def _L0_ffn_ref(features, router_w1, router_b1, router_w2, router_b2, expert_w1, expert_b1, expert_w2, expert_b2, expert_w3, expert_b3):
        import jax, jax.numpy as jnp
        import numpy as np
        E, D, H, TOP_K = (6, 64, 64, 2)
        ROUTER_H = D // 2
        rh = jax.nn.relu(features @ router_w1 + router_b1)
        expert_logits = jax.nn.softmax(rh @ router_w2 + router_b2, axis=-1)
        top_w, top_i = jax.lax.top_k(expert_logits, TOP_K)
        routing_weights = jax.nn.softmax(top_w, axis=-1)
        h1 = jax.nn.relu(jnp.einsum('bsd,edh->bseh', features, expert_w1) + expert_b1)
        h2 = jax.nn.relu(jnp.einsum('bseh,ehf->bsef', h1, expert_w2) + expert_b2)
        expert_out = jnp.einsum('bsef,efo->bseo', h2, expert_w3) + expert_b3
        sel = jnp.take_along_axis(expert_out, top_i[:, :, :, None], axis=2)
        combined = jnp.sum(sel * routing_weights[..., None], axis=2)
        return combined

    def _L1_attn_ref(x, Wq_comp, Wkv_comp, Wqc, Wqr, Wkc, Wkr, Wv):
        import jax, jax.numpy as jnp
        import numpy as np
        HEAD_SIZE = 64
        HEAD_SIZE_R = HEAD_SIZE // 4
        HEAD_SIZE_C = HEAD_SIZE - HEAD_SIZE_R
        N_EMBD = 64

        def rope(x, start_pos=0):
            B, T, d = x.shape
            half = d // 2
            theta = 1.0 / 10000.0 ** (jnp.arange(half, dtype=x.dtype) / half)
            idx = jnp.arange(start_pos, start_pos + T, dtype=x.dtype)[:, None] * theta[None, :]
            sin, cos = (jnp.sin(idx), jnp.cos(idx))
            xs = x.reshape(B, T, half, 2)
            x1, x2 = (xs[..., 0], xs[..., 1])
            rot = jnp.stack([x1 * cos - x2 * sin, x1 * sin + x2 * cos], axis=-1)
            return rot.reshape(B, T, d)

        def _reference_tuple_inner(x, Wq_comp, Wkv_comp, Wqc, Wqr, Wkc, Wkr, Wv):
            c_q = x @ Wq_comp
            c_kv = x @ Wkv_comp
            q_c = c_q @ Wqc
            q_r = rope(c_q @ Wqr, start_pos=0)
            q = jnp.concatenate([q_c, q_r], axis=-1)
            k_c = c_kv @ Wkc
            k_r = rope(c_kv @ Wkr, start_pos=0)
            k = jnp.concatenate([k_c, k_r], axis=-1)
            v = c_kv @ Wv
            scale = 1.0 / jnp.sqrt(jnp.asarray(HEAD_SIZE, dtype=x.dtype))
            wei = jnp.einsum('bqd,bkd->bqk', q, k) * scale
            T_q = q.shape[1]
            mask = jnp.tril(jnp.ones((T_q, T_q), dtype=bool))
            wei = jnp.where(mask, wei, jnp.asarray(-jnp.inf, dtype=wei.dtype))
            wei = jax.nn.softmax(wei, axis=-1)
            out = jnp.einsum('bqk,bkd->bqd', wei, v)
            return (out, (k, v))
        return _reference_tuple_inner(x, Wq_comp, Wkv_comp, Wqc, Wqr, Wkc, Wkr, Wv)[0]

    def _L1_ffn_ref(input_embeddings, router_w, w1, b1, w2, b2):
        import jax, jax.numpy as jnp
        import numpy as np
        NUM_EXPERTS = 8
        TOP_K = 2
        B, S, D = (8, 2048, 64)

        def _moe(tokens, router_w, w1, b1, w2, b2):
            N = tokens.shape[0]
            E = router_w.shape[0]
            logits = tokens.astype(jnp.float32) @ router_w.astype(jnp.float32).T
            probs = jax.nn.softmax(logits, axis=-1)
            rw, re = jax.lax.top_k(probs, TOP_K)
            if TOP_K > 1:
                rw = rw / jnp.maximum(rw.sum(-1, keepdims=True), 1e-12)
            rw = rw.astype(tokens.dtype)
            combine = jnp.zeros((N, E), tokens.dtype).at[jnp.arange(N)[:, None], re].set(rw)
            out = tokens
            for e in range(E):
                h = jax.nn.gelu(tokens @ w1[e] + b1[e], approximate=False)
                y = h @ w2[e] + b2[e]
                out = out + combine[:, e:e + 1] * y
            return out
        b, s, d = input_embeddings.shape
        tokens = input_embeddings.reshape(b * s, d)
        return _moe(tokens, router_w, w1, b1, w2, b2).reshape(b, s, d)
    h = _L0_tok_ref(x, L0_tok_weight, L0_tok_bias)
    h = h + _L0_attn_ref(_layernorm(h, axis=-1), L0_attn_Wq, L0_attn_Wk, L0_attn_Wv, L0_attn_Wo)
    h = h + _L0_ffn_ref(_layernorm(h, axis=-1), L0_ffn_router_w1, L0_ffn_router_b1, L0_ffn_router_w2, L0_ffn_router_b2, L0_ffn_expert_w1, L0_ffn_expert_b1, L0_ffn_expert_w2, L0_ffn_expert_b2, L0_ffn_expert_w3, L0_ffn_expert_b3)
    h = h + _L1_attn_ref(_layernorm(h, axis=-1), L1_attn_Wq_comp, L1_attn_Wkv_comp, L1_attn_Wqc, L1_attn_Wqr, L1_attn_Wkc, L1_attn_Wkr, L1_attn_Wv)
    h = h + _L1_ffn_ref(_layernorm(h, axis=-1), L1_ffn_router_w, L1_ffn_w1, L1_ffn_b1, L1_ffn_w2, L1_ffn_b2)
    return h

_drawn_inputs = setup_inputs


def setup_inputs(seed=0):
    import zlib

    import numpy as np

    out = dict(_drawn_inputs(seed))
    spreads = {'L0_tok_bias': (0.0, 0.1),
     'L0_ffn_router_b1': (0.0, 0.1),
     'L0_ffn_router_b2': (0.0, 0.1),
     'L0_ffn_expert_b1': (0.0, 0.293),
     'L0_ffn_expert_b2': (0.0, 0.1),
     'L0_ffn_expert_b3': (0.0, 0.1),
     'L1_ffn_b1': (0.0, 0.269),
     'L1_ffn_b2': (0.0, 0.1)}
    factors = {'L0_attn_Wq': 6.473,
     'L0_attn_Wk': 4.902,
     'L0_attn_Wv': 4.53,
     'L0_attn_Wo': 5.148,
     'L1_attn_Wq_comp': 6.825,
     'L1_attn_Wqc': 6.915,
     'L1_attn_Wqr': 8.0,
     'L1_attn_Wkc': 6.346,
     'L1_attn_Wkr': 8.0}
    for name, (base, spread) in spreads.items():
        noise = np.random.default_rng([zlib.crc32(name.encode()), seed]).standard_normal(out[name].shape)
        drawn = base * np.exp(spread * noise) if base else spread * noise
        out[name] = jnp.asarray(drawn.astype(out[name].dtype))
    for name, factor in factors.items():
        out[name] = (out[name] * factor).astype(out[name].dtype)
    return out
```

```python
from contextlib import ExitStack

import concourse.bass as bass
import numpy as np
from concourse import mybir

F32 = mybir.dt.float32
F32R = mybir.dt.float32r
BF16 = mybir.dt.bfloat16
ALU = mybir.AluOpType
ACT = mybir.ActivationFunctionType
AX_X = mybir.AxisListType.X

B = 128
R = 64
T = 1000
PW, SW = 25, 12
L = (T - PW) // SW + 1
D = 64
G = 8
NG = B // G
NPAIR = G // 2
HALF = NPAIR * L
HS_SHIFT = SW // 2
NCH = 2 * HS_SHIFT + 1
E0, E1 = 6, 8
EP = 8
RH = 32
ROPE0 = 48
EPS = 1e-5
BIG = 1e30
LOOP0, LOOP1 = 2, NG - 2


def constants():
    l = np.arange(L)
    count = np.maximum(l, 1).astype(np.float32)
    relu_mask = (l[:, None] <= l[None, :]).astype(np.float32) / count[None, :]
    causal_bias = np.where(l[None, :] <= l[:, None], 0.0, -BIG).astype(np.float32)
    half = (D - ROPE0) // 2
    theta = (np.float32(1.0) / np.power(np.float32(10000.0), np.arange(half, dtype=np.float32) / np.float32(half))).astype(np.float32)
    angle = (np.arange(L, dtype=np.float32)[:, None] * theta[None, :]).astype(np.float32)
    cos, sin = np.cos(angle).astype(np.float32), np.sin(angle).astype(np.float32)
    rope_c, rope_s = np.ones((2, D, L), np.float32), np.zeros((2, D, L), np.float32)
    for i in range(half):
        rope_c[:, ROPE0 + 2 * i] = rope_c[:, ROPE0 + 2 * i + 1] = cos[:, i]
        rope_s[:, ROPE0 + 2 * i] = -sin[:, i]
        rope_s[:, ROPE0 + 2 * i + 1] = sin[:, i]
    out = {
        "c_ident": np.eye(128, dtype=np.float32),
        "c_relu_mask": relu_mask,
        "c_causal_bias": causal_bias,
        "c_rope_c": rope_c.reshape(2 * D, L),
        "c_rope_s": rope_s.reshape(2 * D, L),
    }
    for tag, E in (("0", E0), ("1", E1)):
        sel = np.zeros((3, 3, EP, E // 2, 2, D), np.float32)
        part = np.zeros((3, 3, EP, 3), np.float32)
        for e in range(E):
            sel[:, 0, e, e // 2, e % 2, :] = 1.0
        for j in range(3):
            part[:, j, :, j] = 1.0
        out["c_sel" + tag] = sel.reshape(9 * EP, E // 2 * 2 * D)
        out["c_part" + tag] = part.reshape(9 * EP, 3)
        out["c_first" + tag] = np.tile((E - np.arange(E)).astype(np.float32), (L, 1))
    return out


def in_groups(eng, step):
    for g in range(LOOP0):
        step(g, g % 2)
    with eng.Fori(LOOP0 // 2, LOOP1 // 2) as i:
        for p in (0, 1):
            step(i * 2 + p, p)
    for g in range(LOOP1, NG):
        step(g, g % 2)


def exists(g):
    return not isinstance(g, int) or 0 <= g < NG


def wait(eng, sem, value):
    if not isinstance(value, int) or value > 0:
        eng.wait_ge(sem, value)


class Chain:

    def __init__(self, eng, sem):
        self.eng, self.sem, self.base, self.k, self.per = eng, sem, 0, 0, None

    def __call__(self, ins):
        ins.then_inc(self.sem, 1)
        self.k += 1
        self.eng.wait_ge(self.sem, self.base + self.k)

    def group(self, g):
        if isinstance(g, int):
            if not isinstance(self.base, int):
                self.base, self.k = self.start + (LOOP1 - LOOP0) * self.k, 0
            return
        if isinstance(self.base, int):
            self.start = self.base + self.k
            self.base = self.start + (g - LOOP0) * self.size
        else:
            assert self.k == self.size, (self.k, self.size)
            self.base = self.start + (g - LOOP0) * self.size
        self.k = 0

    def expect(self, size):
        self.size = size
        return self


def slots(t, g):
    return t[:, bass.ds(g * G, G), :]


def slot(t, g, b):
    return t[:, bass.ds(g * G + b, 1), :].rearrange("p a d -> p (a d)")


def column(t, g, b):
    return t[:, bass.ds(g * G + b, 1)]


def build(nc, A, out):
    with ExitStack() as ctx:
        def sb(name, shape, dt=F32):
            return ctx.enter_context(nc.sbuf_tensor(name, shape, dt))

        banks = [ctx.enter_context(nc.psum_tensor(f"bank{i}", [128, 512], F32)) for i in range(8)]

        h = sb("h", [L, B, D])
        stats = sb("stats", [L, B, 6])
        mean = sb("mean", [L, B])
        rstd = sb("rstd", [L, B])
        ident = sb("ident", [128, 128])
        ident16 = sb("ident16", [128, 128], BF16)

        stage_patches(nc, A, banks, sb, h, stats, ident, ident16)
        stage_relu_attention(nc, A, banks, sb, h, stats, mean, rstd, ident)
        stage_moe(nc, A, banks, sb, h, stats, mean, rstd, ident, ident16, 0, None)
        stage_rope_attention(nc, A, banks, sb, h, stats, mean, rstd, ident)
        stage_moe(nc, A, banks, sb, h, stats, mean, rstd, ident, ident16, 1, out)


def stage_patches(nc, A, banks, sb, h, stats, ident, ident16):
    with ExitStack() as ctx:
        def sb(name, shape, dt=F32):
            return ctx.enter_context(nc.sbuf_tensor(name, shape, dt))

        def sem(name):
            return ctx.enter_context(nc.semaphore(name))

        x = A["x"].rearrange("b o r t -> (o r) b t")
        image = [sb(f"image{p}", [128, G, T]) for p in (0, 1)]
        weight = sb("tok_weight", [128, NCH, D])
        bias = sb("tok_bias", [128, 1])
        fm = [sb(f"tok_fm{p}", [128, HALF]) for p in (0, 1)]
        loaded = [[sem(f"image_loaded{p}{q}") for q in (0, 1)] for p in (0, 1)]
        consts = sem("consts_loaded")
        cleared = sem("tok_cleared")
        shifted = sem("image_shifted")
        summed = sem("patches_summed")
        activated = sem("patches_activated")
        turned = sem("patches_turned")
        stored = sem("patches_stored")
        own = sem("patches_own")
        w = A["L0_tok_weight"].rearrange("(r c) d -> r c d", c=PW)
        S = HS_SHIFT
        runs = ((0, 0), (S, 2 * S))
        b1 = A["L0_tok_bias"].rearrange("(d a) -> d a", a=1)

        with nc.Block() as block:
            @block.sync
            def _(sp):
                for g in range(2):
                    for q in (0, 1):
                        sp.dma_start(image[g][0:R, 4 * q:4 * q + 4, :], x[:, G * g + 4 * q:G * g + 4 * q + 4, :]).then_inc(loaded[g][q], 16)

                def step(g, p):
                    if exists(g + 2) and (not isinstance(g, int) or g + 2 < NG):
                        sp.wait_ge(summed, g + 1)
                        for q in (0, 1):
                            sp.dma_start(image[p][0:R, 4 * q:4 * q + 4, :], x[:, bass.ds(g * G + (2 * G + 4 * q), 4), :]).then_inc(loaded[p][q], 16)

                in_groups(sp, step)

            @block.gpsimd
            def _(pool):
                for p in (0, 1):
                    pool.memset(image[p][R:128, :, (L + 1) * SW:T], 0.0).then_inc(cleared, 1)

            @block.scalar
            def _(act):
                for lo, c in runs:
                    act.dma_start(weight[0:R, lo:lo + S, :], w[:, c:c + S, :]).then_inc(consts, 16)
                    act.dma_start(weight[R:128, lo:lo + S, :], w[:, c + S:c + 2 * S, :]).then_inc(consts, 16)
                act.dma_start(weight[0:R, NCH - 1:NCH, :], w[:, PW - 1:PW, :]).then_inc(consts, 16)
                for q in (0, 1):
                    act.dma_start(bias[q * D:(q + 1) * D, :], b1).then_inc(consts, 16)
                act.dma_start(ident[:], A["c_ident"]).then_inc(consts, 16)
                act.wait_ge(consts, 8 * 16)

                def step(g, p):
                    act.wait_ge(summed, g + 1)
                    if not (isinstance(g, int) and g < 2):
                        act.wait_ge(turned, g - 1)
                    act.activation(fm[p][:], banks[p][:, 0:HALF], ACT.Gelu, bias=bias[:]).then_inc(activated, 1)

                in_groups(act, step)

            @block.tensor
            def _(pe):
                pe.wait_ge(consts, 8 * 16)
                pe.wait_ge(own, 1)
                pe.wait_ge(cleared, 2)

                def turn(g, p):
                    pe.wait_ge(activated, g + 1)
                    if not (isinstance(g, int) and g < 2):
                        pe.wait_ge(stored, g - 1)
                    for j in range(NPAIR):
                        mm = pe.transpose(banks[2 + p][0:L, 128 * j:128 * j + 128], fm[p][:, L * j:L * j + L], ident[:])
                    mm.then_inc(turned, 1)

                def step(g, p):
                    pe.wait_ge(shifted, g * 2 + 2)
                    if not (isinstance(g, int) and g < 2):
                        pe.wait_ge(activated, g - 1)
                    for n in range(NCH):
                        t0 = n if n < S else n + S if n < 2 * S else PW - 1
                        for s in (0, 1):
                            mm = pe.matmul(banks[p][s * D:(s + 1) * D, 0:HALF], weight[:, n, :],
                                           image[p][:, s:G:2, t0:t0 + SW * (L - 1) + 1:SW],
                                           start=(n == 0), stop=(n == NCH - 1))
                    mm.then_inc(summed, 1)
                    if not (isinstance(g, int) and g < 1):
                        turn(g - 1, 1 - p)

                in_groups(pe, step)
                turn(NG - 1, (NG - 1) % 2)

            @block.vector
            def _(dve):
                dve.memset(weight[R:128, NCH - 1:NCH, :], 0.0).then_inc(own, 1)
                dve.wait_ge(consts, 8 * 16)
                dve.tensor_copy(ident16[:], ident[:]).then_inc(own, 1)

                def store(g, p):
                    dve.wait_ge(turned, g + 1)
                    dve.tensor_copy(slots(h, g), banks[2 + p][0:L, :].rearrange("p (b d) -> p b d", d=D)).then_inc(stored, 1)
                    dve.wait_ge(stored, g + 1)
                    for b in range(G):
                        dve.bn_stats(slot(stats, g, b), slot(h, g, b))

                def step(g, p):
                    for q in (0, 1):
                        dve.wait_ge(loaded[p][q], (g // 2 if isinstance(g, int) else (g - p) // 2) * 16 + 16)
                        v = image[p][:, 4 * q:4 * q + 4, 0:(L + 1) * SW].rearrange("r b (m c) -> r b m c", c=SW)
                        dve.tensor_copy(v[R:128, :, :, 0:S], v[0:R, :, :, S:SW]).then_inc(shifted, 1)
                    if not (isinstance(g, int) and g < 1):
                        store(g - 1, 1 - p)

                in_groups(dve, step)
                store(NG - 1, (NG - 1) % 2)


def row_scale(nc, dve, act, stats, mean, rstd, tmp, own, rooted):
    if act is not None:
        act.wait_ge(own, 4)
        act.activation(rstd[:], tmp[:, 0, :], ACT.Sqrt).then_inc(rooted, 1)
        return
    even, odd = stats[:, :, 1], stats[:, :, 4]
    var, d, q = tmp[:, 0, :], tmp[:, 1, :], tmp[:, 2, :]
    n = D // 2

    def link(ins, k):
        ins.then_inc(own, 1)
        dve.wait_ge(own, k)

    link(dve.tensor_tensor(d, even, odd, ALU.subtract), 1)
    link(dve.scalar_tensor_tensor(var, d, float(n * n) / D / D, d, ALU.mult, ALU.mult), 2)
    link(dve.tensor_tensor(q, stats[:, :, 2], stats[:, :, 5], ALU.add), 3)
    dve.scalar_tensor_tensor(var, q, 1.0 / D, var, ALU.mult, ALU.add).then_inc(rooted, 1)
    dve.wait_ge(rooted, 1)
    link(dve.tensor_scalar(var, var, EPS, None, ALU.add), 4)
    link(dve.tensor_tensor(d, even, odd, ALU.add), 5)
    link(dve.tensor_scalar(mean[:], d, 0.5, None, ALU.mult), 6)
    dve.wait_ge(rooted, 2)
    link(dve.reciprocal(d, rstd[:]), 7)
    link(dve.tensor_tensor(q, d, d, ALU.mult), 8)
    link(dve.tensor_tensor(q, q, var, ALU.mult), 9)
    link(dve.tensor_scalar(q, q, -0.5, 1.5, ALU.mult, ALU.add), 10)
    link(dve.tensor_tensor(rstd[:], d, q, ALU.mult), 11)


ROW_SCALE_STEPS = 11


def normalise(dve, xn, h, mean, rstd, g, done):
    for b in range(G):
        x = slot(h, g, b)
        if len(xn.shape) == 4:
            x = x.unsqueeze(1).broadcast_to([L, 2, D])
        ins = dve.tensor_scalar(xn[0:L, b], x, column(mean, g, b), column(rstd, g, b), ALU.subtract, ALU.mult)
    ins.then_inc(done, 1)


def stage_relu_attention(nc, A, banks, sb, h, stats, mean, rstd, ident):
    with ExitStack() as ctx:
        def sb(name, shape, dt=F32):
            return ctx.enter_context(nc.sbuf_tensor(name, shape, dt))

        def sem(name):
            return ctx.enter_context(nc.semaphore("ra_" + name))

        raw = sb("ra_raw", [D, 4, D])
        wo_t = sb("ra_wo_t", [D, D])
        w_qk = sb("ra_w_qk", [128, 128])
        w_vo = sb("ra_w_vo", [128, 128])
        mask = sb("ra_mask", [L, L])
        tmp = sb("ra_tmp", [L, 3, B])
        xn = [sb(f"ra_xn{p}", [L, G, D]) for p in (0, 1)]
        xt = [sb(f"ra_xt{p}", [128, HALF]) for p in (0, 1)]
        qz = [sb(f"ra_qz{p}", [128, NPAIR, 2, L]) for p in (0, 1)]
        v = [sb(f"ra_v{p}", [128, NPAIR * 2 * D]) for p in (0, 1)]
        pt = [sb(f"ra_pt{p}", [128, G, L]) for p in (0, 1)]
        x_bank, q_bank, v_bank, s_bank, o_bank = banks[0], banks[1], banks[2], banks[3:5], banks[5]

        loaded, cleared, own, rooted = sem("loaded"), sem("cleared"), sem("own"), sem("rooted")
        w_ps, w_sb = sem("w_ps"), sem("w_sb")
        normed = sem("normed")
        x_turned = sem("x_turned")
        x_ready = sem("x_ready")
        q_done = sem("q_done")
        v_done = sem("v_done")
        q_low = sem("q_low")
        q_high = sem("q_high")
        v_ready = sem("v_ready")
        scored = sem("scored")
        weighed = sem("weighed")
        mixed = sem("mixed")
        added = sem("added")

        with nc.Block() as block:
            @block.sync
            def _(sp):
                for i, n in enumerate(("L0_attn_Wq", "L0_attn_Wk", "L0_attn_Wv", "L0_attn_Wo")):
                    sp.dma_start(raw[:, i, :], A[n]).then_inc(loaded, 16)
                sp.dma_start(mask[:], A["c_relu_mask"]).then_inc(loaded, 16)

            @block.gpsimd
            def _(pool):
                for t in (w_qk, w_vo, *qz, *v, *pt):
                    pool.memset(t[:], 0.0).then_inc(cleared, 1)

            @block.scalar
            def _(act):
                row_scale(nc, None, act, stats, mean, rstd, tmp, own, rooted)
                act.wait_ge(cleared, 8)

                def copy_x(g, p):
                    act.wait_ge(x_turned, g + 1)
                    act.activation(xt[p][:], x_bank[:, 0:HALF], ACT.Copy).then_inc(x_ready, 1)

                def copy_qv(g, p):
                    act.wait_ge(q_done, g + 1)
                    wait(act, scored, 2 * g - 2)
                    act.activation(qz[p][0:D, :, 0, :], q_bank[0:D, 0:HALF].rearrange("p (j l) -> p j l", l=L), ACT.Copy).then_inc(q_low, 1)
                    act.wait_ge(v_done, g + 1)
                    wait(act, mixed, g - 1)
                    act.activation(v[p][0:L, :], v_bank[0:L, :], ACT.Copy).then_inc(v_ready, 1)

                copy_x(0, 0)
                copy_x(1, 1)
                copy_qv(0, 0)

                def step(g, p):
                    if exists(g + 2):
                        copy_x(g + 2, p)
                    if exists(g + 1):
                        copy_qv(g + 1, 1 - p)

                in_groups(act, step)

            @block.tensor
            def _(pe):
                pe.wait_ge(loaded, 5 * 16)
                pe.transpose(x_bank[0:D, 0:D], raw[:, 3, :], ident[0:D, 0:D]).then_inc(w_ps, 1)
                for s in (0, 1):
                    mm = pe.matmul(q_bank[s * D:(s + 1) * D, s * D:(s + 1) * D], raw[:, 0, :], raw[:, 1, :], start=True, stop=True)
                mm.then_inc(w_ps, 1)
                pe.wait_ge(w_sb, 1)
                for s in (0, 1):
                    mm = pe.matmul(v_bank[s * D:(s + 1) * D, s * D:(s + 1) * D], raw[:, 2, :], wo_t[:], start=True, stop=True)
                mm.then_inc(w_ps, 1)
                pe.wait_ge(w_sb, 5)

                def turn(g, p):
                    pe.wait_ge(normed, g + 1)
                    wait(pe, x_ready, g)
                    for j in range(NPAIR):
                        mm = pe.transpose(x_bank[:, L * j:L * j + L], xn[p][:, 2 * j:2 * j + 2, :], ident[0:L, 0:L])
                    mm.then_inc(x_turned, 1)

                def project(g, p):
                    pe.wait_ge(x_ready, g + 1)
                    wait(pe, q_low, g)
                    wait(pe, q_high, g)
                    pe.matmul(q_bank[:, 0:HALF], w_qk[:], xt[p][:], start=True, stop=True).then_inc(q_done, 1)
                    wait(pe, v_ready, g)
                    for j in range(NPAIR):
                        mm = pe.matmul(v_bank[0:L, 128 * j:128 * j + 128], xt[p][:, L * j:L * j + L], w_vo[:], start=True, stop=True)
                    mm.then_inc(v_done, 1)

                turn(0, 0)
                turn(1, 1)
                project(0, 0)

                def step(g, p):
                    pe.wait_ge(q_low, g + 1)
                    pe.wait_ge(q_high, g + 1)
                    for c in (0, 1):
                        wait(pe, weighed, 2 * g - 1 + c)
                        for j in (2 * c, 2 * c + 1):
                            mm = pe.matmul(s_bank[c][0:L, (j % 2) * 2 * L:(j % 2 + 1) * 2 * L], xt[p][:, L * j:L * j + L],
                                           qz[p][:, j, :, :], start=True, stop=True)
                        mm.then_inc(scored, 1)
                    if exists(g + 2):
                        turn(g + 2, p)
                    if exists(g + 1):
                        project(g + 1, 1 - p)
                    pe.wait_ge(v_ready, g + 1)
                    pe.wait_ge(weighed, 2 * g + 2)
                    wait(pe, added, g)
                    for b in range(G):
                        mm = pe.matmul(o_bank[0:L, D * b:D * b + D], pt[p][:, b, :], v[p][:, D * b:D * b + D], start=True, stop=True)
                    mm.then_inc(mixed, 1)

                in_groups(pe, step)

            @block.vector
            def _(dve):
                row_scale(nc, dve, None, stats, mean, rstd, tmp, own, rooted)
                normalise(dve, xn[0], h, mean, rstd, 0, normed)
                normalise(dve, xn[1], h, mean, rstd, 1, normed)
                dve.wait_ge(cleared, 8)
                dve.wait_ge(w_ps, 1)
                dve.tensor_copy(wo_t[:], x_bank[0:D, 0:D]).then_inc(w_sb, 1)
                for bank, t, n in ((q_bank, w_qk, 2), (v_bank, w_vo, 3)):
                    dve.wait_ge(w_ps, n)
                    for s in (0, 1):
                        dve.tensor_copy(t[s * D:(s + 1) * D, s * D:(s + 1) * D], bank[s * D:(s + 1) * D, s * D:(s + 1) * D]).then_inc(w_sb, 1)
                dve.wait_ge(loaded, 5 * 16)

                def copy_q(g, p):
                    dve.wait_ge(q_done, g + 1)
                    wait(dve, scored, 2 * g - 2)
                    dve.tensor_copy(qz[p][D:128, :, 1, :], q_bank[D:128, 0:HALF].rearrange("p (j l) -> p j l", l=L)).then_inc(q_high, 1)

                copy_q(0, 0)

                def step(g, p):
                    if exists(g + 2):
                        dve.wait_ge(x_turned, g + 1)
                        normalise(dve, xn[p], h, mean, rstd, g + 2, normed)
                    for c in (0, 1):
                        dve.wait_ge(scored, 2 * g + 1 + c)
                        wait(dve, mixed, g - 1)
                        dve.scalar_tensor_tensor(
                            pt[p][0:L, NPAIR * c:NPAIR * c + NPAIR, :], s_bank[c][0:L, 0:HALF].rearrange("p (b l) -> p b l", l=L), 0.0,
                            mask[:].unsqueeze(1).broadcast_to([L, NPAIR, L]), ALU.max, ALU.mult).then_inc(weighed, 1)
                    if exists(g + 1):
                        copy_q(g + 1, 1 - p)
                    dve.wait_ge(mixed, g + 1)
                    dve.tensor_tensor(slots(h, g), o_bank[0:L, :].rearrange("p (b d) -> p b d", d=D), slots(h, g), ALU.add).then_inc(added, 1)
                    dve.wait_ge(added, g + 1)
                    for b in range(G):
                        dve.bn_stats(slot(stats, g, b), slot(h, g, b))

                in_groups(dve, step)


def stage_rope_attention(nc, A, banks, sb, h, stats, mean, rstd, ident):
    with ExitStack() as ctx:
        def sb(name, shape, dt=F32):
            return ctx.enter_context(nc.sbuf_tensor(name, shape, dt))

        def sem(name):
            return ctx.enter_context(nc.semaphore("sa_" + name))

        comp = sb("sa_comp", [D, 2, D])
        comp_t = sb("sa_comp_t", [D, 2, D])
        heads = sb("sa_heads", [D, 3, D])
        w = sb("sa_w", [128, 5, 128])
        rope = sb("sa_rope", [128, 2, L])
        bias = sb("sa_bias", [L, L])
        tmp = sb("sa_tmp", [L, 3, B])
        xn = [sb(f"sa_xn{p}", [L, G, D]) for p in (0, 1)]
        xt = [sb(f"sa_xt{p}", [128, HALF]) for p in (0, 1)]
        turn_c = sb("sa_turn_c", [128, 2, NPAIR, L])
        turn_s = sb("sa_turn_s", [128, 2, NPAIR, L])
        q = [sb(f"sa_q{p}", [128, NPAIR, L]) for p in (0, 1)]
        kz = [sb(f"sa_kz{p}", [128, NPAIR, 2, L]) for p in (0, 1)]
        v = [sb(f"sa_v{p}", [128, NPAIR * 2 * D]) for p in (0, 1)]
        masked = sb("sa_masked", [L, G, L])
        top = sb("sa_top", [L, G])
        low = sb("sa_low", [L, G])
        prob = sb("sa_prob", [L, G, L])
        total = sb("sa_total", [L, G])
        share = sb("sa_share", [L, G])
        pt = [sb(f"sa_pt{p}", [128, G, L]) for p in (0, 1)]
        mixed_sb = sb("sa_mixed", [L, G, D])
        xo_bank, v_bank = banks[0], banks[1]
        qk_bank, sw_bank, s_bank = banks[2:4], banks[4:6], banks[6:8]
        p_bank = sw_bank

        loaded, cleared, own, rooted = sem("loaded"), sem("cleared"), sem("own"), sem("rooted")
        w_ps, w_sb = sem("w_ps"), sem("w_sb")
        normed = sem("normed")
        x_turned = sem("x_turned")
        x_ready = sem("x_ready")
        qk_done = sem("qk_done")
        sw_done = sem("sw_done")
        v_done = sem("v_done")
        v_ready = sem("v_ready")
        cos_done = sem("cos_done")
        sin_done = sem("sin_done")
        rotated = sem("rotated")
        scored = sem("scored")
        biased = sem("biased")
        topped = sem("topped")
        shifted = sem("shifted")
        raised = sem("raised")
        p_turned = sem("p_turned")
        p_ready = sem("p_ready")
        mixed = sem("mixed")
        shared = sem("shared")
        scaled = sem("scaled")
        added = sem("added")
        SCALE = float(D) ** -0.5

        with nc.Block() as block:
            @block.sync
            def _(sp):
                for i, n in enumerate(("L1_attn_Wq_comp", "L1_attn_Wkv_comp")):
                    sp.dma_start(comp[:, i, :], A[n]).then_inc(loaded, 16)
                for i, n in enumerate(("L1_attn_Wqc", "L1_attn_Wkc")):
                    sp.dma_start(heads[:, i, 0:ROPE0], A[n]).then_inc(loaded, 16)
                for i, n in enumerate(("L1_attn_Wqr", "L1_attn_Wkr")):
                    sp.dma_start(heads[:, i, ROPE0:D], A[n]).then_inc(loaded, 16)
                sp.dma_start(heads[:, 2, :], A["L1_attn_Wv"]).then_inc(loaded, 16)
                sp.dma_start(rope[:, 0, :], A["c_rope_c"]).then_inc(loaded, 16)
                sp.dma_start(rope[:, 1, :], A["c_rope_s"]).then_inc(loaded, 16)
                sp.dma_start(bias[:], A["c_causal_bias"]).then_inc(loaded, 16)

            @block.gpsimd
            def _(pool):
                for t in (w, *kz, *v, *pt):
                    pool.memset(t[:], 0.0).then_inc(cleared, 1)
                pool.wait_ge(cleared, 7)

                def rotate(g, p):
                    pool.wait_ge(cos_done, g + 1)
                    pool.wait_ge(sin_done, g + 1)
                    wait(pool, scored, 2 * g - 2)
                    pool.tensor_tensor(q[p][:], turn_c[:, 0], turn_s[:, 0], ALU.add).then_inc(rotated, 1)
                    pool.wait_ge(rotated, 3 * g + 1)
                    for s in (0, 1):
                        ins = pool.tensor_tensor(kz[p][s * D:(s + 1) * D, :, s, :], turn_c[s * D:(s + 1) * D, 1],
                                                 turn_s[s * D:(s + 1) * D, 1], ALU.add)
                        ins.then_inc(rotated, 1)

                rotate(0, 0)

                def step(g, p):
                    if exists(g + 1):
                        rotate(g + 1, 1 - p)

                in_groups(pool, step)

            @block.scalar
            def _(act):
                row_scale(nc, None, act, stats, mean, rstd, tmp, own, rooted)
                act.wait_ge(cleared, 7)

                def copy_x(g, p):
                    act.wait_ge(x_turned, g + 1)
                    act.activation(xt[p][:], xo_bank[:, 0:HALF], ACT.Copy).then_inc(x_ready, 1)

                def copy_v(g, p):
                    act.wait_ge(v_done, g + 1)
                    wait(act, mixed, g - 1)
                    act.activation(v[p][0:L, :], v_bank[0:L, :], ACT.Copy).then_inc(v_ready, 1)

                copy_x(0, 0)
                copy_x(1, 1)
                copy_v(0, 0)

                def step(g, p):
                    if exists(g + 2):
                        copy_x(g + 2, p)
                    act.wait_ge(shifted, g + 1)
                    wait(act, p_turned, g)
                    wait(act, shared, g)
                    for b in range(G):
                        act.activation(prob[:, b, :], masked[:, b, :], ACT.Exp, bias=low[:, b:b + 1], scale=SCALE,
                                       accum_out=total[:, b:b + 1]).then_inc(raised, 1)
                    if exists(g + 1):
                        copy_v(g + 1, 1 - p)
                    act.wait_ge(p_turned, g + 1)
                    wait(act, mixed, g - 1)
                    for c in (0, 1):
                        act.activation(pt[p][0:L, NPAIR * c:NPAIR * c + NPAIR, :], p_bank[c][0:L, 0:HALF].rearrange("p (b l) -> p b l", l=L),
                                       ACT.Copy).then_inc(p_ready, 1)

                in_groups(act, step)

            @block.tensor
            def _(pe):
                pe.wait_ge(loaded, 10 * 16)
                for i in (0, 1):
                    mm = pe.transpose(xo_bank[0:D, D * i:D * i + D], comp[:, i, :], ident[0:D, 0:D])
                mm.then_inc(w_ps, 1)
                pe.wait_ge(w_sb, 1)
                for i in range(3):
                    for s in (0, 1):
                        mm = pe.matmul(v_bank[s * D:(s + 1) * D, D * i:D * i + D], comp_t[:, min(i, 1), :], heads[:, i, :], start=True, stop=True)
                mm.then_inc(w_ps, 1)
                pe.wait_ge(w_sb, 15)

                def turn(g, p):
                    pe.wait_ge(normed, g + 1)
                    wait(pe, x_ready, g)
                    if not (isinstance(g, int) and g < 3):
                        pe.wait_ge(scaled, g - 2)
                    for j in range(NPAIR):
                        mm = pe.transpose(xo_bank[:, L * j:L * j + L], xn[p][:, 2 * j:2 * j + 2, :], ident[0:L, 0:L])
                    mm.then_inc(x_turned, 1)

                def project(g, p):
                    pe.wait_ge(x_ready, g + 1)
                    wait(pe, cos_done, g)
                    for i in (0, 1):
                        mm = pe.matmul(qk_bank[i][:, 0:HALF], w[:, i, :], xt[p][:], start=True, stop=True)
                    mm.then_inc(qk_done, 1)
                    wait(pe, sin_done, g)
                    wait(pe, p_ready, 2 * g - 2)
                    for i in (0, 1):
                        mm = pe.matmul(sw_bank[i][:, 0:HALF], w[:, 2 + i, :], xt[p][:], start=True, stop=True)
                    mm.then_inc(sw_done, 1)
                    wait(pe, v_ready, g)
                    for j in range(NPAIR):
                        mm = pe.matmul(v_bank[0:L, 128 * j:128 * j + 128], xt[p][:, L * j:L * j + L], w[:, 4, :], start=True, stop=True)
                    mm.then_inc(v_done, 1)

                turn(0, 0)
                turn(1, 1)
                project(0, 0)

                def step(g, p):
                    pe.wait_ge(rotated, 3 * g + 3)
                    for c in (0, 1):
                        wait(pe, biased, 2 * g - 1 + c)
                        for j in (2 * c, 2 * c + 1):
                            mm = pe.matmul(s_bank[c][0:L, (j % 2) * 2 * L:(j % 2 + 1) * 2 * L], q[p][:, j, :],
                                           kz[p][:, j, :, :], start=True, stop=True)
                        mm.then_inc(scored, 1)
                    if exists(g + 2):
                        turn(g + 2, p)
                    if exists(g + 1):
                        project(g + 1, 1 - p)
                        pe.wait_ge(sin_done, g + 2)
                    pe.wait_ge(raised, G * g + G)
                    for b in range(G):
                        mm = pe.transpose(p_bank[b // NPAIR][0:L, L * (b % NPAIR):L * (b % NPAIR) + L], prob[:, b, :], ident[0:L, 0:L])
                    mm.then_inc(p_turned, 1)
                    pe.wait_ge(v_ready, g + 1)
                    pe.wait_ge(p_ready, 2 * g + 2)
                    if exists(g + 2):
                        pe.wait_ge(x_ready, g + 3)
                    wait(pe, scaled, g)
                    for b in range(G):
                        mm = pe.matmul(xo_bank[0:L, D * b:D * b + D], pt[p][:, b, :], v[p][:, D * b:D * b + D], start=True, stop=True)
                    mm.then_inc(mixed, 1)

                in_groups(pe, step)

            @block.vector
            def _(dve):
                row_scale(nc, dve, None, stats, mean, rstd, tmp, own, rooted)
                normalise(dve, xn[0], h, mean, rstd, 0, normed)
                normalise(dve, xn[1], h, mean, rstd, 1, normed)
                dve.wait_ge(cleared, 7)
                dve.wait_ge(w_ps, 1)
                dve.tensor_copy(comp_t[:], xo_bank[0:D, 0:2 * D].rearrange("p (i d) -> p i d", d=D)).then_inc(w_sb, 1)
                dve.wait_ge(w_ps, 2)
                for s in (0, 1):
                    rows, cols = slice(s * D, (s + 1) * D), slice(s * D, (s + 1) * D)
                    for i, at in ((0, 0), (1, 1), (2, 4)):
                        dve.tensor_copy(w[rows, at, cols], v_bank[rows, D * i:D * i + D]).then_inc(w_sb, 1)
                    for i in (0, 1):
                        for a in (0, 1):
                            dve.tensor_copy(w[rows, 2 + i, s * D + ROPE0 + a:(s + 1) * D:2],
                                            v_bank[rows, D * i + ROPE0 + 1 - a:D * i + D:2]).then_inc(w_sb, 1)
                dve.wait_ge(loaded, 10 * 16)

                def rope_parts(g, p):
                    dve.wait_ge(qk_done, g + 1)
                    wait(dve, rotated, 3 * g)
                    for i in (0, 1):
                        ins = dve.tensor_tensor(turn_c[:, i], qk_bank[i][:, 0:HALF].rearrange("p (j l) -> p j l", l=L),
                                                rope[:, 0, :].unsqueeze(1).broadcast_to([128, NPAIR, L]), ALU.mult)
                    ins.then_inc(cos_done, 1)
                    dve.wait_ge(sw_done, g + 1)
                    for i in (0, 1):
                        ins = dve.tensor_tensor(turn_s[:, i], sw_bank[i][:, 0:HALF].rearrange("p (j l) -> p j l", l=L),
                                                rope[:, 1, :].unsqueeze(1).broadcast_to([128, NPAIR, L]), ALU.mult)
                    ins.then_inc(sin_done, 1)

                rope_parts(0, 0)

                def step(g, p):
                    if exists(g + 2):
                        dve.wait_ge(x_turned, g + 1)
                        normalise(dve, xn[p], h, mean, rstd, g + 2, normed)
                    wait(dve, raised, G * g)
                    for c in (0, 1):
                        dve.wait_ge(scored, 2 * g + 1 + c)
                        dve.tensor_tensor(masked[:, NPAIR * c:NPAIR * c + NPAIR, :], s_bank[c][0:L, 0:HALF].rearrange("p (b l) -> p b l", l=L),
                                          bias[:].unsqueeze(1).broadcast_to([L, NPAIR, L]), ALU.add).then_inc(biased, 1)
                    dve.wait_ge(biased, 2 * g + 2)
                    dve.tensor_reduce(top[:], masked[:], AX_X, ALU.max).then_inc(topped, 1)
                    dve.wait_ge(topped, g + 1)
                    dve.tensor_scalar(low[:], top[:], -SCALE, None, ALU.mult).then_inc(shifted, 1)
                    if exists(g + 1):
                        rope_parts(g + 1, 1 - p)
                    dve.wait_ge(raised, G * g + G)
                    dve.reciprocal(share[:], total[:]).then_inc(shared, 1)
                    dve.wait_ge(shared, g + 1)
                    dve.wait_ge(mixed, g + 1)
                    dve.tensor_tensor(mixed_sb[:], xo_bank[0:L, :].rearrange("p (b d) -> p b d", d=D),
                                      share[:].unsqueeze(2).broadcast_to([L, G, D]), ALU.mult).then_inc(scaled, 1)
                    dve.wait_ge(scaled, g + 1)
                    dve.tensor_tensor(slots(h, g), mixed_sb[:], slots(h, g), ALU.add).then_inc(added, 1)
                    dve.wait_ge(added, g + 1)
                    for b in range(G):
                        dve.bn_stats(slot(stats, g, b), slot(h, g, b))

                in_groups(dve, step)


def stage_moe(nc, A, banks, sb, h, stats, mean, rstd, ident, ident16, layer, out):
    last = layer == 1
    E = E1 if last else E0
    NP = E // 2
    U = 2 * NP
    NR = 9 * EP
    with ExitStack() as ctx:
        def sb(name, shape, dt=F32):
            return ctx.enter_context(nc.sbuf_tensor(f"m{layer}_{name}", shape, dt))

        def sem(name):
            return ctx.enter_context(nc.semaphore(f"m{layer}_{name}"))

        w1_raw = sb("w1_raw", [128, E, D])
        w1_hi, w1_lo = sb("w1_hi", [128, E, D], F32R), sb("w1_lo", [128, E, D], F32R)
        b1 = sb("b1", [128, NP])
        RC = D if last else 128
        wr_raw = sb("wr_raw", [128, RC])
        wr_hi, wr_lo = sb("wr_hi", [128, RC], F32R), sb("wr_lo", [128, RC], F32R)
        wo = sb("wo", [128, NP, D])
        bo_raw, bo_rest = sb("bo_raw", [NR, D]), sb("bo_rest", [NR, D])
        bo_part = sb("bo_part", [NR, D], BF16)
        bo_sum = sb("bo_sum", [NR, D])
        bo = sb("bo", [128, D], BF16)
        part = sb("part", [NR, 3])
        sel_raw = sb("sel_raw", [NR, NP * 128])
        sel = sb("sel", [128, NP * 128], BF16)
        first = sb("first", [L, E])
        if not last:
            w2 = sb("w2", [128, NP, 128])
            b2 = sb("b2", [128, NP])
            br1 = sb("br1", [RH, 1])
            wr2 = sb("wr2", [128, D])
            rh = sb("rh", [128, G, L])
        else:
            router_rows = sb("router_rows", [E, D])
        tmp = sb("tmp", [L, 3, B])
        xn = [sb(f"xn{p}", [L, G, 2, D]) for p in (0, 1)]
        xs = [sb(f"xs{p}", [128, G, L], F32R) for p in (0, 1)]
        ct = [sb(f"ct{p}", [128, G, L], BF16) for p in (0, 1)]
        h1 = [sb(f"h1_{n}", [128, HALF]) for n in (0, 1)]
        h2 = [sb(f"h2_{n}", [128, HALF]) for n in (0, 1)]
        hm = [sb(f"hm{u}", [128, HALF]) for u in range(U)]
        osb = sb("osb", [128, HALF])
        lg, ev, idx = sb("lg", [L, G, E]), sb("ev", [L, G, E]), sb("idx", [L, G, E])
        s1, s2 = sb("s1", [L, G, E]), sb("s2", [L, G, E])
        cw, rest = sb("cw", [L, G, E]), sb("rest", [L, G, E])
        small = sb("small", [L, 8, G])
        cp = [sb(f"cp{p}", [L, G, 3, 3, EP], BF16) for p in (0, 1)]
        fin = [sb(f"fin{p}", [L, G, D]) for p in (0, 1)] if last else None

        a_bank, o_bank = banks[0:2], banks[2]
        h1_bank, cb_bank = banks[3:5], banks[5:7]
        h2_bank = banks[7]

        loaded, cleared, own, rooted = sem("loaded"), sem("cleared"), sem("own"), sem("rooted")
        prepared = sem("prepared")
        normed = sem("normed")
        carried = sem("carried")
        x_turned = sem("x_turned")
        x_high = sem("x_high")
        x_ready = sem("x_ready")
        r_done = sem("r_done")
        r_ready = sem("r_ready")
        routed = sem("routed")
        lg_read = sem("lg_read")
        exp_in, exp_out = sem("exp_in"), sem("exp_out")
        cp_ready = sem("cp_ready")
        c_turned = sem("c_turned")
        c_ready = sem("c_ready")
        h1_done, h1_ready = sem("h1_done"), sem("h1_ready")
        h2_done, h2_ready = sem("h2_done"), sem("h2_ready")
        cb_done = sem("cb_done")
        hm_ready = sem("hm_ready")
        o_pairs = sem("o_pairs")
        o_done = sem("o_done")
        o_ready = sem("o_ready")
        o_turned = sem("o_turned")
        added = sem("added")
        chain = sem("chain")
        sent = [sem(f"sent{p}") for p in (0, 1)] if last else None

        pre = "L1_ffn_" if last else "L0_ffn_"
        w_in = A["L1_ffn_w1"] if last else A["L0_ffn_expert_w1"]
        b_in = A["L1_ffn_b1"] if last else A["L0_ffn_expert_b1"]
        w_out = A["L1_ffn_w2"] if last else A["L0_ffn_expert_w3"]
        b_out = A["L1_ffn_b2"] if last else A["L0_ffn_expert_b3"]
        LAST = U - 1
        R_A, R_B, RES = 3, 4, 5
        n_clear = 10 if last else 12

        with nc.Block() as block:
            @block.sync
            def _(sp):
                n = [0]

                def load(dst, src):
                    n[0] += 1
                    sp.dma_start(dst, src).then_inc(loaded, 16)

                sp.wait_ge(cleared, n_clear)
                with nc.allow_non_contiguous_dma(reason="small biases"):
                    for s in (0, 1):
                        load(w1_raw[s * D:(s + 1) * D, :, :], w_in.rearrange("e d h -> d e h"))
                        load(b1[s * D:(s + 1) * D, :], b_in.rearrange("(k e) h -> e h k", e=2)[s])
                    for s in (0, 1):
                        load(wo[s * D:(s + 1) * D, :, :], w_out.rearrange("(k e) h d -> e h k d", e=2)[s])
                    for i in range(9):
                        load(bo_raw[i * EP:i * EP + E, :], b_out)
                    load(part[:], A[f"c_part{layer}"])
                    load(sel_raw[:], A[f"c_sel{layer}"])
                    load(first[:], A[f"c_first{layer}"])
                    if last:
                        load(router_rows[:], A["L1_ffn_router_w"])
                    else:
                        for s in (0, 1):
                            load(wr_raw[s * D:(s + 1) * D, 0:RH], A["L0_ffn_router_w1"])
                            load(b2[s * D:(s + 1) * D, :], A["L0_ffn_expert_b2"].rearrange("(k e) h -> e h k", e=2)[s])
                        for e in range(E):
                            s = e % 2
                            load(w2[s * D:(s + 1) * D, e // 2, s * D:(s + 1) * D], A["L0_ffn_expert_w2"][e])
                        load(br1[:], A["L0_ffn_router_b1"].rearrange("(r a) -> r a", a=1))
                        load(wr2[0:RH, 0:E], A["L0_ffn_router_w2"])
                        load(wr2[RH:RH + 1, 0:E], A["L0_ffn_router_b2"].rearrange("(a e) -> a e", a=1))
                assert n[0] == N_LOADS[layer], n[0]
                if last:
                    dst = out.rearrange("b l d -> l b d")

                    def step(g, p):
                        sp.wait_ge(added, g + 1)
                        sp.dma_start(dst[:, bass.ds(g * G, G), :], fin[p][:]).then_inc(sent[p], 16)

                    in_groups(sp, step)
                    for p in (0, 1):
                        sp.wait_ge(sent[p], NG // 2 * 16)

            @block.gpsimd
            def _(pool):
                for t in (wr_raw, bo, bo_raw, sel, *ct, *cp) + (() if last else (w2, wr2, rh)):
                    pool.memset(t[:], 0.0).then_inc(cleared, 1)
                if last:
                    for p in (0, 1):
                        pool.memset(fin[p][:], 0.0).then_inc(cleared, 1)
                else:
                    pool.wait_ge(cleared, 11)
                    pool.memset(rh[RH:RH + 1, :, :], 1.0).then_inc(cleared, 1)
                if last:
                    def step(g, p):
                        pool.wait_ge(normed, g + 1)
                        pool.tensor_tensor(slots(h, g), xn[p][:, :, 0, :], slots(h, g), ALU.add).then_inc(carried, 1)

                    in_groups(pool, step)

            @block.scalar
            def _(act):
                row_scale(nc, None, act, stats, mean, rstd, tmp, own, rooted)
                act.wait_ge(loaded, N_LOADS[layer] * 16)

                def high(g, p):
                    for c in (0, 1):
                        act.wait_ge(x_turned, 2 * g + 1 + c)
                        act.activation(xs[p][:, NPAIR * c:NPAIR * c + NPAIR, :], a_bank[c][:, 0:HALF].rearrange("p (b l) -> p b l", l=L),
                                       ACT.Copy).then_inc(x_high, 1)

                def router_hidden(g, p):
                    for c in (0, 1):
                        act.wait_ge(r_done, 2 * g + 1 + c)
                        act.activation(rh[0:RH, NPAIR * c:NPAIR * c + NPAIR, :], a_bank[c][0:RH, 0:HALF].rearrange("p (b l) -> p b l", l=L),
                                       ACT.Relu, bias=br1[:]).then_inc(r_ready, 1)

                def router_exp_a(g):
                    act.wait_ge(lg_read, g + 1)
                    act.activation(ev[:], lg[:], ACT.Exp).then_inc(exp_out, 1)

                def router_exp_b(g):
                    act.wait_ge(exp_in, g + 1)
                    if last:
                        act.activation(small[:, 3, :], small[:, 2, :], ACT.Tanh, scale=-0.5).then_inc(exp_out, 1)
                    else:
                        act.activation(small[:, 4, :], small[:, 3, :], ACT.Exp).then_inc(exp_out, 1)

                def combine(g, p):
                    act.wait_ge(c_turned, g + 1)
                    act.activation(ct[p][0:NR, :, :], a_bank[1][0:NR, 0:G * L // 2].bitcast(BF16).rearrange("p (b l) -> p b l", l=L),
                                   ACT.Copy).then_inc(c_ready, 1)

                def hidden1(g, u):
                    n = g * U + u
                    act.wait_ge(h1_done, n + 1)
                    wait(act, hm_ready if last else h2_done, n - 1)
                    act.activation(h1[u % 2][:], h1_bank[u % 2][:, 0:HALF], ACT.Gelu if last else ACT.Relu,
                                   bias=b1[:, u // 2:u // 2 + 1]).then_inc(h1_ready, 1)

                def hidden2(g, u):
                    n = g * U + u
                    act.wait_ge(h2_done, n + 1)
                    wait(act, hm_ready, n - 1)
                    act.activation(h2[u % 2][:], h2_bank[:, 0:HALF], ACT.Relu, bias=b2[:, u // 2:u // 2 + 1]).then_inc(h2_ready, 1)

                def output(g):
                    act.wait_ge(o_done, g + 1)
                    wait(act, o_turned, g)
                    act.activation(osb[:], o_bank[:, 0:HALF], ACT.Copy).then_inc(o_ready, 1)

                high(0, 0)
                if not last:
                    router_hidden(0, 0)
                    router_exp_a(0)
                router_exp_b(0)
                combine(0, 0)
                hidden1(0, 0)

                def step(g, p):
                    for u in range(U):
                        if u == 0 and exists(g + 1):
                            high(g + 1, 1 - p)
                        if u == 1 and exists(g + 1) and not last:
                            router_hidden(g + 1, 1 - p)
                        if u == 2 and exists(g - 1):
                            output(g - 1)
                        if u == R_A and exists(g + 1) and not last:
                            router_exp_a(g + 1)
                        if u == R_B and exists(g + 1):
                            router_exp_b(g + 1)
                        if u < LAST:
                            hidden1(g, u + 1)
                        elif exists(g + 1):
                            hidden1(g + 1, 0)
                        if not last:
                            hidden2(g, u)
                        if u == LAST and exists(g + 1):
                            combine(g + 1, 1 - p)

                in_groups(act, step)
                output(NG - 1)

            @block.tensor
            def _(pe):
                pe.wait_ge(loaded, N_LOADS[layer] * 16)
                pe.wait_ge(cleared, n_clear)
                if last:
                    pe.transpose(a_bank[0][0:D, 0:E], router_rows[:], ident[0:E, 0:E]).then_inc(prepared, 1)
                pe.wait_ge(prepared, N_PREPARED[layer])

                def turn(g, p):
                    pe.wait_ge(normed, g + 1)
                    wait(pe, lg_read, g)
                    wait(pe, c_ready, g)
                    for c in (0, 1):
                        for j in range(NPAIR):
                            b = NPAIR * c + j
                            mm = pe.transpose(a_bank[c][:, L * j:L * j + L], xn[p][:, b].rearrange("p a d -> p (a d)"), ident[0:L, 0:L])
                        mm.then_inc(x_turned, 1)

                def router(g, p):
                    for c in (0, 1):
                        pe.wait_ge(x_ready, 2 * g + 1 + c)
                        x = xs[p][:, NPAIR * c:NPAIR * c + NPAIR, :]
                        pe.matmul(a_bank[c][:, 0:HALF], wr_hi[:], x, start=True, stop=False)
                        pe.matmul(a_bank[c][:, 0:HALF], wr_lo[:], x, start=False, stop=True).then_inc(r_done, 1)

                def logits(g, p):
                    if last:
                        pe.wait_ge(x_ready, 2 * g + 2)
                    else:
                        pe.wait_ge(r_ready, 2 * g + 2)
                    for b in range(G):
                        if last:
                            pe.matmul(a_bank[0][0:L, D * b:D * b + D], xs[p][:, b, :], wr_hi[:], start=True, stop=False)
                            mm = pe.matmul(a_bank[0][0:L, D * b:D * b + D], xs[p][:, b, :], wr_lo[:], start=False, stop=True)
                        else:
                            mm = pe.matmul(a_bank[0][0:L, D * b:D * b + D], rh[:, b, :], wr2[:], start=True, stop=True)
                    mm.then_inc(routed, 1)

                def turn_combine(g, p):
                    pe.wait_ge(cp_ready, g + 1)
                    bank = a_bank[1][:, :].bitcast(BF16)
                    for b in range(G):
                        mm = pe.transpose(bank[0:NR, L * b:L * b + L], cp[p][:, b].rearrange("p i j e -> p (i j e)"), ident16[0:L, 0:L])
                    mm.then_inc(c_turned, 1)

                def layer1(g, p, u):
                    n = g * U + u
                    k, c = u // 2, u % 2
                    pe.wait_ge(x_ready, 2 * g + 1 + c)
                    wait(pe, h1_ready, n - 1)
                    x = xs[p][:, NPAIR * c:NPAIR * c + NPAIR, :]
                    o = h1_bank[u % 2][:, 0:HALF]
                    pe.matmul(o, w1_hi[:, 2 * k:2 * k + 2, :], x, start=True, stop=False)
                    pe.matmul(o, w1_lo[:, 2 * k:2 * k + 2, :], x, start=False, stop=True).then_inc(h1_done, 1)

                def spread(g, p, u):
                    n = g * U + u
                    k, c = u // 2, u % 2
                    pe.wait_ge(c_ready, g + 1)
                    wait(pe, hm_ready, n - 1)
                    pe.matmul(cb_bank[u % 2][:, 0:HALF], sel[:, 128 * k:128 * k + 128], ct[p][:, NPAIR * c:NPAIR * c + NPAIR, :],
                              start=True, stop=True).then_inc(cb_done, 1)

                def layer2(g, u):
                    n = g * U + u
                    pe.wait_ge(h1_ready, n + 1)
                    wait(pe, h2_ready, n)
                    pe.matmul(h2_bank[:, 0:HALF], w2[:, u // 2, :], h1[u % 2][:], start=True, stop=True).then_inc(h2_done, 1)

                def sum_pair(g, p, k):
                    pe.wait_ge(hm_ready, g * U + 2 * k + 2)
                    if k == 0:
                        wait(pe, o_ready, g)
                    for c in (0, 1):
                        mm = pe.matmul(o_bank[c * D:(c + 1) * D, 0:HALF], wo[:, k, :], hm[2 * k + c][:], start=(k == 0), stop=False)
                    mm.then_inc(o_pairs, 1)

                def finish_sum(g, p):
                    sum_pair(g, p, NP - 1)
                    for c in (0, 1):
                        mm = pe.matmul(o_bank[c * D:(c + 1) * D, 0:HALF], bo[:], ct[p][:, NPAIR * c:NPAIR * c + NPAIR, :],
                                       start=False, stop=True)
                    mm.then_inc(o_done, 1)

                def turn_output(g):
                    pe.wait_ge(o_ready, g + 1)
                    for j in range(NPAIR):
                        mm = pe.transpose(a_bank[1][0:L, 128 * j:128 * j + 128], osb[:, L * j:L * j + L], ident[:])
                    mm.then_inc(o_turned, 1)

                turn(0, 0)
                if not last:
                    router(0, 0)
                logits(0, 0)
                turn_combine(0, 0)
                layer1(0, 0, 0)

                def step(g, p):
                    for u in range(U):
                        if u == 0 and exists(g + 1):
                            turn(g + 1, 1 - p)
                        if u < LAST:
                            layer1(g, p, u + 1)
                        elif exists(g + 1):
                            layer1(g + 1, 1 - p, 0)
                        if u == 1 and exists(g + 1) and not last:
                            router(g + 1, 1 - p)
                        if u == 2 and exists(g + 1):
                            logits(g + 1, 1 - p)
                        if not last:
                            layer2(g, u)
                        spread(g, p, u)
                        if u == 1 and exists(g - 1):
                            finish_sum(g - 1, 1 - p)
                        if u == 3 and exists(g - 1):
                            if exists(g + 1):
                                if last:
                                    pe.wait_ge(x_ready, 2 * g + 4)
                                else:
                                    pe.wait_ge(r_ready, 2 * g + 4)
                            turn_output(g - 1)
                        if u % 2 == 1 and u >= 3:
                            sum_pair(g, p, (u - 3) // 2)
                    if exists(g + 1):
                        wait(pe, added, g)
                        turn_combine(g + 1, 1 - p)

                in_groups(pe, step)
                finish_sum(NG - 1, (NG - 1) % 2)
                turn_output(NG - 1)

            @block.vector
            def _(dve):
                row_scale(nc, dve, None, stats, mean, rstd, tmp, own, rooted)
                normalise(dve, xn[0], h, mean, rstd, 0, normed)
                normalise(dve, xn[1], h, mean, rstd, 1, normed)
                dve.wait_ge(loaded, N_LOADS[layer] * 16)
                dve.wait_ge(cleared, n_clear)
                done = [0]

                def link(ins):
                    done[0] += 1
                    ins.then_inc(prepared, 1)
                    dve.wait_ge(prepared, done[0])

                if last:
                    done[0] = 1
                    dve.wait_ge(prepared, 1)
                    for s in (0, 1):
                        link(dve.tensor_copy(wr_raw[s * D:(s + 1) * D, 0:E], a_bank[0][0:D, 0:E]))
                for raw, hi, lo in ((w1_raw, w1_hi, w1_lo), (wr_raw, wr_hi, wr_lo)):
                    link(dve.tensor_copy(hi[:], raw[:]))
                    link(dve.tensor_tensor(lo[:], raw[:], hi[:].bitcast(F32), ALU.subtract))
                link(dve.tensor_copy(sel[0:NR, :], sel_raw[:]))
                for j in range(3):
                    src = bo_raw if j == 0 else bo_rest
                    link(dve.tensor_copy(bo_part[:], src[:]))
                    if j == 0:
                        link(dve.tensor_scalar(bo_sum[:], bo_part[:], part[:, j:j + 1], None, ALU.mult))
                    else:
                        link(dve.scalar_tensor_tensor(bo_sum[:], bo_part[:], part[:, j:j + 1], bo_sum[:], ALU.mult, ALU.add))
                    if j < 2:
                        link(dve.tensor_tensor(bo_rest[:], src[:], bo_part[:], ALU.subtract))
                link(dve.tensor_copy(bo[0:NR, :], bo_sum[:]))
                assert done[0] == N_PREPARED[layer], done[0]

                ch = Chain(dve, chain).expect(CHAIN[layer])

                def low(g, p):
                    for c in (0, 1):
                        dve.wait_ge(x_high, 2 * g + 1 + c)
                        x = xs[p][D:128, NPAIR * c:NPAIR * c + NPAIR, :]
                        dve.tensor_tensor(x, a_bank[c][D:128, 0:HALF].rearrange("p (b l) -> p b l", l=L), x.bitcast(F32),
                                          ALU.subtract).then_inc(x_ready, 1)

                def wide(t):
                    return t.unsqueeze(2).broadcast_to([L, G, E])

                firsts = first[:].unsqueeze(1).broadcast_to([L, G, E])

                def route_a(g, p):
                    dve.wait_ge(routed, g + 1)
                    bank = a_bank[0][0:L, :].rearrange("p (b d) -> p b d", d=D)[:, :, 0:E]
                    ch(dve.tensor_reduce(small[:, 0, :], bank, AX_X, ALU.max))
                    ins = dve.tensor_tensor(lg[:], bank, wide(small[:, 0, :]), ALU.subtract)
                    ins.then_inc(lg_read, 1)
                    dve.wait_ge(lg_read, g + 1)
                    if last:
                        ch(dve.scalar_tensor_tensor(idx[:], lg[:], 0.0, firsts, ALU.is_ge, ALU.mult))
                    else:
                        dve.wait_ge(exp_out, 2 * g + 1)
                        ch(dve.scalar_tensor_tensor(idx[:], ev[:], 1.0, firsts, ALU.is_ge, ALU.mult))
                    ch(dve.tensor_reduce(small[:, 1, :], idx[:], AX_X, ALU.max))
                    ch(dve.tensor_tensor(s1[:], idx[:], wide(small[:, 1, :]), ALU.is_equal))

                def route_b(g, p):
                    src, off = (lg, -BIG) if last else (ev, -4.0)
                    ch(dve.scalar_tensor_tensor(rest[:], s1[:], off, src[:], ALU.mult, ALU.add))
                    second = small[:, 2, :]
                    ins = dve.tensor_reduce(second, rest[:], AX_X, ALU.max)
                    if last:
                        ins.then_inc(exp_in, 1)
                        dve.wait_ge(exp_in, g + 1)
                    else:
                        ch(ins)
                        ch(dve.tensor_reduce(small[:, 5, :], ev[:], AX_X, ALU.add))
                        ch(dve.reciprocal(small[:, 6, :], small[:, 5, :]))
                        dve.scalar_tensor_tensor(small[:, 3, :], second, -1.0, small[:, 6, :], ALU.add, ALU.mult).then_inc(exp_in, 1)
                    ch(dve.tensor_tensor(idx[:], rest[:], wide(second), ALU.subtract))
                    ch(dve.scalar_tensor_tensor(rest[:], idx[:], 0.0, firsts, ALU.is_ge, ALU.mult))
                    ch(dve.tensor_reduce(small[:, 1, :], rest[:], AX_X, ALU.max))
                    ch(dve.tensor_tensor(s2[:], rest[:], wide(small[:, 1, :]), ALU.is_equal))
                    if last:
                        dve.wait_ge(exp_out, g + 1)
                        ch(dve.tensor_scalar(small[:, 6, :], small[:, 3, :], 0.5, 0.5, ALU.mult, ALU.add))
                        ch(dve.tensor_scalar(small[:, 7, :], small[:, 3, :], -0.5, 0.5, ALU.mult, ALU.add))
                    else:
                        dve.wait_ge(exp_out, 2 * g + 2)
                        ch(dve.tensor_scalar(small[:, 5, :], small[:, 4, :], 1.0, None, ALU.add))
                        ch(dve.reciprocal(small[:, 6, :], small[:, 5, :]))
                        ch(dve.tensor_tensor(small[:, 7, :], small[:, 4, :], small[:, 6, :], ALU.mult))
                    ch(dve.tensor_tensor(s1[:], s1[:], wide(small[:, 6, :]), ALU.mult))
                    ch(dve.tensor_tensor(s2[:], s2[:], wide(small[:, 7, :]), ALU.mult))
                    ch(dve.tensor_tensor(cw[:], s1[:], s2[:], ALU.add))
                    wait(dve, c_turned, g - 1)
                    for i in range(3):
                        src = cw if i == 0 else rest
                        part_i = cp[p][:, :, i, :, 0:E]
                        ins = dve.tensor_copy(part_i, src[:].unsqueeze(2).broadcast_to([L, G, 3, E]))
                        if i == 2:
                            ins.then_inc(cp_ready, 1)
                        else:
                            ch(ins)
                            ch(dve.tensor_tensor(rest[:], src[:], part_i[:, :, 0, :], ALU.subtract))

                def weigh(g, u):
                    n = g * U + u
                    dve.wait_ge(cb_done, n + 1)
                    dve.wait_ge(h1_ready if last else h2_ready, n + 1)
                    if not (isinstance(g, int) and g < 1):
                        dve.wait_ge(o_pairs, g * NP - NP + u // 2 + 1)
                    src = h1 if last else h2
                    dve.tensor_tensor(hm[u][:], cb_bank[u % 2][:, 0:HALF], src[u % 2][:], ALU.mult).then_inc(hm_ready, 1)

                def residual(g, p):
                    dve.wait_ge(o_turned, g + 1)
                    src = a_bank[1][0:L, :].rearrange("p (j c d) -> p c j d", c=2, d=D)
                    for c in (0, 1):
                        here = h[:, bass.ds(g * G + NPAIR * c, NPAIR), :]
                        dst = here
                        if last:
                            if c == 0:
                                dve.wait_ge(carried, g + 1)
                                if not (isinstance(g, int) and g < 2):
                                    dve.wait_ge(sent[p], (g - p) * 8)
                            dst = fin[p][:, NPAIR * c:NPAIR * c + NPAIR, :]
                        ins = dve.tensor_tensor(dst, src[:, c], here, ALU.add)
                        if c == 1:
                            ins.then_inc(added, 1)
                    if not last:
                        dve.wait_ge(added, g + 1)
                        for b in range(G):
                            dve.bn_stats(slot(stats, g, b), slot(h, g, b))

                low(0, 0)
                route_a(0, 0)
                route_b(0, 0)

                def step(g, p):
                    ch.group(g)
                    for u in range(U):
                        if u == 0 and exists(g + 1):
                            low(g + 1, 1 - p)
                        if u == R_A and exists(g + 1):
                            route_a(g + 1, 1 - p)
                        if u == R_B and exists(g + 1):
                            route_b(g + 1, 1 - p)
                        if u == RES and exists(g - 1):
                            residual(g - 1, 1 - p)
                        weigh(g, u)
                        if u == LAST and exists(g + 2):
                            dve.wait_ge(x_turned, 2 * g + 2)
                            if last:
                                dve.wait_ge(carried, g + 1)
                            normalise(dve, xn[p], h, mean, rstd, g + 2, normed)

                in_groups(dve, step)
                residual(NG - 1, (NG - 1) % 2)


N_LOADS = {0: 2 + 2 + 2 + 9 + 3 + 4 + E0 + 3, 1: 2 + 2 + 2 + 9 + 3 + 1}
N_PREPARED = {0: 14, 1: 17}
CHAIN = {0: 22, 1: 18}


_INS = [
    "x", "L0_tok_weight", "L0_tok_bias", "L0_attn_Wq", "L0_attn_Wk", "L0_attn_Wv", "L0_attn_Wo",
    "L0_ffn_router_w1", "L0_ffn_router_b1", "L0_ffn_router_w2", "L0_ffn_router_b2",
    "L0_ffn_expert_w1", "L0_ffn_expert_b1", "L0_ffn_expert_w2", "L0_ffn_expert_b2", "L0_ffn_expert_w3", "L0_ffn_expert_b3",
    "L1_attn_Wq_comp", "L1_attn_Wkv_comp", "L1_attn_Wqc", "L1_attn_Wqr", "L1_attn_Wkc", "L1_attn_Wkr", "L1_attn_Wv",
    "L1_ffn_router_w", "L1_ffn_w1", "L1_ffn_b1", "L1_ffn_w2", "L1_ffn_b2",
]


def kernel(**inputs):
    import concourse.bacc as _bacc
    from concourse.bass_utils import run_bass_kernel_spmd as _run

    nc = _bacc.Bacc("TRN2", target_bir_lowering=False, num_devices=1)
    arrays, A = {}, {}
    for name in _INS:
        a = np.ascontiguousarray(inputs[name])
        arrays[f"in_{name}_dram"] = a
        A[name] = nc.dram_tensor(f"in_{name}_dram", a.shape, mybir.dt.from_np(a.dtype), kind="ExternalInput").ap()
    for name, a in constants().items():
        arrays[f"{name}_dram"] = np.ascontiguousarray(a)
        A[name] = nc.dram_tensor(f"{name}_dram", a.shape, mybir.dt.from_np(a.dtype), kind="ExternalInput").ap()
    out = nc.dram_tensor("out_0_dram", (B, L, D), F32, kind="ExternalOutput").ap()
    build(nc, A, out)
    r = _run(nc, [arrays], core_ids=[0])
    return r.results[0]["out_0_dram"]
```

```python
from contextlib import ExitStack

import concourse.bass as bass
import numpy as np
from concourse import mybir

F32 = mybir.dt.float32
F32R = mybir.dt.float32r
BF16 = mybir.dt.bfloat16
ALU = mybir.AluOpType
ACT = mybir.ActivationFunctionType
AX_X = mybir.AxisListType.X

B = 128
R = 64
T = 1000
PW, SW = 25, 12
L = (T - PW) // SW + 1
D = 64
G = 8
NG = B // G
NPAIR = G // 2
HALF = NPAIR * L
HS_SHIFT = SW // 2
NCH = 2 * HS_SHIFT + 1
E0, E1 = 6, 8
EP = 8
RH = 32
ROPE0 = 48
EPS = 1e-5
BIG = 1e30
NR = 9 * EP
LOAD_AT, PREPARE_AT = (1, 2), (6, 8)
AHEAD = 3
RESIDUAL = 4


def constants():
    l = np.arange(L)
    count = np.maximum(l, 1).astype(np.float32)
    relu_mask = (l[:, None] <= l[None, :]).astype(np.float32) / count[None, :]
    causal_bias = np.where(l[None, :] <= l[:, None], 0.0, -BIG).astype(np.float32)
    half = (D - ROPE0) // 2
    theta = (np.float32(1.0) / np.power(np.float32(10000.0), np.arange(half, dtype=np.float32) / np.float32(half))).astype(np.float32)
    angle = (np.arange(L, dtype=np.float32)[:, None] * theta[None, :]).astype(np.float32)
    cos, sin = np.cos(angle).astype(np.float32), np.sin(angle).astype(np.float32)
    rope_c, rope_s = np.ones((2, D, L), np.float32), np.zeros((2, D, L), np.float32)
    for i in range(half):
        rope_c[:, ROPE0 + 2 * i] = rope_c[:, ROPE0 + 2 * i + 1] = cos[:, i]
        rope_s[:, ROPE0 + 2 * i] = -sin[:, i]
        rope_s[:, ROPE0 + 2 * i + 1] = sin[:, i]
    out = {
        "c_ident": np.eye(128, dtype=np.float32),
        "c_relu_mask": relu_mask,
        "c_causal_bias": causal_bias,
        "c_rope_c": rope_c.reshape(2 * D, L),
        "c_rope_s": rope_s.reshape(2 * D, L),
    }
    for tag, E in (("0", E0), ("1", E1)):
        sel = np.zeros((3, 3, EP, E // 2, 2, D), np.float32)
        part = np.zeros((3, 3, EP, 3), np.float32)
        for e in range(E):
            sel[:, 0, e, e // 2, e % 2, :] = 1.0
        for j in range(3):
            part[:, j, :, j] = 1.0
        out["c_sel" + tag] = sel.reshape(9 * EP, E // 2 * 2 * D)
        out["c_part" + tag] = part.reshape(9 * EP, 3)
        out["c_first" + tag] = np.tile((E - np.arange(E)).astype(np.float32), (L, 1))
    return out


def in_groups(step, first=0):
    for g in range(first, NG):
        step(g)


def exists(g):
    return 0 <= g < NG


def wait(eng, sem, value):
    if value > 0:
        eng.wait_ge(sem, value)


class Chain:

    def __init__(self, eng, sem):
        self.eng, self.sem, self.k = eng, sem, 0

    def mark(self, ins):
        ins.then_inc(self.sem, 1)
        self.k += 1

    def settle(self):
        if self.k:
            self.eng.wait_ge(self.sem, self.k)

    def __call__(self, ins):
        self.mark(ins)
        self.settle()


def slots(t, g):
    return t[:, g * G:g * G + G, :]


def slot(t, g, b):
    return t[:, g * G + b, :]


def column(t, g, b):
    return t[:, g * G + b:g * G + b + 1]


def build(nc, A, out):
    with ExitStack() as ctx:
        def sb(name, shape, dt=F32):
            return ctx.enter_context(nc.sbuf_tensor(name, shape, dt))

        banks = [ctx.enter_context(nc.psum_tensor(f"bank{i}", [128, 512], F32)) for i in range(8)]

        h = sb("h", [L, B, D])
        stats = sb("stats", [L, B, 6])
        mean = sb("mean", [L, B])
        rstd = sb("rstd", [L, B])
        ident = sb("ident", [128, 128])
        ident16 = sb("ident16", [128, 128], BF16)

        def sem(name):
            return ctx.enter_context(nc.semaphore(name))

        moe = [moe_weights(nc, A, sb, sem, layer) for layer in (0, 1)]

        stage_patches(nc, A, banks, h, stats, ident, ident16, moe)
        stage_relu_attention(nc, A, banks, sb, h, stats, mean, rstd, ident)
        stage_moe(nc, banks, h, stats, mean, rstd, ident, ident16, 0, moe[0], None)
        stage_rope_attention(nc, A, banks, sb, h, stats, mean, rstd, ident)
        stage_moe(nc, banks, h, stats, mean, rstd, ident, ident16, 1, moe[1], out)


def stage_patches(nc, A, banks, h, stats, ident, ident16, moe):
    with ExitStack() as ctx:
        def sb(name, shape, dt=F32):
            return ctx.enter_context(nc.sbuf_tensor(name, shape, dt))

        def sem(name):
            return ctx.enter_context(nc.semaphore(name))

        x = A["x"].rearrange("b o r t -> (o r) b t")
        image = [sb(f"image{p}", [128, G, T]) for p in (0, 1)]
        weight = sb("tok_weight", [128, NCH, D])
        bias = sb("tok_bias", [128, 1])
        fm = [sb(f"tok_fm{p}", [128, HALF]) for p in (0, 1)]
        loaded = [[sem(f"image_loaded{p}{q}") for q in (0, 1)] for p in (0, 1)]
        consts = sem("consts_loaded")
        cleared = sem("tok_cleared")
        shifted = sem("image_shifted")
        summed = sem("patches_summed")
        activated = sem("patches_activated")
        turned = sem("patches_turned")
        stored = sem("patches_stored")
        own = sem("patches_own")
        w = A["L0_tok_weight"].rearrange("(r c) d -> r c d", c=PW)
        S = HS_SHIFT
        runs = ((0, 0), (S, 2 * S))
        b1 = A["L0_tok_bias"].rearrange("(d a) -> d a", a=1)

        with nc.Block() as block:
            @block.sync
            def _(sp):
                for g in range(2):
                    for q in (0, 1):
                        sp.dma_start(image[g][0:R, 4 * q:4 * q + 4, :], x[:, G * g + 4 * q:G * g + 4 * q + 4, :]).then_inc(loaded[g][q], 16)

                def step(g):
                    p = g % 2
                    if exists(g + 2):
                        sp.wait_ge(summed, g + 1)
                        for q in (0, 1):
                            sp.dma_start(image[p][0:R, 4 * q:4 * q + 4, :], x[:, G * (g + 2) + 4 * q:G * (g + 2) + 4 * q + 4, :]).then_inc(loaded[p][q], 16)

                in_groups(step)

            @block.gpsimd
            def _(pool):
                for p in (0, 1):
                    pool.memset(image[p][R:128, :, (L + 1) * SW:T], 0.0).then_inc(cleared, 1)
                pool.wait_ge(cleared, 2)
                for W in moe:
                    W.clear(pool)

            @block.scalar
            def _(act):
                for lo, c in runs:
                    act.dma_start(weight[0:R, lo:lo + S, :], w[:, c:c + S, :]).then_inc(consts, 16)
                    act.dma_start(weight[R:128, lo:lo + S, :], w[:, c + S:c + 2 * S, :]).then_inc(consts, 16)
                act.dma_start(weight[0:R, NCH - 1:NCH, :], w[:, PW - 1:PW, :]).then_inc(consts, 16)
                for q in (0, 1):
                    act.dma_start(bias[q * D:(q + 1) * D, :], b1).then_inc(consts, 16)
                act.dma_start(ident[:], A["c_ident"]).then_inc(consts, 16)
                act.wait_ge(consts, 8 * 16)

                def step(g):
                    p = g % 2
                    act.wait_ge(summed, g + 1)
                    if g >= 2:
                        act.wait_ge(turned, g - 1)
                    act.activation(fm[p][:], banks[p][:, 0:HALF], ACT.Gelu, bias=bias[:]).then_inc(activated, 1)
                    if g in LOAD_AT:
                        moe[LOAD_AT.index(g)].load(act)

                in_groups(step)

            @block.tensor
            def _(pe):
                pe.wait_ge(consts, 8 * 16)
                pe.wait_ge(own, 1)
                pe.wait_ge(cleared, 2)

                def turn(g, p):
                    pe.wait_ge(activated, g + 1)
                    if g >= 2:
                        pe.wait_ge(stored, g - 1)
                    for j in range(NPAIR):
                        mm = pe.transpose(banks[2 + p][0:L, 128 * j:128 * j + 128], fm[p][:, L * j:L * j + L], ident[:])
                    mm.then_inc(turned, 1)

                def step(g):
                    p = g % 2
                    pe.wait_ge(shifted, g * 2 + 2)
                    if g >= 2:
                        pe.wait_ge(activated, g - 1)
                    for n in range(NCH):
                        t0 = n if n < S else n + S if n < 2 * S else PW - 1
                        for s in (0, 1):
                            mm = pe.matmul(banks[p][s * D:(s + 1) * D, 0:HALF], weight[:, n, :],
                                           image[p][:, s:G:2, t0:t0 + SW * (L - 1) + 1:SW],
                                           start=(n == 0), stop=(n == NCH - 1))
                    mm.then_inc(summed, 1)
                    if g >= 1:
                        turn(g - 1, 1 - p)

                in_groups(step)
                turn(NG - 1, (NG - 1) % 2)

            @block.vector
            def _(dve):
                dve.memset(weight[R:128, NCH - 1:NCH, :], 0.0).then_inc(own, 1)
                dve.wait_ge(consts, 8 * 16)
                dve.tensor_copy(ident16[:], ident[:]).then_inc(own, 1)

                def store(g, p):
                    dve.wait_ge(turned, g + 1)
                    dve.tensor_copy(slots(h, g), banks[2 + p][0:L, :].rearrange("p (b d) -> p b d", d=D)).then_inc(stored, 1)
                    dve.wait_ge(stored, g + 1)
                    for b in range(G):
                        dve.bn_stats(slot(stats, g, b), slot(h, g, b))

                def shift(g, p):
                    for q in (0, 1):
                        dve.wait_ge(loaded[p][q], g // 2 * 16 + 16)
                        v = image[p][:, 4 * q:4 * q + 4, 0:(L + 1) * SW].rearrange("r b (m c) -> r b m c", c=SW)
                        dve.tensor_copy(v[R:128, :, :, 0:S], v[0:R, :, :, S:SW]).then_inc(shifted, 1)

                shift(0, 0)

                def step(g):
                    if exists(g + 1):
                        shift(g + 1, 1 - g % 2)
                    if exists(g - 1):
                        store(g - 1, 1 - g % 2)
                    if g in PREPARE_AT:
                        moe[PREPARE_AT.index(g)].prepare(dve)

                in_groups(step)
                store(NG - 1, (NG - 1) % 2)


def row_scale(nc, dve, act, stats, mean, rstd, tmp, own, rooted):
    if act is not None:
        act.wait_ge(own, 4)
        act.activation(rstd[:], tmp[:, 0, :], ACT.Sqrt).then_inc(rooted, 1)
        return
    even, odd = stats[:, :, 1], stats[:, :, 4]
    var, d, q = tmp[:, 0, :], tmp[:, 1, :], tmp[:, 2, :]
    n = D // 2

    def link(ins, k):
        ins.then_inc(own, 1)
        dve.wait_ge(own, k)

    link(dve.tensor_tensor(d, even, odd, ALU.subtract), 1)
    link(dve.scalar_tensor_tensor(var, d, float(n * n) / D / D, d, ALU.mult, ALU.mult), 2)
    link(dve.tensor_tensor(q, stats[:, :, 2], stats[:, :, 5], ALU.add), 3)
    dve.scalar_tensor_tensor(var, q, 1.0 / D, var, ALU.mult, ALU.add).then_inc(rooted, 1)
    dve.wait_ge(rooted, 1)
    link(dve.tensor_scalar(var, var, EPS, None, ALU.add), 4)
    link(dve.tensor_tensor(d, even, odd, ALU.add), 5)
    link(dve.tensor_scalar(mean[:], d, 0.5, None, ALU.mult), 6)
    dve.wait_ge(rooted, 2)
    link(dve.reciprocal(d, rstd[:]), 7)
    link(dve.tensor_tensor(q, d, d, ALU.mult), 8)
    link(dve.tensor_tensor(q, q, var, ALU.mult), 9)
    link(dve.tensor_scalar(q, q, -0.5, 1.5, ALU.mult, ALU.add), 10)
    link(dve.tensor_tensor(rstd[:], d, q, ALU.mult), 11)


ROW_SCALE_STEPS = 11


def normalise(dve, xn, h, mean, rstd, g, done):
    for b in range(G):
        x = slot(h, g, b)
        if len(xn.shape) == 4:
            x = x.unsqueeze(1).broadcast_to([L, 2, D])
        ins = dve.tensor_scalar(xn[0:L, b], x, column(mean, g, b), column(rstd, g, b), ALU.subtract, ALU.mult)
    ins.then_inc(done, 1)


def normalise_group(pool, xn, centred, h, mean, rstd, g, middle, k, done):
    per_row = [t[:, G * g:G * g + G].unsqueeze(2) for t in (mean, rstd)]
    pool.tensor_tensor(centred[:], slots(h, g), per_row[0].broadcast_to([L, G, D]), ALU.subtract).then_inc(middle, 1)
    pool.wait_ge(middle, k)
    if len(xn.shape) == 4:
        pool.tensor_tensor(xn[:], centred[:].unsqueeze(2).broadcast_to([L, G, 2, D]),
                           per_row[1].unsqueeze(3).broadcast_to([L, G, 2, D]), ALU.mult).then_inc(done, 1)
    else:
        pool.tensor_tensor(xn[:], centred[:], per_row[1].broadcast_to([L, G, D]), ALU.mult).then_inc(done, 1)


def stage_relu_attention(nc, A, banks, sb, h, stats, mean, rstd, ident):
    with ExitStack() as ctx:
        def sb(name, shape, dt=F32):
            return ctx.enter_context(nc.sbuf_tensor(name, shape, dt))

        def sem(name):
            return ctx.enter_context(nc.semaphore("ra_" + name))

        raw = sb("ra_raw", [D, 4, D])
        wo_t = sb("ra_wo_t", [D, D])
        w_qk = sb("ra_w_qk", [128, 128])
        w_vo = sb("ra_w_vo", [128, 128])
        mask = sb("ra_mask", [L, L])
        tmp = sb("ra_tmp", [L, 3, B])
        xn = [sb(f"ra_xn{p}", [L, G, D]) for p in (0, 1)]
        xt = [sb(f"ra_xt{p}", [128, HALF]) for p in (0, 1)]
        qz = [sb(f"ra_qz{p}", [128, NPAIR, 2, L]) for p in (0, 1)]
        v = [sb(f"ra_v{p}", [128, NPAIR * 2 * D]) for p in (0, 1)]
        pt = [sb(f"ra_pt{p}", [128, G, L]) for p in (0, 1)]
        x_bank, q_bank, v_bank, s_bank, o_bank = banks[0], banks[1], banks[2], banks[3:5], banks[5]

        loaded, cleared, own, rooted = sem("loaded"), sem("cleared"), sem("own"), sem("rooted")
        w_ps, w_sb = sem("w_ps"), sem("w_sb")
        normed = sem("normed")
        x_turned = sem("x_turned")
        x_ready = sem("x_ready")
        q_done = sem("q_done")
        v_done = sem("v_done")
        q_low = sem("q_low")
        q_high = sem("q_high")
        v_ready = sem("v_ready")
        scored = sem("scored")
        weighed = sem("weighed")
        mixed = sem("mixed")
        added = sem("added")

        with nc.Block() as block:
            @block.sync
            def _(sp):
                for i, n in enumerate(("L0_attn_Wq", "L0_attn_Wk", "L0_attn_Wv", "L0_attn_Wo")):
                    sp.dma_start(raw[:, i, :], A[n]).then_inc(loaded, 16)
                sp.dma_start(mask[:], A["c_relu_mask"]).then_inc(loaded, 16)

            @block.gpsimd
            def _(pool):
                for t in (w_qk, w_vo, *qz, *v, *pt):
                    pool.memset(t[:], 0.0).then_inc(cleared, 1)

            @block.scalar
            def _(act):
                row_scale(nc, None, act, stats, mean, rstd, tmp, own, rooted)
                act.wait_ge(cleared, 8)

                def copy_x(g, p):
                    act.wait_ge(x_turned, g + 1)
                    act.activation(xt[p][:], x_bank[:, 0:HALF], ACT.Copy).then_inc(x_ready, 1)

                def copy_qv(g, p):
                    act.wait_ge(q_done, g + 1)
                    wait(act, scored, 2 * g - 2)
                    act.activation(qz[p][0:D, :, 0, :], q_bank[0:D, 0:HALF].rearrange("p (j l) -> p j l", l=L), ACT.Copy).then_inc(q_low, 1)
                    act.wait_ge(v_done, g + 1)
                    wait(act, mixed, g - 1)
                    act.activation(v[p][0:L, :], v_bank[0:L, :], ACT.Copy).then_inc(v_ready, 1)

                copy_x(0, 0)
                copy_x(1, 1)
                copy_qv(0, 0)

                def step(g):
                    p = g % 2
                    if exists(g + 2):
                        copy_x(g + 2, p)
                    if exists(g + 1):
                        copy_qv(g + 1, 1 - p)

                in_groups(step)

            @block.tensor
            def _(pe):
                pe.wait_ge(loaded, 5 * 16)
                pe.transpose(x_bank[0:D, 0:D], raw[:, 3, :], ident[0:D, 0:D]).then_inc(w_ps, 1)
                for s in (0, 1):
                    mm = pe.matmul(q_bank[s * D:(s + 1) * D, s * D:(s + 1) * D], raw[:, 0, :], raw[:, 1, :], start=True, stop=True)
                mm.then_inc(w_ps, 1)
                pe.wait_ge(w_sb, 1)
                for s in (0, 1):
                    mm = pe.matmul(v_bank[s * D:(s + 1) * D, s * D:(s + 1) * D], raw[:, 2, :], wo_t[:], start=True, stop=True)
                mm.then_inc(w_ps, 1)
                pe.wait_ge(w_sb, 5)

                def turn(g, p):
                    pe.wait_ge(normed, g + 1)
                    wait(pe, x_ready, g)
                    for j in range(NPAIR):
                        mm = pe.transpose(x_bank[:, L * j:L * j + L], xn[p][:, 2 * j:2 * j + 2, :], ident[0:L, 0:L])
                    mm.then_inc(x_turned, 1)

                def project(g, p):
                    pe.wait_ge(x_ready, g + 1)
                    wait(pe, q_low, g)
                    wait(pe, q_high, g)
                    pe.matmul(q_bank[:, 0:HALF], w_qk[:], xt[p][:], start=True, stop=True).then_inc(q_done, 1)
                    wait(pe, v_ready, g)
                    for j in range(NPAIR):
                        mm = pe.matmul(v_bank[0:L, 128 * j:128 * j + 128], xt[p][:, L * j:L * j + L], w_vo[:], start=True, stop=True)
                    mm.then_inc(v_done, 1)

                turn(0, 0)
                turn(1, 1)
                project(0, 0)

                def step(g):
                    p = g % 2
                    pe.wait_ge(q_low, g + 1)
                    pe.wait_ge(q_high, g + 1)
                    for c in (0, 1):
                        wait(pe, weighed, 2 * g - 1 + c)
                        for j in (2 * c, 2 * c + 1):
                            mm = pe.matmul(s_bank[c][0:L, (j % 2) * 2 * L:(j % 2 + 1) * 2 * L], xt[p][:, L * j:L * j + L],
                                           qz[p][:, j, :, :], start=True, stop=True)
                        mm.then_inc(scored, 1)
                    if exists(g + 2):
                        turn(g + 2, p)
                    if exists(g + 1):
                        project(g + 1, 1 - p)
                    pe.wait_ge(v_ready, g + 1)
                    pe.wait_ge(weighed, 2 * g + 2)
                    wait(pe, added, g)
                    for b in range(G):
                        mm = pe.matmul(o_bank[0:L, D * b:D * b + D], pt[p][:, b, :], v[p][:, D * b:D * b + D], start=True, stop=True)
                    mm.then_inc(mixed, 1)

                in_groups(step)

            @block.vector
            def _(dve):
                row_scale(nc, dve, None, stats, mean, rstd, tmp, own, rooted)
                normalise(dve, xn[0], h, mean, rstd, 0, normed)
                normalise(dve, xn[1], h, mean, rstd, 1, normed)
                dve.wait_ge(cleared, 8)
                dve.wait_ge(w_ps, 1)
                dve.tensor_copy(wo_t[:], x_bank[0:D, 0:D]).then_inc(w_sb, 1)
                for bank, t, n in ((q_bank, w_qk, 2), (v_bank, w_vo, 3)):
                    dve.wait_ge(w_ps, n)
                    for s in (0, 1):
                        dve.tensor_copy(t[s * D:(s + 1) * D, s * D:(s + 1) * D], bank[s * D:(s + 1) * D, s * D:(s + 1) * D]).then_inc(w_sb, 1)
                dve.wait_ge(loaded, 5 * 16)

                def copy_q(g, p):
                    dve.wait_ge(q_done, g + 1)
                    wait(dve, scored, 2 * g - 2)
                    dve.tensor_copy(qz[p][D:128, :, 1, :], q_bank[D:128, 0:HALF].rearrange("p (j l) -> p j l", l=L)).then_inc(q_high, 1)

                copy_q(0, 0)

                def step(g):
                    p = g % 2
                    if exists(g + 2):
                        dve.wait_ge(x_turned, g + 1)
                        normalise(dve, xn[p], h, mean, rstd, g + 2, normed)
                    for c in (0, 1):
                        dve.wait_ge(scored, 2 * g + 1 + c)
                        wait(dve, mixed, g - 1)
                        dve.scalar_tensor_tensor(
                            pt[p][0:L, NPAIR * c:NPAIR * c + NPAIR, :], s_bank[c][0:L, 0:HALF].rearrange("p (b l) -> p b l", l=L), 0.0,
                            mask[:].unsqueeze(1).broadcast_to([L, NPAIR, L]), ALU.max, ALU.mult).then_inc(weighed, 1)
                    if exists(g + 1):
                        copy_q(g + 1, 1 - p)
                    dve.wait_ge(mixed, g + 1)
                    dve.tensor_tensor(slots(h, g), o_bank[0:L, :].rearrange("p (b d) -> p b d", d=D), slots(h, g), ALU.add).then_inc(added, 1)
                    dve.wait_ge(added, g + 1)
                    for b in range(G):
                        dve.bn_stats(slot(stats, g, b), slot(h, g, b))

                in_groups(step)


def stage_rope_attention(nc, A, banks, sb, h, stats, mean, rstd, ident):
    with ExitStack() as ctx:
        def sb(name, shape, dt=F32):
            return ctx.enter_context(nc.sbuf_tensor(name, shape, dt))

        def sem(name):
            return ctx.enter_context(nc.semaphore("sa_" + name))

        comp = sb("sa_comp", [D, 2, D])
        comp_t = sb("sa_comp_t", [D, 2, D])
        heads = sb("sa_heads", [D, 3, D])
        w = sb("sa_w", [128, 5, 128])
        rope = sb("sa_rope", [128, 2, L])
        bias = sb("sa_bias", [L, L])
        tmp = sb("sa_tmp", [L, 3, B])
        xn = [sb(f"sa_xn{p}", [L, G, D]) for p in (0, 1)]
        xt = [sb(f"sa_xt{p}", [128, HALF]) for p in (0, 1)]
        turn_c = sb("sa_turn_c", [128, 2, NPAIR, L])
        turn_s = sb("sa_turn_s", [128, 2, NPAIR, L])
        q = [sb(f"sa_q{p}", [128, NPAIR, L]) for p in (0, 1)]
        kz = [sb(f"sa_kz{p}", [128, NPAIR, 2, L]) for p in (0, 1)]
        v = [sb(f"sa_v{p}", [128, NPAIR * 2 * D]) for p in (0, 1)]
        masked = sb("sa_masked", [L, G, L])
        top = sb("sa_top", [L, G])
        low = sb("sa_low", [L, G])
        prob = sb("sa_prob", [L, G, L])
        total = sb("sa_total", [L, G])
        share = sb("sa_share", [L, G])
        pt = [sb(f"sa_pt{p}", [128, G, L]) for p in (0, 1)]
        mixed_sb = sb("sa_mixed", [L, G, D])
        xo_bank, v_bank = banks[0], banks[1]
        qk_bank, sw_bank, s_bank = banks[2:4], banks[4:6], banks[6:8]
        p_bank = sw_bank

        loaded, cleared, own, rooted = sem("loaded"), sem("cleared"), sem("own"), sem("rooted")
        w_ps, w_sb = sem("w_ps"), sem("w_sb")
        normed = sem("normed")
        x_turned = sem("x_turned")
        x_ready = sem("x_ready")
        qk_done = sem("qk_done")
        sw_done = sem("sw_done")
        v_done = sem("v_done")
        v_ready = sem("v_ready")
        cos_done = sem("cos_done")
        sin_done = sem("sin_done")
        rotated = sem("rotated")
        scored = sem("scored")
        biased = sem("biased")
        topped = sem("topped")
        shifted = sem("shifted")
        raised = sem("raised")
        p_turned = sem("p_turned")
        p_ready = sem("p_ready")
        mixed = sem("mixed")
        shared = sem("shared")
        scaled = sem("scaled")
        added = sem("added")
        SCALE = float(D) ** -0.5

        with nc.Block() as block:
            @block.sync
            def _(sp):
                for i, n in enumerate(("L1_attn_Wq_comp", "L1_attn_Wkv_comp")):
                    sp.dma_start(comp[:, i, :], A[n]).then_inc(loaded, 16)
                for i, n in enumerate(("L1_attn_Wqc", "L1_attn_Wkc")):
                    sp.dma_start(heads[:, i, 0:ROPE0], A[n]).then_inc(loaded, 16)
                for i, n in enumerate(("L1_attn_Wqr", "L1_attn_Wkr")):
                    sp.dma_start(heads[:, i, ROPE0:D], A[n]).then_inc(loaded, 16)
                sp.dma_start(heads[:, 2, :], A["L1_attn_Wv"]).then_inc(loaded, 16)
                sp.dma_start(rope[:, 0, :], A["c_rope_c"]).then_inc(loaded, 16)
                sp.dma_start(rope[:, 1, :], A["c_rope_s"]).then_inc(loaded, 16)
                sp.dma_start(bias[:], A["c_causal_bias"]).then_inc(loaded, 16)

            @block.gpsimd
            def _(pool):
                for t in (w, *kz, *v, *pt):
                    pool.memset(t[:], 0.0).then_inc(cleared, 1)
                pool.wait_ge(cleared, 7)

                def rotate(g, p):
                    pool.wait_ge(cos_done, g + 1)
                    pool.wait_ge(sin_done, g + 1)
                    wait(pool, scored, 2 * g - 2)
                    pool.tensor_tensor(q[p][:], turn_c[:, 0], turn_s[:, 0], ALU.add).then_inc(rotated, 1)
                    pool.wait_ge(rotated, 3 * g + 1)
                    for s in (0, 1):
                        ins = pool.tensor_tensor(kz[p][s * D:(s + 1) * D, :, s, :], turn_c[s * D:(s + 1) * D, 1],
                                                 turn_s[s * D:(s + 1) * D, 1], ALU.add)
                        ins.then_inc(rotated, 1)

                rotate(0, 0)

                def step(g):
                    p = g % 2
                    if exists(g + 1):
                        rotate(g + 1, 1 - p)

                in_groups(step)

            @block.scalar
            def _(act):
                row_scale(nc, None, act, stats, mean, rstd, tmp, own, rooted)
                act.wait_ge(cleared, 7)

                def copy_x(g, p):
                    act.wait_ge(x_turned, g + 1)
                    act.activation(xt[p][:], xo_bank[:, 0:HALF], ACT.Copy).then_inc(x_ready, 1)

                def copy_v(g, p):
                    act.wait_ge(v_done, g + 1)
                    wait(act, mixed, g - 1)
                    act.activation(v[p][0:L, :], v_bank[0:L, :], ACT.Copy).then_inc(v_ready, 1)

                copy_x(0, 0)
                copy_x(1, 1)
                copy_v(0, 0)

                def step(g):
                    p = g % 2
                    if exists(g + 2):
                        copy_x(g + 2, p)
                    act.wait_ge(shifted, g + 1)
                    wait(act, p_turned, g)
                    wait(act, shared, g)
                    for b in range(G):
                        act.activation(prob[:, b, :], masked[:, b, :], ACT.Exp, bias=low[:, b:b + 1], scale=SCALE,
                                       accum_out=total[:, b:b + 1]).then_inc(raised, 1)
                    if exists(g + 1):
                        copy_v(g + 1, 1 - p)
                    act.wait_ge(p_turned, g + 1)
                    wait(act, mixed, g - 1)
                    for c in (0, 1):
                        act.activation(pt[p][0:L, NPAIR * c:NPAIR * c + NPAIR, :], p_bank[c][0:L, 0:HALF].rearrange("p (b l) -> p b l", l=L),
                                       ACT.Copy).then_inc(p_ready, 1)

                in_groups(step)

            @block.tensor
            def _(pe):
                pe.wait_ge(loaded, 10 * 16)
                for i in (0, 1):
                    mm = pe.transpose(xo_bank[0:D, D * i:D * i + D], comp[:, i, :], ident[0:D, 0:D])
                mm.then_inc(w_ps, 1)
                pe.wait_ge(w_sb, 1)
                for i in range(3):
                    for s in (0, 1):
                        mm = pe.matmul(v_bank[s * D:(s + 1) * D, D * i:D * i + D], comp_t[:, min(i, 1), :], heads[:, i, :], start=True, stop=True)
                mm.then_inc(w_ps, 1)
                pe.wait_ge(w_sb, 15)

                def turn(g, p):
                    pe.wait_ge(normed, g + 1)
                    wait(pe, x_ready, g)
                    if g >= 3:
                        pe.wait_ge(scaled, g - 2)
                    for j in range(NPAIR):
                        mm = pe.transpose(xo_bank[:, L * j:L * j + L], xn[p][:, 2 * j:2 * j + 2, :], ident[0:L, 0:L])
                    mm.then_inc(x_turned, 1)

                def project(g, p):
                    pe.wait_ge(x_ready, g + 1)
                    wait(pe, cos_done, g)
                    for i in (0, 1):
                        mm = pe.matmul(qk_bank[i][:, 0:HALF], w[:, i, :], xt[p][:], start=True, stop=True)
                    mm.then_inc(qk_done, 1)
                    wait(pe, sin_done, g)
                    wait(pe, p_ready, 2 * g - 2)
                    for i in (0, 1):
                        mm = pe.matmul(sw_bank[i][:, 0:HALF], w[:, 2 + i, :], xt[p][:], start=True, stop=True)
                    mm.then_inc(sw_done, 1)
                    wait(pe, v_ready, g)
                    for j in range(NPAIR):
                        mm = pe.matmul(v_bank[0:L, 128 * j:128 * j + 128], xt[p][:, L * j:L * j + L], w[:, 4, :], start=True, stop=True)
                    mm.then_inc(v_done, 1)

                turn(0, 0)
                turn(1, 1)
                project(0, 0)

                def step(g):
                    p = g % 2
                    pe.wait_ge(rotated, 3 * g + 3)
                    for c in (0, 1):
                        wait(pe, biased, 2 * g - 1 + c)
                        for j in (2 * c, 2 * c + 1):
                            mm = pe.matmul(s_bank[c][0:L, (j % 2) * 2 * L:(j % 2 + 1) * 2 * L], q[p][:, j, :],
                                           kz[p][:, j, :, :], start=True, stop=True)
                        mm.then_inc(scored, 1)
                    if exists(g + 2):
                        turn(g + 2, p)
                    if exists(g + 1):
                        project(g + 1, 1 - p)
                        pe.wait_ge(sin_done, g + 2)
                    pe.wait_ge(raised, G * g + G)
                    for b in range(G):
                        mm = pe.transpose(p_bank[b // NPAIR][0:L, L * (b % NPAIR):L * (b % NPAIR) + L], prob[:, b, :], ident[0:L, 0:L])
                    mm.then_inc(p_turned, 1)
                    pe.wait_ge(v_ready, g + 1)
                    pe.wait_ge(p_ready, 2 * g + 2)
                    if exists(g + 2):
                        pe.wait_ge(x_ready, g + 3)
                    wait(pe, scaled, g)
                    for b in range(G):
                        mm = pe.matmul(xo_bank[0:L, D * b:D * b + D], pt[p][:, b, :], v[p][:, D * b:D * b + D], start=True, stop=True)
                    mm.then_inc(mixed, 1)

                in_groups(step)

            @block.vector
            def _(dve):
                row_scale(nc, dve, None, stats, mean, rstd, tmp, own, rooted)
                normalise(dve, xn[0], h, mean, rstd, 0, normed)
                normalise(dve, xn[1], h, mean, rstd, 1, normed)
                dve.wait_ge(cleared, 7)
                dve.wait_ge(w_ps, 1)
                dve.tensor_copy(comp_t[:], xo_bank[0:D, 0:2 * D].rearrange("p (i d) -> p i d", d=D)).then_inc(w_sb, 1)
                dve.wait_ge(w_ps, 2)
                for s in (0, 1):
                    rows, cols = slice(s * D, (s + 1) * D), slice(s * D, (s + 1) * D)
                    for i, at in ((0, 0), (1, 1), (2, 4)):
                        dve.tensor_copy(w[rows, at, cols], v_bank[rows, D * i:D * i + D]).then_inc(w_sb, 1)
                    for i in (0, 1):
                        for a in (0, 1):
                            dve.tensor_copy(w[rows, 2 + i, s * D + ROPE0 + a:(s + 1) * D:2],
                                            v_bank[rows, D * i + ROPE0 + 1 - a:D * i + D:2]).then_inc(w_sb, 1)
                dve.wait_ge(loaded, 10 * 16)

                def rope_parts(g, p):
                    dve.wait_ge(qk_done, g + 1)
                    wait(dve, rotated, 3 * g)
                    for i in (0, 1):
                        ins = dve.tensor_tensor(turn_c[:, i], qk_bank[i][:, 0:HALF].rearrange("p (j l) -> p j l", l=L),
                                                rope[:, 0, :].unsqueeze(1).broadcast_to([128, NPAIR, L]), ALU.mult)
                    ins.then_inc(cos_done, 1)
                    dve.wait_ge(sw_done, g + 1)
                    for i in (0, 1):
                        ins = dve.tensor_tensor(turn_s[:, i], sw_bank[i][:, 0:HALF].rearrange("p (j l) -> p j l", l=L),
                                                rope[:, 1, :].unsqueeze(1).broadcast_to([128, NPAIR, L]), ALU.mult)
                    ins.then_inc(sin_done, 1)

                rope_parts(0, 0)

                def step(g):
                    p = g % 2
                    if exists(g + 2):
                        dve.wait_ge(x_turned, g + 1)
                        normalise(dve, xn[p], h, mean, rstd, g + 2, normed)
                    wait(dve, raised, G * g)
                    for c in (0, 1):
                        dve.wait_ge(scored, 2 * g + 1 + c)
                        dve.tensor_tensor(masked[:, NPAIR * c:NPAIR * c + NPAIR, :], s_bank[c][0:L, 0:HALF].rearrange("p (b l) -> p b l", l=L),
                                          bias[:].unsqueeze(1).broadcast_to([L, NPAIR, L]), ALU.add).then_inc(biased, 1)
                    dve.wait_ge(biased, 2 * g + 2)
                    dve.tensor_reduce(top[:], masked[:], AX_X, ALU.max).then_inc(topped, 1)
                    dve.wait_ge(topped, g + 1)
                    dve.tensor_scalar(low[:], top[:], -SCALE, None, ALU.mult).then_inc(shifted, 1)
                    if exists(g + 1):
                        rope_parts(g + 1, 1 - p)
                    dve.wait_ge(raised, G * g + G)
                    dve.reciprocal(share[:], total[:]).then_inc(shared, 1)
                    dve.wait_ge(shared, g + 1)
                    dve.wait_ge(mixed, g + 1)
                    dve.tensor_tensor(mixed_sb[:], xo_bank[0:L, :].rearrange("p (b d) -> p b d", d=D),
                                      share[:].unsqueeze(2).broadcast_to([L, G, D]), ALU.mult).then_inc(scaled, 1)
                    dve.wait_ge(scaled, g + 1)
                    dve.tensor_tensor(slots(h, g), mixed_sb[:], slots(h, g), ALU.add).then_inc(added, 1)
                    dve.wait_ge(added, g + 1)
                    for b in range(G):
                        dve.bn_stats(slot(stats, g, b), slot(h, g, b))

                in_groups(step)


class Weights:
    pass


def moe_weights(nc, A, sb, sem, layer):
    last = layer == 1
    E = E1 if last else E0
    NP = E // 2
    tag = f"m{layer}_"
    W = Weights()
    W.w1_raw = sb(tag + "w1_raw", [128, E, D])
    W.w1_hi, W.w1_lo = sb(tag + "w1_hi", [128, E, D], F32R), sb(tag + "w1_lo", [128, E, D], F32R)
    W.b1 = sb(tag + "b1", [128, NP])
    RC = D if last else 128
    W.wr_raw = sb(tag + "wr_raw", [128, RC])
    W.wr_hi, W.wr_lo = sb(tag + "wr_hi", [128, RC], F32R), sb(tag + "wr_lo", [128, RC], F32R)
    W.wo = sb(tag + "wo", [128, NP, D])
    W.bo_raw, W.bo_rest = sb(tag + "bo_raw", [NR, D]), sb(tag + "bo_rest", [NR, D])
    W.bo_part = sb(tag + "bo_part", [NR, D], BF16)
    W.bo_sum = sb(tag + "bo_sum", [NR, D])
    W.bo = sb(tag + "bo", [128, D], BF16)
    W.part = sb(tag + "part", [NR, 3])
    W.sel_raw = sb(tag + "sel_raw", [NR, NP * 128])
    W.sel = sb(tag + "sel", [128, NP * 128], BF16)
    W.first = sb(tag + "first", [L, E])
    if not last:
        W.w2 = sb(tag + "w2", [128, NP, 128])
        W.b2 = sb(tag + "b2", [128, NP])
        W.br1 = sb(tag + "br1", [RH, 1])
        W.wr2 = sb(tag + "wr2", [128, D])
    W.loaded, W.cleared, W.prepared = sem(tag + "loaded"), sem(tag + "cleared"), sem(tag + "prepared")
    zeroed = (W.wr_raw, W.bo, W.bo_raw, W.sel) + (() if last else (W.w2, W.wr2))
    W.n_loads, W.n_prepared = 0, 14

    def clear(pool):
        for i, t in enumerate(zeroed):
            pool.memset(t[:], 0.0).then_inc(W.cleared, 1)
            pool.wait_ge(W.cleared, i + 1)

    def load(eng):
        def get(dst, src):
            W.n_loads += 1
            eng.dma_start(dst, src).then_inc(W.loaded, 16)

        w_in, b_in = A["L1_ffn_w1" if last else "L0_ffn_expert_w1"], A["L1_ffn_b1" if last else "L0_ffn_expert_b1"]
        w_out, b_out = A["L1_ffn_w2" if last else "L0_ffn_expert_w3"], A["L1_ffn_b2" if last else "L0_ffn_expert_b3"]
        eng.wait_ge(W.cleared, len(zeroed))
        with nc.allow_non_contiguous_dma(reason="small biases"):
            for s in (0, 1):
                get(W.w1_raw[s * D:(s + 1) * D, :, :], w_in.rearrange("e d h -> d e h"))
                get(W.b1[s * D:(s + 1) * D, :], b_in.rearrange("(k e) h -> e h k", e=2)[s])
                get(W.wo[s * D:(s + 1) * D, :, :], w_out.rearrange("(k e) h d -> e h k d", e=2)[s])
            for i in range(9):
                get(W.bo_raw[i * EP:i * EP + E, :], b_out)
            get(W.part[:], A[f"c_part{layer}"])
            get(W.sel_raw[:], A[f"c_sel{layer}"])
            get(W.first[:], A[f"c_first{layer}"])
            for s in (0, 1):
                if last:
                    get(W.wr_raw[s * D:(s + 1) * D, 0:E], A["L1_ffn_router_w"].rearrange("e d -> d e"))
                else:
                    get(W.wr_raw[s * D:(s + 1) * D, 0:RH], A["L0_ffn_router_w1"])
                    get(W.b2[s * D:(s + 1) * D, :], A["L0_ffn_expert_b2"].rearrange("(k e) h -> e h k", e=2)[s])
            if not last:
                for e in range(E):
                    s = e % 2
                    get(W.w2[s * D:(s + 1) * D, e // 2, s * D:(s + 1) * D], A["L0_ffn_expert_w2"][e])
                get(W.br1[:], A["L0_ffn_router_b1"].rearrange("(r a) -> r a", a=1))
                get(W.wr2[0:RH, 0:E], A["L0_ffn_router_w2"])
                get(W.wr2[RH:RH + 1, 0:E], A["L0_ffn_router_b2"].rearrange("(a e) -> a e", a=1))

    def prepare(dve):
        done = 0

        def link(ins):
            nonlocal done
            done += 1
            ins.then_inc(W.prepared, 1)
            dve.wait_ge(W.prepared, done)

        dve.wait_ge(W.loaded, W.n_loads * 16)
        for raw, hi, lo in ((W.w1_raw, W.w1_hi, W.w1_lo), (W.wr_raw, W.wr_hi, W.wr_lo)):
            link(dve.tensor_copy(hi[:], raw[:]))
            link(dve.tensor_tensor(lo[:], raw[:], hi[:].bitcast(F32), ALU.subtract))
        link(dve.tensor_copy(W.sel[0:NR, :], W.sel_raw[:]))
        for j in range(3):
            src = W.bo_raw if j == 0 else W.bo_rest
            link(dve.tensor_copy(W.bo_part[:], src[:]))
            if j == 0:
                link(dve.tensor_scalar(W.bo_sum[:], W.bo_part[:], W.part[:, j:j + 1], None, ALU.mult))
            else:
                link(dve.scalar_tensor_tensor(W.bo_sum[:], W.bo_part[:], W.part[:, j:j + 1], W.bo_sum[:], ALU.mult, ALU.add))
            if j < 2:
                link(dve.tensor_tensor(W.bo_rest[:], src[:], W.bo_part[:], ALU.subtract))
        link(dve.tensor_copy(W.bo[0:NR, :], W.bo_sum[:]))
        assert done == W.n_prepared, done

    W.clear, W.load, W.prepare = clear, load, prepare
    return W


def stage_moe(nc, banks, h, stats, mean, rstd, ident, ident16, layer, W, out):
    last = layer == 1
    E = E1 if last else E0
    NP = E // 2
    U = 2 * NP
    LAST = U - 1
    with ExitStack() as ctx:
        def sb(name, shape, dt=F32):
            return ctx.enter_context(nc.sbuf_tensor(f"m{layer}_{name}", shape, dt))

        def sem(name):
            return ctx.enter_context(nc.semaphore(f"m{layer}_{name}"))

        tmp = sb("tmp", [L, 3, B])
        centred = sb("centred", [L, G, D])
        xn = [sb(f"xn{p}", [L, G, 2, D]) for p in range(3)]
        xs = [sb(f"xs{p}", [128, G, L], F32R) for p in range(4)]
        ct = [sb(f"ct{p}", [128, G, L], BF16) for p in (0, 1)]
        h1 = [sb(f"h1_{n}", [128, HALF]) for n in (0, 1)]
        h2 = [sb(f"h2_{n}", [128, HALF]) for n in (0, 1)]
        hm = [sb(f"hm{u}", [128, HALF]) for u in range(U)]
        osb = sb("osb", [128, HALF])
        lg = [sb(f"lg{p}", [L, 2 * G, E]) for p in (0, 1)]
        top = sb("top", [L, 2, G])
        ev, idx = sb("ev", [L, 2 * G, E]), sb("idx", [L, 2 * G, E])
        s1, s2 = sb("s1", [L, 2 * G, E]), sb("s2", [L, 2 * G, E])
        cw, rest = sb("cw", [L, 2 * G, E]), sb("rest", [L, 2 * G, E])
        small = sb("small", [L, 8, 2 * G])
        cp = sb("cp", [L, 2 * G, 3, 3, EP], BF16)
        rh = None if last else sb("rh", [128, G, L])
        fin = [sb(f"fin{p}", [L, G, D]) for p in (0, 1)] if last else None

        a_bank, o_bank = banks[0:2], banks[2]
        h1_bank, cb_bank = banks[3:5], banks[5:7]
        h2_bank = banks[7]

        cleared, own, rooted = sem("zeroed"), sem("own"), sem("rooted")
        shifted = sem("centred")
        normed = sem("normed")
        carried = sem("carried")
        x_turned = sem("x_turned")
        x_high = sem("x_high")
        x_ready = sem("x_ready")
        r_done = sem("r_done")
        r_ready = sem("r_ready")
        routed = sem("routed")
        lg_read = sem("lg_read")
        exp_a, exp_in, exp_b = sem("exp_a"), sem("exp_in"), sem("exp_b")
        cp_ready = sem("cp_ready")
        c_turned = sem("c_turned")
        c_ready = sem("c_ready")
        h1_done, h1_ready = sem("h1_done"), sem("h1_ready")
        h2_done, h2_ready = sem("h2_done"), sem("h2_ready")
        cb_done = sem("cb_done")
        hm_ready = sem("hm_ready")
        o_pairs = sem("o_pairs")
        o_done = sem("o_done")
        o_ready = sem("o_ready")
        o_turned = sem("o_turned")
        added = sem("added")
        chain = sem("chain")
        sent = [sem(f"sent{p}") for p in (0, 1)] if last else None
        n_clear = 5

        with nc.Block() as block:
            @block.sync
            def _(sp):
                if last:
                    dst = out.rearrange("b l d -> l b d")

                    def step(g):
                        sp.wait_ge(added, g + 1)
                        sp.dma_start(dst[:, G * g:G * g + G, :], fin[g % 2][:]).then_inc(sent[g % 2], 16)

                    in_groups(step)
                    for p in (0, 1):
                        sp.wait_ge(sent[p], NG // 2 * 16)

            @block.gpsimd
            def _(pool):
                for i, t in enumerate((cp, *ct)):
                    pool.memset(t[:], 0.0).then_inc(cleared, 1)
                    pool.wait_ge(cleared, i + 1)
                if last:
                    for p in (0, 1):
                        pool.memset(fin[p][:], 0.0).then_inc(cleared, 1)
                else:
                    pool.memset(rh[:], 0.0).then_inc(cleared, 1)
                    pool.wait_ge(cleared, 4)
                    pool.memset(rh[RH:RH + 1, :, :], 1.0).then_inc(cleared, 1)
                pool.wait_ge(cleared, n_clear)
                pool.wait_ge(normed, 1)
                if last:
                    pool.wait_ge(normed, 1)
                    pool.tensor_tensor(slots(h, 0), xn[0][:, :, 0, :], slots(h, 0), ALU.add).then_inc(carried, 1)

                def normal(f):
                    wait(pool, x_turned, 2 * (f - 2))
                    pool.wait_ge(normed, f)
                    normalise_group(pool, xn[f % 3], centred, h, mean, rstd, f, shifted, f, normed)
                    if last:
                        pool.wait_ge(normed, f + 1)
                        pool.tensor_tensor(slots(h, f), xn[f % 3][:, :, 0, :], slots(h, f), ALU.add).then_inc(carried, 1)

                in_groups(normal, 1)

            @block.scalar
            def _(act):
                row_scale(nc, None, act, stats, mean, rstd, tmp, own, rooted)

                def high(f):
                    for c in (0, 1):
                        act.wait_ge(x_turned, 2 * f + 1 + c)
                        if c == 0:
                            wait(act, h1_done, (f - 3) * U)
                        act.activation(xs[f % 4][:, NPAIR * c:NPAIR * c + NPAIR, :], a_bank[c][:, 0:HALF].rearrange("p (b l) -> p b l", l=L),
                                       ACT.Copy).then_inc(x_high, 1)

                def router_hidden(f):
                    for c in (0, 1):
                        act.wait_ge(r_done, 2 * f + 1 + c)
                        if f == 0 and c == 0:
                            act.wait_ge(cleared, n_clear)
                        wait(act, routed, f)
                        act.activation(rh[0:RH, NPAIR * c:NPAIR * c + NPAIR, :], a_bank[c][0:RH, 0:HALF].rearrange("p (b l) -> p b l", l=L),
                                       ACT.Relu, bias=W.br1[:]).then_inc(r_ready, 1)

                def exponents(n):
                    act.wait_ge(lg_read, 2 * n + 2)
                    act.activation(ev[:], lg[n % 2][:], ACT.Exp).then_inc(exp_a, 1)

                def weight_of_second(n):
                    act.wait_ge(exp_in, n + 1)
                    if last:
                        act.activation(small[:, 3, :], small[:, 2, :], ACT.Tanh, scale=-0.5).then_inc(exp_b, 1)
                    else:
                        act.activation(small[:, 4, :], small[:, 3, :], ACT.Exp).then_inc(exp_b, 1)

                def combine(g):
                    act.wait_ge(c_turned, g + 1)
                    wait(act, o_done, g - 1)
                    act.activation(ct[g % 2][0:NR, :, :], a_bank[1][0:NR, 0:G * L // 2].bitcast(BF16).rearrange("p (b l) -> p b l", l=L),
                                   ACT.Copy).then_inc(c_ready, 1)

                def hidden1(g, u):
                    n = g * U + u
                    act.wait_ge(h1_done, n + 1)
                    wait(act, hm_ready if last else h2_done, n - 1)
                    act.activation(h1[u % 2][:], h1_bank[u % 2][:, 0:HALF], ACT.Gelu if last else ACT.Relu,
                                   bias=W.b1[:, u // 2:u // 2 + 1]).then_inc(h1_ready, 1)

                def hidden2(g, u):
                    n = g * U + u
                    act.wait_ge(h2_done, n + 1)
                    wait(act, hm_ready, n - 1)
                    act.activation(h2[u % 2][:], h2_bank[:, 0:HALF], ACT.Relu, bias=W.b2[:, u // 2:u // 2 + 1]).then_inc(h2_ready, 1)

                def output(g):
                    act.wait_ge(o_done, g + 1)
                    wait(act, o_turned, g)
                    act.activation(osb[:], o_bank[:, 0:HALF], ACT.Copy).then_inc(o_ready, 1)

                for f in (0, 1):
                    high(f)
                    if not last:
                        router_hidden(f)
                if not last:
                    exponents(0)
                high(2)
                if not last:
                    router_hidden(2)
                weight_of_second(0)
                combine(0)
                hidden1(0, 0)

                def step(g):
                    f = g + AHEAD
                    for u in range(U):
                        if u == 0 and exists(f):
                            high(f)
                        if u == 1 and exists(f) and not last:
                            router_hidden(f)
                        if u == 2 and exists(g - 1):
                            output(g - 1)
                        if g % 2 == 0 and u == 4 and exists(g + 2) and not last:
                            exponents(g // 2 + 1)
                        if g % 2 == 1 and u == 1 and exists(g + 1):
                            weight_of_second(g // 2 + 1)
                        if u < LAST:
                            hidden1(g, u + 1)
                        elif exists(g + 1):
                            hidden1(g + 1, 0)
                        if not last:
                            hidden2(g, u)
                        if u == LAST and exists(g + 1):
                            combine(g + 1)

                in_groups(step)
                output(NG - 1)

            @block.tensor
            def _(pe):
                def turn(f):
                    pe.wait_ge(normed, f + 1)
                    wait(pe, lg_read, f)
                    wait(pe, c_ready, f - 2)
                    for c in (0, 1):
                        for j in range(NPAIR):
                            b = NPAIR * c + j
                            mm = pe.transpose(a_bank[c][:, L * j:L * j + L], xn[f % 3][:, b].rearrange("p a d -> p (a d)"), ident[0:L, 0:L])
                        mm.then_inc(x_turned, 1)

                def router(f):
                    for c in (0, 1):
                        pe.wait_ge(x_ready, 2 * f + 1 + c)
                        x = xs[f % 4][:, NPAIR * c:NPAIR * c + NPAIR, :]
                        pe.matmul(a_bank[c][:, 0:HALF], W.wr_hi[:], x, start=True, stop=False)
                        pe.matmul(a_bank[c][:, 0:HALF], W.wr_lo[:], x, start=False, stop=True).then_inc(r_done, 1)

                def logits(f):
                    if last:
                        pe.wait_ge(x_ready, 2 * f + 2)
                    else:
                        pe.wait_ge(r_ready, 2 * f + 2)
                    for b in range(G):
                        o = a_bank[0][0:L, D * b:D * b + D]
                        if last:
                            pe.matmul(o, xs[f % 4][:, b, :], W.wr_hi[:], start=True, stop=False)
                            mm = pe.matmul(o, xs[f % 4][:, b, :], W.wr_lo[:], start=False, stop=True)
                        else:
                            mm = pe.matmul(o, rh[:, b, :], W.wr2[:], start=True, stop=True)
                    mm.then_inc(routed, 1)

                def turn_combine(g):
                    pe.wait_ge(cp_ready, g // 2 + 1)
                    for b in range(G):
                        mm = pe.transpose(a_bank[1][0:NR, b * L // 2:(b + 1) * L // 2].bitcast(BF16),
                                          cp[:, G * (g % 2) + b].rearrange("p i j e -> p (i j e)"), ident16[0:L, 0:L])
                    mm.then_inc(c_turned, 1)

                def layer1(g, u):
                    n = g * U + u
                    k, c = u // 2, u % 2
                    wait(pe, h1_ready, n - 1)
                    x = xs[g % 4][:, NPAIR * c:NPAIR * c + NPAIR, :]
                    o = h1_bank[u % 2][:, 0:HALF]
                    pe.matmul(o, W.w1_hi[:, 2 * k:2 * k + 2, :], x, start=True, stop=False)
                    pe.matmul(o, W.w1_lo[:, 2 * k:2 * k + 2, :], x, start=False, stop=True).then_inc(h1_done, 1)

                def spread(g, u):
                    n = g * U + u
                    k, c = u // 2, u % 2
                    pe.wait_ge(c_ready, g + 1)
                    wait(pe, hm_ready, n - 1)
                    pe.matmul(cb_bank[u % 2][:, 0:HALF], W.sel[:, 128 * k:128 * k + 128], ct[g % 2][:, NPAIR * c:NPAIR * c + NPAIR, :],
                              start=True, stop=True).then_inc(cb_done, 1)

                def layer2(g, u):
                    n = g * U + u
                    pe.wait_ge(h1_ready, n + 1)
                    wait(pe, h2_ready, n)
                    pe.matmul(h2_bank[:, 0:HALF], W.w2[:, u // 2, :], h1[u % 2][:], start=True, stop=True).then_inc(h2_done, 1)

                def sum_pair(g, k):
                    pe.wait_ge(hm_ready, g * U + 2 * k + 2)
                    if k == 0:
                        wait(pe, o_ready, g)
                    for c in (0, 1):
                        mm = pe.matmul(o_bank[c * D:(c + 1) * D, 0:HALF], W.wo[:, k, :], hm[2 * k + c][:], start=(k == 0), stop=False)
                    mm.then_inc(o_pairs, 1)

                def finish_sum(g):
                    sum_pair(g, NP - 1)
                    for c in (0, 1):
                        mm = pe.matmul(o_bank[c * D:(c + 1) * D, 0:HALF], W.bo[:], ct[g % 2][:, NPAIR * c:NPAIR * c + NPAIR, :],
                                       start=False, stop=True)
                    mm.then_inc(o_done, 1)

                def turn_output(g):
                    pe.wait_ge(o_ready, g + 1)
                    f = g + 1 + AHEAD
                    if g == NG - 1:
                        pe.wait_ge(added, g)
                    if exists(f):
                        pe.wait_ge(x_ready if last else r_ready, 2 * f + 2)
                    else:
                        pe.wait_ge(c_ready, min(g + 2, NG))
                    for j in range(NPAIR):
                        mm = pe.transpose(a_bank[1][0:L, 128 * j:128 * j + 128], osb[:, L * j:L * j + L], ident[:])
                    mm.then_inc(o_turned, 1)

                for f in range(AHEAD):
                    turn(f)
                    if not last:
                        router(f)
                    logits(f)
                pe.wait_ge(cleared, n_clear)
                pe.wait_ge(x_ready if last else r_ready, 2 * AHEAD)
                turn_combine(0)
                layer1(0, 0)

                def step(g):
                    f = g + AHEAD
                    for u in range(U):
                        if u == 0 and exists(f):
                            turn(f)
                        if u < LAST:
                            layer1(g, u + 1)
                        elif exists(g + 1):
                            layer1(g + 1, 0)
                        if u == 1 and exists(f) and not last:
                            router(f)
                        if u == 2 and exists(f):
                            logits(f)
                        if not last:
                            layer2(g, u)
                        spread(g, u)
                        if u == 1 and exists(g - 1):
                            finish_sum(g - 1)
                        if u == 3 and exists(g - 1):
                            turn_output(g - 1)
                        if u % 2 == 1 and u >= 3:
                            sum_pair(g, (u - 3) // 2)
                        if u == LAST - 1 and exists(g + 1):
                            wait(pe, added, g)
                            if exists(f):
                                pe.wait_ge(x_ready if last else r_ready, 2 * f + 2)
                            turn_combine(g + 1)

                in_groups(step)
                finish_sum(NG - 1)
                turn_output(NG - 1)

            @block.vector
            def _(dve):
                row_scale(nc, dve, None, stats, mean, rstd, tmp, own, rooted)
                normalise(dve, xn[0], h, mean, rstd, 0, normed)
                ch = Chain(dve, chain)

                def low(f):
                    for c in (0, 1):
                        dve.wait_ge(x_high, 2 * f + 1 + c)
                        x = xs[f % 4][D:128, NPAIR * c:NPAIR * c + NPAIR, :]
                        dve.tensor_tensor(x, a_bank[c][D:128, 0:HALF].rearrange("p (b l) -> p b l", l=L), x.bitcast(F32),
                                          ALU.subtract).then_inc(x_ready, 1)

                def wide(t, n=2 * G):
                    return t.unsqueeze(2).broadcast_to([L, n, E])

                firsts = W.first[:].unsqueeze(1).broadcast_to([L, 2 * G, E])

                def take_logits(f):
                    dve.wait_ge(routed, f + 1)
                    bank = a_bank[0][0:L, :].rearrange("p (b d) -> p b d", d=D)[:, :, 0:E]
                    ch(dve.tensor_reduce(top[:, f % 2, :], bank, AX_X, ALU.max))
                    dve.tensor_tensor(lg[f // 2 % 2][:, G * (f % 2):G * (f % 2) + G, :], bank, wide(top[:, f % 2, :], G),
                                      ALU.subtract).then_inc(lg_read, 1)

                def route(n, k):
                    src = lg[n % 2] if last else ev
                    second = small[:, 2, :]
                    ch.settle()
                    if k == 0:
                        dve.wait_ge(lg_read, 2 * n + 2)
                        if last:
                            ch(dve.scalar_tensor_tensor(idx[:], src[:], 0.0, firsts, ALU.is_ge, ALU.mult))
                        else:
                            dve.wait_ge(exp_a, n + 1)
                            ch.mark(dve.tensor_reduce(small[:, 5, :], ev[:], AX_X, ALU.add))
                            ch(dve.scalar_tensor_tensor(idx[:], ev[:], 1.0, firsts, ALU.is_ge, ALU.mult))
                        ch(dve.tensor_reduce(small[:, 1, :], idx[:], AX_X, ALU.max))
                        ch.mark(dve.tensor_tensor(s1[:], idx[:], wide(small[:, 1, :]), ALU.is_equal))
                    if k == 1:
                        off = -BIG if last else -4.0
                        if not last:
                            ch.mark(dve.reciprocal(small[:, 6, :], small[:, 5, :]))
                        ch(dve.scalar_tensor_tensor(rest[:], s1[:], off, src[:], ALU.mult, ALU.add))
                        ins = dve.tensor_reduce(second, rest[:], AX_X, ALU.max)
                        if last:
                            ins.then_inc(exp_in, 1)
                            dve.wait_ge(exp_in, n + 1)
                        else:
                            ch(ins)
                            dve.scalar_tensor_tensor(small[:, 3, :], second, -1.0, small[:, 6, :], ALU.add, ALU.mult).then_inc(exp_in, 1)
                        ch.mark(dve.tensor_tensor(idx[:], rest[:], wide(second), ALU.subtract))
                    if k == 2:
                        ch(dve.scalar_tensor_tensor(rest[:], idx[:], 0.0, firsts, ALU.is_ge, ALU.mult))
                        ch(dve.tensor_reduce(small[:, 1, :], rest[:], AX_X, ALU.max))
                        ch.mark(dve.tensor_tensor(s2[:], rest[:], wide(small[:, 1, :]), ALU.is_equal))
                    if k == 3:
                        dve.wait_ge(exp_b, n + 1)
                        if last:
                            ch.mark(dve.tensor_scalar(small[:, 6, :], small[:, 3, :], 0.5, 0.5, ALU.mult, ALU.add))
                            ch(dve.tensor_scalar(small[:, 7, :], small[:, 3, :], -0.5, 0.5, ALU.mult, ALU.add))
                        else:
                            ch(dve.tensor_scalar(small[:, 5, :], small[:, 4, :], 1.0, None, ALU.add))
                            ch(dve.reciprocal(small[:, 6, :], small[:, 5, :]))
                            ch(dve.tensor_tensor(small[:, 7, :], small[:, 4, :], small[:, 6, :], ALU.mult))
                        ch.mark(dve.tensor_tensor(s1[:], s1[:], wide(small[:, 6, :]), ALU.mult))
                        ch(dve.tensor_tensor(s2[:], s2[:], wide(small[:, 7, :]), ALU.mult))
                        ch.mark(dve.tensor_tensor(cw[:], s1[:], s2[:], ALU.add))
                        if n == 0:
                            dve.wait_ge(cleared, 1)
                    if k >= 4:
                        wait(dve, c_turned, 2 * n)
                        for i in ((0, 1) if k == 4 else (2,)):
                            above = cw if i < 2 else rest
                            if i > 0:
                                ch(dve.tensor_tensor(rest[:], above[:], cp[:, :, i - 1, 0, 0:E], ALU.subtract))
                            ins = dve.tensor_copy(cp[:, :, i, :, 0:E], (cw if i == 0 else rest)[:].unsqueeze(2).broadcast_to([L, 2 * G, 3, E]))
                            if i == 2:
                                ins.then_inc(cp_ready, 1)
                            elif i == 0:
                                ch(ins)
                            else:
                                ch.mark(ins)

                def weigh(g, u):
                    n = g * U + u
                    dve.wait_ge(cb_done, n + 1)
                    dve.wait_ge(h1_ready if last else h2_ready, n + 1)
                    if g > 0:
                        dve.wait_ge(o_pairs, (g - 1) * NP + u // 2 + 1)
                    src = h1 if last else h2
                    dve.tensor_tensor(hm[u][:], cb_bank[u % 2][:, 0:HALF], src[u % 2][:], ALU.mult).then_inc(hm_ready, 1)

                def residual(g):
                    p = g % 2
                    dve.wait_ge(o_turned, g + 1)
                    src = a_bank[1][0:L, :].rearrange("p (j c d) -> p c j d", c=2, d=D)
                    for c in (0, 1):
                        here = h[:, G * g + NPAIR * c:G * g + NPAIR * c + NPAIR, :]
                        dst = here
                        if last:
                            if c == 0:
                                dve.wait_ge(carried, g + 1)
                                if g < 2:
                                    dve.wait_ge(cleared, n_clear)
                                else:
                                    dve.wait_ge(sent[p], g // 2 * 16)
                            dst = fin[p][:, NPAIR * c:NPAIR * c + NPAIR, :]
                        ins = dve.tensor_tensor(dst, src[:, c], here, ALU.add)
                        if c == 1:
                            ins.then_inc(added, 1)

                def statistics(g):
                    dve.wait_ge(added, g + 1)
                    for b in range(G):
                        dve.bn_stats(slot(stats, g, b), slot(h, g, b))

                for f in (0, 1):
                    low(f)
                    take_logits(f)
                low(2)
                for k in range(4):
                    route(0, k)
                take_logits(2)
                for k in (4, 5):
                    route(0, k)

                def step(g):
                    f = g + AHEAD
                    n = g // 2 + 1
                    for u in range(U):
                        if u == 0 and exists(f):
                            low(f)
                        if u == 3 and exists(f):
                            take_logits(f)
                        if u == RESIDUAL and exists(g - 1):
                            residual(g - 1)
                        if u == LAST and exists(g - 1) and not last:
                            statistics(g - 1)
                        weigh(g, u)
                        if exists(2 * n) and g % 2 == 0 and u == LAST:
                            route(n, 0)
                        if exists(2 * n) and g % 2 == 1 and u < min(LAST - 1, 5):
                            route(n, u + 1)
                            if u == 3 and LAST == 5:
                                route(n, 5)

                in_groups(step)
                residual(NG - 1)
                if not last:
                    statistics(NG - 1)


_INS = [
    "x", "L0_tok_weight", "L0_tok_bias", "L0_attn_Wq", "L0_attn_Wk", "L0_attn_Wv", "L0_attn_Wo",
    "L0_ffn_router_w1", "L0_ffn_router_b1", "L0_ffn_router_w2", "L0_ffn_router_b2",
    "L0_ffn_expert_w1", "L0_ffn_expert_b1", "L0_ffn_expert_w2", "L0_ffn_expert_b2", "L0_ffn_expert_w3", "L0_ffn_expert_b3",
    "L1_attn_Wq_comp", "L1_attn_Wkv_comp", "L1_attn_Wqc", "L1_attn_Wqr", "L1_attn_Wkc", "L1_attn_Wkr", "L1_attn_Wv",
    "L1_ffn_router_w", "L1_ffn_w1", "L1_ffn_b1", "L1_ffn_w2", "L1_ffn_b2",
]


def kernel(**inputs):
    import concourse.bacc as _bacc
    from concourse.bass_utils import run_bass_kernel_spmd as _run

    nc = _bacc.Bacc("TRN2", target_bir_lowering=False, num_devices=1)
    arrays, A = {}, {}
    for name in _INS:
        a = np.ascontiguousarray(inputs[name])
        arrays[f"in_{name}_dram"] = a
        A[name] = nc.dram_tensor(f"in_{name}_dram", a.shape, mybir.dt.from_np(a.dtype), kind="ExternalInput").ap()
    for name, a in constants().items():
        arrays[f"{name}_dram"] = np.ascontiguousarray(a)
        A[name] = nc.dram_tensor(f"{name}_dram", a.shape, mybir.dt.from_np(a.dtype), kind="ExternalInput").ap()
    out = nc.dram_tensor("out_0_dram", (B, L, D), F32, kind="ExternalOutput").ap()
    build(nc, A, out)
    r = _run(nc, [arrays], core_ids=[0])
    return r.results[0]["out_0_dram"]
```

```python
from contextlib import ExitStack

import concourse.bass as bass
import numpy as np
from concourse import mybir

F32 = mybir.dt.float32
F32R = mybir.dt.float32r
BF16 = mybir.dt.bfloat16
ALU = mybir.AluOpType
ACT = mybir.ActivationFunctionType
AX_X = mybir.AxisListType.X

B = 128
R = 64
T = 1000
PW, SW = 25, 12
L = (T - PW) // SW + 1
D = 64
G = 8
NG = B // G
NPAIR = G // 2
HALF = NPAIR * L
HS_SHIFT = SW // 2
NCH = 2 * HS_SHIFT + 1
E0, E1 = 6, 8
EP = 8
RH = 32
ROPE0 = 48
EPS = 1e-5
BIG = 1e30
NR = 9 * EP
LOAD_AT, MULTIPLY_AT, PREPARE_AT = (0, 1, 3, 5), (4, 6), (8, 9)
RING = 4
AHEAD = 3


def constants():
    l = np.arange(L)
    count = np.maximum(l, 1).astype(np.float32)
    relu_mask = (l[:, None] <= l[None, :]).astype(np.float32) / count[None, :]
    causal_bias = np.where(l[None, :] <= l[:, None], 0.0, -BIG).astype(np.float32)
    half = (D - ROPE0) // 2
    theta = (np.float32(1.0) / np.power(np.float32(10000.0), np.arange(half, dtype=np.float32) / np.float32(half))).astype(np.float32)
    angle = (np.arange(L, dtype=np.float32)[:, None] * theta[None, :]).astype(np.float32)
    cos, sin = np.cos(angle).astype(np.float32), np.sin(angle).astype(np.float32)
    rope_c, rope_s = np.ones((2, D, L), np.float32), np.zeros((2, D, L), np.float32)
    for i in range(half):
        rope_c[:, ROPE0 + 2 * i] = rope_c[:, ROPE0 + 2 * i + 1] = cos[:, i]
        rope_s[:, ROPE0 + 2 * i] = -sin[:, i]
        rope_s[:, ROPE0 + 2 * i + 1] = sin[:, i]
    out = {
        "c_ident": np.eye(128, dtype=np.float32),
        "c_relu_mask": relu_mask,
        "c_causal_bias": causal_bias,
        "c_rope_c": rope_c.reshape(2 * D, L),
        "c_rope_s": rope_s.reshape(2 * D, L),
    }
    for tag, E in (("0", E0), ("1", E1)):
        sel = np.zeros((3, 3, EP, E // 2, 2, D), np.float32)
        part = np.zeros((3, 3, EP, 3), np.float32)
        for e in range(E):
            sel[:, 0, e, e // 2, e % 2, :] = 1.0
        for j in range(3):
            part[:, j, :, j] = 1.0
        out["c_sel" + tag] = sel.reshape(9 * EP, E // 2 * 2 * D)
        out["c_part" + tag] = part.reshape(9 * EP, 3)
        out["c_first" + tag] = np.tile((E - np.arange(E)).astype(np.float32), (L, 1))
    return out


def in_groups(step, first=0):
    for g in range(first, NG):
        step(g)


def exists(g):
    return 0 <= g < NG


def wait(eng, sem, value):
    if value > 0:
        eng.wait_ge(sem, value)


class Chain:

    def __init__(self, eng, sem):
        self.eng, self.sem, self.k = eng, sem, 0

    def mark(self, ins):
        ins.then_inc(self.sem, 1)
        self.k += 1

    def settle(self):
        if self.k:
            self.eng.wait_ge(self.sem, self.k)

    def __call__(self, ins):
        self.mark(ins)
        self.settle()


class Tiles:
    pass


def slots(t, g):
    return t[:, g * G:g * G + G, :]


def slot(t, g, b):
    return t[:, g * G + b, :]


def column(t, g, b):
    return t[:, g * G + b:g * G + b + 1]


def build(nc, A, out):
    with ExitStack() as ctx:
        def sb(name, shape, dt=F32):
            return ctx.enter_context(nc.sbuf_tensor(name, shape, dt))

        banks = [ctx.enter_context(nc.psum_tensor(f"bank{i}", [128, 512], F32)) for i in range(8)]

        h = sb("h", [L, B, D])
        stats = sb("stats", [L, B, 6])
        mean = sb("mean", [L, B])
        rstd = sb("rstd", [L, B])
        tmp = sb("tmp", [L, 3, B])
        centred = sb("centred", [L, G, D])
        ident = sb("ident", [128, 128])
        ident16 = sb("ident16", [128, 128], BF16)

        def sem(name):
            return ctx.enter_context(nc.semaphore(name))

        attn = [relu_weights(nc, A, sb, sem, ident), rope_weights(nc, A, sb, sem, ident)]
        moe = [moe_weights(nc, A, sb, sem, layer) for layer in (0, 1)]

        shared = (h, stats, mean, rstd, tmp, centred)
        xn_once = [sb(f"xn_once{p}", [L, G * D]) for p in range(3)]
        xn_twice = [sb(f"xn_twice{p}", [L, G * 2 * D]) for p in range(3)]
        norm = [LayerNorm(sem, f"ln{i}", shared, xn_twice if i % 2 else xn_once, i % 2 == 1, i == 1) for i in range(4)]

        stage_patches(nc, A, banks, h, stats, ident, ident16, attn, moe, norm[0])
        Z = zeroed_tiles(sb, sem)
        stage_relu_attention(nc, banks, h, stats, ident, attn[0], norm[0], norm[1], Z)
        stage_moe(nc, banks, h, stats, ident, ident16, 0, moe[0], norm[1], norm[2], Z, None)
        stage_rope_attention(nc, banks, h, stats, ident, attn[1], norm[2], norm[3], Z)
        stage_moe(nc, banks, h, stats, ident, ident16, 1, moe[1], norm[3], None, Z, out)


def zeroed_tiles(sb, sem):
    Z = Tiles()
    Z.z = [sb(f"z{p}", [128, NPAIR, 2, L]) for p in (0, 1)]
    Z.v = [sb(f"v{p}", [128, NPAIR * 2 * D]) for p in range(4)]
    Z.pt = [sb(f"pt{p}", [128, G, L]) for p in (0, 1)]
    Z.cp = sb("cp", [L, 2 * G, 3, 3, EP], BF16)
    Z.ct = [sb(f"ct{p}", [128, G, L], BF16) for p in (0, 1)]
    Z.rh = sb("rh", [128, G, L])
    Z.pool_cleared, Z.dve_cleared = sem("z_pool_cleared"), sem("z_dve_cleared")
    return Z


def stage_patches(nc, A, banks, h, stats, ident, ident16, attn, moe, following):
    with ExitStack() as ctx:
        def sb(name, shape, dt=F32):
            return ctx.enter_context(nc.sbuf_tensor(name, shape, dt))

        def sem(name):
            return ctx.enter_context(nc.semaphore(name))

        x = A["x"].rearrange("b o r t -> (o r) b t")
        image = [sb(f"image{p}", [128, G, T]) for p in range(3)]
        weight = sb("tok_weight", [128, NCH, D])
        bias = sb("tok_bias", [128, 1])
        fm = [sb(f"tok_fm{p}", [128, HALF]) for p in (0, 1)]
        loaded = [[sem(f"image_loaded{p}{q}") for q in (0, 1)] for p in range(3)]
        weights, consts = sem("weights_loaded"), sem("consts_loaded")
        cleared = sem("tok_cleared")
        shifted = sem("image_shifted")
        summed = sem("patches_summed")
        activated = sem("patches_activated")
        turned = sem("patches_turned")
        stored = sem("patches_stored")
        own = sem("patches_own")
        w = A["L0_tok_weight"].rearrange("(r c) d -> r c d", c=PW)
        S = HS_SHIFT
        runs = ((0, 0), (S, 2 * S))
        b1 = A["L0_tok_bias"].rearrange("(d a) -> d a", a=1)

        with nc.Block() as block:
            @block.sync
            def _(sp):
                for lo, c in runs:
                    sp.dma_start(weight[0:R, lo:lo + S, :], w[:, c:c + S, :]).then_inc(weights, 16)
                    sp.dma_start(weight[R:128, lo:lo + S, :], w[:, c + S:c + 2 * S, :]).then_inc(weights, 16)
                sp.dma_start(weight[0:R, NCH - 1:NCH, :], w[:, PW - 1:PW, :]).then_inc(weights, 16)

                def load(g):
                    for q in (0, 1):
                        sp.dma_start(image[g % 3][0:R, 4 * q:4 * q + 4, :], x[:, G * g + 4 * q:G * g + 4 * q + 4, :]).then_inc(loaded[g % 3][q], 16)

                load(0)
                for q in (0, 1):
                    sp.dma_start(bias[q * D:(q + 1) * D, :], b1).then_inc(consts, 16)
                sp.dma_start(ident[:], A["c_ident"]).then_inc(consts, 16)
                load(1)
                load(2)

                def step(g):
                    if exists(g + 3):
                        sp.wait_ge(summed, g + 1)
                        load(g + 3)
                    if g in LOAD_AT:
                        (*attn, *moe)[LOAD_AT.index(g)].load(sp)

                in_groups(step)

            @block.gpsimd
            def _(pool):
                for p in range(3):
                    pool.memset(image[p][R:128, :, (L + 1) * SW:T], 0.0).then_inc(cleared, 1)
                pool.wait_ge(cleared, 3)
                for W in (*attn, *moe):
                    W.clear(pool)
                for f in range(AHEAD):
                    following.normalise(pool, f)

            @block.scalar
            def _(act):
                act.wait_ge(consts, 3 * 16)

                def step(g):
                    p = g % 2
                    act.wait_ge(summed, g + 1)
                    if g >= 2:
                        act.wait_ge(turned, g - 1)
                    act.activation(fm[p][:], banks[p][:, 0:HALF], ACT.Gelu, bias=bias[:]).then_inc(activated, 1)
                    LayerNorm.after_act(act, g, None, following)

                in_groups(step)

            @block.tensor
            def _(pe):
                pe.wait_ge(weights, 5 * 16)
                pe.wait_ge(own, 1)
                pe.wait_ge(cleared, 3)

                def turn(g, p):
                    if g == 0:
                        pe.wait_ge(consts, 3 * 16)
                    pe.wait_ge(activated, g + 1)
                    if g >= 2:
                        pe.wait_ge(stored, g - 1)
                    for j in range(NPAIR):
                        mm = pe.transpose(banks[2 + p][0:L, 128 * j:128 * j + 128], fm[p][:, L * j:L * j + L], ident[:])
                    mm.then_inc(turned, 1)

                def step(g):
                    p = g % 2
                    if g == 0:
                        for q in (0, 1):
                            pe.wait_ge(shifted, q + 1)
                            for n in range(NCH):
                                t0 = n if n < S else n + S if n < 2 * S else PW - 1
                                for s in (0, 1):
                                    mm = pe.matmul(banks[0][s * D:(s + 1) * D, q * HALF // 2:(q + 1) * HALF // 2], weight[:, n, :],
                                                   image[0][:, 4 * q + s:4 * q + 4:2, t0:t0 + SW * (L - 1) + 1:SW],
                                                   start=(n == 0), stop=(n == NCH - 1))
                        mm.then_inc(summed, 1)
                        return
                    pe.wait_ge(shifted, g * 2 + 2)
                    if g >= 2:
                        pe.wait_ge(activated, g - 1)
                    for n in range(NCH):
                        t0 = n if n < S else n + S if n < 2 * S else PW - 1
                        for s in (0, 1):
                            mm = pe.matmul(banks[p][s * D:(s + 1) * D, 0:HALF], weight[:, n, :],
                                           image[g % 3][:, s:G:2, t0:t0 + SW * (L - 1) + 1:SW],
                                           start=(n == 0), stop=(n == NCH - 1))
                    mm.then_inc(summed, 1)
                    if g >= 1:
                        turn(g - 1, 1 - p)
                    if g in MULTIPLY_AT:
                        k = MULTIPLY_AT.index(g)
                        for i in (0, 1):
                            attn[i].multiply(pe, k, banks[4 + i])

                in_groups(step)
                turn(NG - 1, (NG - 1) % 2)

            @block.vector
            def _(dve):
                dve.memset(weight[R:128, NCH - 1:NCH, :], 0.0).then_inc(own, 1)

                def store(g, p):
                    dve.wait_ge(turned, g + 1)
                    dve.tensor_copy(slots(h, g), banks[2 + p][0:L, :].rearrange("p (b d) -> p b d", d=D)).then_inc(stored, 1)
                    if exists(g + 1):
                        dve.wait_ge(stored, g + 1)
                        for b in range(G):
                            dve.bn_stats(slot(stats, g, b), slot(h, g, b))

                def shift(g):
                    p = g % 3
                    for q in (0, 1):
                        dve.wait_ge(loaded[p][q], g // 3 * 16 + 16)
                        v = image[p][:, 4 * q:4 * q + 4, 0:(L + 1) * SW].rearrange("r b (m c) -> r b m c", c=SW)
                        dve.tensor_copy(v[R:128, :, :, 0:S], v[0:R, :, :, S:SW]).then_inc(shifted, 1)

                shift(0)
                dve.wait_ge(consts, 3 * 16)
                dve.tensor_copy(ident16[:], ident[:]).then_inc(own, 1)

                def step(g):
                    if exists(g + 1):
                        shift(g + 1)
                    if exists(g - 1):
                        store(g - 1, 1 - g % 2)
                    if g in MULTIPLY_AT:
                        k = MULTIPLY_AT.index(g)
                        for i in (0, 1):
                            attn[i].place(dve, k, banks[4 + i])
                    if g in PREPARE_AT:
                        moe[PREPARE_AT.index(g)].prepare(dve)
                    LayerNorm.after_dve(dve, g, None, following)

                in_groups(step)
                store(NG - 1, (NG - 1) % 2)


class LayerNorm:

    def __init__(self, sem, name, shared, xn, doubled, delay):
        self.h, self.stats, self.mean, self.rstd, self.tmp, self.centred = shared
        self.doubled = doubled
        self.xn = xn
        self.delay = delay
        self.own, self.varied = sem(name + "_own"), sem(name + "_varied")
        self.rooted, self.scaled = sem(name + "_rooted"), sem(name + "_scaled")
        self.shifted, self.normed = sem(name + "_shifted"), sem(name + "_normed")
        self.k = 0

    def link(self, dve, ins):
        self.k += 1
        ins.then_inc(self.own, 1)
        dve.wait_ge(self.own, self.k)

    def vary(self, dve, half):
        cols = slice(half * B // 2, (half + 1) * B // 2)
        even, odd = self.stats[:, cols, 1], self.stats[:, cols, 4]
        var, d, q = (self.tmp[:, i, cols] for i in range(3))
        n = D // 2
        self.link(dve, dve.tensor_tensor(d, even, odd, ALU.subtract))
        self.link(dve, dve.scalar_tensor_tensor(var, d, float(n * n) / D / D, d, ALU.mult, ALU.mult))
        self.link(dve, dve.tensor_tensor(q, self.stats[:, cols, 2], self.stats[:, cols, 5], ALU.add))
        self.link(dve, dve.scalar_tensor_tensor(var, q, 1.0 / D, var, ALU.mult, ALU.add))
        dve.tensor_scalar(var, var, EPS, None, ALU.add).then_inc(self.varied, 1)
        self.link(dve, dve.tensor_tensor(d, even, odd, ALU.add))
        self.link(dve, dve.tensor_scalar(self.mean[:, cols], d, 0.5, None, ALU.mult))

    def root(self, act, half):
        cols = slice(half * B // 2, (half + 1) * B // 2)
        act.wait_ge(self.varied, half + 1)
        act.activation(self.rstd[:, cols], self.tmp[:, 0, cols], ACT.Sqrt).then_inc(self.rooted, 1)

    def invert(self, dve, half):
        cols = slice(half * B // 2, (half + 1) * B // 2)
        var, d, q = (self.tmp[:, i, cols] for i in range(3))
        rstd = self.rstd[:, cols]
        dve.wait_ge(self.varied, half + 1)
        dve.wait_ge(self.rooted, half + 1)
        self.link(dve, dve.reciprocal(d, rstd))
        self.link(dve, dve.tensor_tensor(q, d, d, ALU.mult))
        self.link(dve, dve.tensor_tensor(q, q, var, ALU.mult))
        self.link(dve, dve.tensor_scalar(q, q, -0.5, 1.5, ALU.mult, ALU.add))
        dve.tensor_tensor(rstd, d, q, ALU.mult).then_inc(self.scaled, 1)

    def rows(self, g):
        t = self.xn[g % 3][:]
        return t.rearrange("p (b a d) -> p b a d", a=2, d=D) if self.doubled else t.rearrange("p (b d) -> p b d", d=D)

    def normalise(self, pool, g):
        pool.wait_ge(self.scaled, 2 if g >= NG // 2 else 1)
        wait(pool, self.normed, g)
        mean, rstd = (t[:, G * g:G * g + G].unsqueeze(2) for t in (self.mean, self.rstd))
        pool.tensor_tensor(self.centred[:], slots(self.h, g), mean.broadcast_to([L, G, D]), ALU.subtract).then_inc(self.shifted, 1)
        pool.wait_ge(self.shifted, g + 1)
        if self.doubled:
            pool.tensor_tensor(self.rows(g), self.centred[:].unsqueeze(2).broadcast_to([L, G, 2, D]),
                               rstd.unsqueeze(3).broadcast_to([L, G, 2, D]), ALU.mult).then_inc(self.normed, 1)
        else:
            pool.tensor_tensor(self.rows(g), self.centred[:], rstd.broadcast_to([L, G, D]), ALU.mult).then_inc(self.normed, 1)

    @staticmethod
    def after_dve(dve, g, mine, following):
        if mine is not None and g == 0:
            for b in range(G):
                ins = dve.bn_stats(slot(mine.stats, NG - 1, b), slot(mine.h, NG - 1, b))
            mine.link(dve, ins)
        if mine is not None and g == 1:
            mine.vary(dve, 1)
        if mine is not None and g == 2 + mine.delay:
            mine.invert(dve, 1)
        if following is not None and g == 10:
            if mine is not None:
                dve.wait_ge(mine.normed, NG // 2)
            following.vary(dve, 0)
        if following is not None and g == 12:
            following.invert(dve, 0)

    @staticmethod
    def after_act(act, g, mine, following):
        if mine is not None and g == 1 + mine.delay:
            mine.root(act, 1)
        if following is not None and g == 11:
            following.root(act, 0)


def relu_weights(nc, A, sb, sem, ident):
    W = Tiles()
    raw = sb("ra_raw", [D, 4, D])
    wo_t = sb("ra_wo_t", [D, D])
    W.qk = sb("ra_w_qk", [128, 128])
    W.vo = sb("ra_w_vo", [128, 128])
    W.mask = sb("ra_mask", [L, L])
    loaded, cleared, in_bank, placed = sem("ra_loaded"), sem("ra_cleared"), sem("ra_in_bank"), sem("ra_placed")

    def clear(pool):
        for t in (W.qk, W.vo):
            pool.memset(t[:], 0.0).then_inc(cleared, 1)

    def load(eng):
        for i, n in enumerate(("L0_attn_Wq", "L0_attn_Wk", "L0_attn_Wv", "L0_attn_Wo")):
            eng.dma_start(raw[:, i, :], A[n]).then_inc(loaded, 16)
        eng.dma_start(W.mask[:], A["c_relu_mask"]).then_inc(loaded, 16)

    def multiply(pe, k, bank):
        if k == 0:
            pe.wait_ge(loaded, 5 * 16)
            for s in (0, 1):
                pe.matmul(bank[s * D:(s + 1) * D, s * D:(s + 1) * D], raw[:, 0, :], raw[:, 1, :], start=True, stop=True)
            pe.transpose(bank[0:D, 3 * D:4 * D], raw[:, 3, :], ident[0:D, 0:D]).then_inc(in_bank, 1)
        else:
            pe.wait_ge(placed, 3)
            for s in (0, 1):
                mm = pe.matmul(bank[s * D:(s + 1) * D, s * D:(s + 1) * D], raw[:, 2, :], wo_t[:], start=True, stop=True)
            mm.then_inc(in_bank, 1)

    def place(dve, k, bank):
        dve.wait_ge(cleared, 2)
        dve.wait_ge(in_bank, k + 1)
        for s in (0, 1):
            block = slice(s * D, (s + 1) * D)
            dve.tensor_copy((W.vo if k else W.qk)[block, block], bank[block, block]).then_inc(placed, 1)
        if k == 0:
            dve.tensor_copy(wo_t[:], bank[0:D, 3 * D:4 * D]).then_inc(placed, 1)

    W.clear, W.load, W.multiply, W.place = clear, load, multiply, place
    return W


def rope_weights(nc, A, sb, sem, ident):
    W = Tiles()
    comp = sb("sa_comp", [D, 2, D])
    comp_t = sb("sa_comp_t", [D, 2, D])
    heads = sb("sa_heads", [D, 3, D])
    W.w = sb("sa_w", [128, 5, 128])
    W.rope = sb("sa_rope", [128, 2, L])
    W.bias = sb("sa_bias", [L, L])
    loaded, cleared, in_bank, placed = sem("sa_loaded"), sem("sa_cleared"), sem("sa_in_bank"), sem("sa_placed")

    def clear(pool):
        pool.memset(W.w[:], 0.0).then_inc(cleared, 1)

    def load(eng):
        for i, n in enumerate(("L1_attn_Wq_comp", "L1_attn_Wkv_comp")):
            eng.dma_start(comp[:, i, :], A[n]).then_inc(loaded, 16)
        for i, n in enumerate(("L1_attn_Wqc", "L1_attn_Wkc")):
            eng.dma_start(heads[:, i, 0:ROPE0], A[n]).then_inc(loaded, 16)
        for i, n in enumerate(("L1_attn_Wqr", "L1_attn_Wkr")):
            eng.dma_start(heads[:, i, ROPE0:D], A[n]).then_inc(loaded, 16)
        eng.dma_start(heads[:, 2, :], A["L1_attn_Wv"]).then_inc(loaded, 16)
        eng.dma_start(W.rope[:, 0, :], A["c_rope_c"]).then_inc(loaded, 16)
        eng.dma_start(W.rope[:, 1, :], A["c_rope_s"]).then_inc(loaded, 16)
        eng.dma_start(W.bias[:], A["c_causal_bias"]).then_inc(loaded, 16)

    def multiply(pe, k, bank):
        if k == 0:
            pe.wait_ge(loaded, 10 * 16)
            for i in (0, 1):
                mm = pe.transpose(bank[0:D, D * i:D * i + D], comp[:, i, :], ident[0:D, 0:D])
            mm.then_inc(in_bank, 1)
        else:
            pe.wait_ge(placed, 1)
            for i in range(3):
                for s in (0, 1):
                    mm = pe.matmul(bank[s * D:(s + 1) * D, D * i:D * i + D], comp_t[:, min(i, 1), :], heads[:, i, :], start=True, stop=True)
            mm.then_inc(in_bank, 1)

    def place(dve, k, bank):
        dve.wait_ge(in_bank, k + 1)
        if k == 0:
            dve.tensor_copy(comp_t[:], bank[0:D, 0:2 * D].rearrange("p (i d) -> p i d", d=D)).then_inc(placed, 1)
            return
        dve.wait_ge(cleared, 1)
        for s in (0, 1):
            rows, cols = slice(s * D, (s + 1) * D), slice(s * D, (s + 1) * D)
            for i, at in ((0, 0), (1, 1), (2, 4)):
                dve.tensor_copy(W.w[rows, at, cols], bank[rows, D * i:D * i + D])
            for i in (0, 1):
                for a in (0, 1):
                    dve.tensor_copy(W.w[rows, 2 + i, s * D + ROPE0 + a:(s + 1) * D:2], bank[rows, D * i + ROPE0 + 1 - a:D * i + D:2])

    W.clear, W.load, W.multiply, W.place = clear, load, multiply, place
    return W


def stage_relu_attention(nc, banks, h, stats, ident, W, mine, following, Z):
    with ExitStack() as ctx:
        def sb(name, shape, dt=F32):
            return ctx.enter_context(nc.sbuf_tensor(name, shape, dt))

        def sem(name):
            return ctx.enter_context(nc.semaphore("ra_" + name))

        xt = [sb(f"ra_xt{p}", [128, HALF]) for p in (0, 1)]
        x_bank, q_bank, v_bank, s_bank, o_bank = banks[0], banks[1], banks[2], banks[3:5], banks[5:7]

        normed = mine.normed
        qz, v, pt = Z.z, Z.v, Z.pt
        x_turned = sem("x_turned")
        x_ready = sem("x_ready")
        q_done = sem("q_done")
        v_done = sem("v_done")
        q_ready = sem("q_ready")
        v_ready = sem("v_ready")
        scored = sem("scored")
        weighed = sem("weighed")
        mixed = sem("mixed")
        added = sem("added")

        with nc.Block() as block:
            @block.gpsimd
            def _(pool):
                for t in (*qz, *v):
                    pool.memset(t[:], 0.0).then_inc(Z.pool_cleared, 1)
                pool.wait_ge(Z.pool_cleared, 6)

                def step(f):
                    wait(pool, x_turned, f - 2)
                    mine.normalise(pool, f)

                in_groups(step, AHEAD)
                pool.wait_ge(normed, NG)
                for i, t in enumerate((Z.rh, *Z.ct, Z.cp)):
                    pool.memset(t[:], 0.0).then_inc(Z.pool_cleared, 1)
                    pool.wait_ge(Z.pool_cleared, 7 + i)
                    if i == 0:
                        pool.memset(Z.rh[RH:RH + 1, :, :], 1.0).then_inc(Z.dve_cleared, 1)
                        pool.wait_ge(Z.dve_cleared, 3)
                for f in range(AHEAD):
                    following.normalise(pool, f)

            @block.scalar
            def _(act):

                def copy_x(g):
                    act.wait_ge(x_turned, g + 1)
                    act.activation(xt[g % 2][:], x_bank[:, 0:HALF], ACT.Copy).then_inc(x_ready, 1)

                def copy_qv(g):
                    act.wait_ge(q_done, g + 1)
                    wait(act, scored, 2 * g - 2)
                    if g == 0:
                        act.wait_ge(Z.pool_cleared, 2)
                    for s in (0, 1):
                        rows = slice(s * D, (s + 1) * D)
                        act.activation(qz[g % 2][rows, :, s, :], q_bank[rows, 0:HALF].rearrange("p (j l) -> p j l", l=L), ACT.Copy).then_inc(q_ready, 1)
                    act.wait_ge(v_done, g + 1)
                    wait(act, mixed, g - 2)
                    if g == 0:
                        act.wait_ge(Z.pool_cleared, 6)
                    act.activation(v[g % 3][0:L, :], v_bank[0:L, :], ACT.Copy).then_inc(v_ready, 1)

                copy_x(0)
                copy_x(1)
                copy_qv(0)

                def step(g):
                    if exists(g + 2):
                        copy_x(g + 2)
                    if exists(g + 1):
                        copy_qv(g + 1)
                    LayerNorm.after_act(act, g, mine, following)

                in_groups(step)

            @block.tensor
            def _(pe):
                def turn(g):
                    pe.wait_ge(normed, g + 1)
                    wait(pe, x_ready, g)
                    for j in range(NPAIR):
                        mm = pe.transpose(x_bank[:, L * j:L * j + L], mine.rows(g)[:, 2 * j:2 * j + 2, :], ident[0:L, 0:L])
                    mm.then_inc(x_turned, 1)

                def project(g):
                    pe.wait_ge(x_ready, g + 1)
                    wait(pe, q_ready, 2 * g)
                    pe.matmul(q_bank[:, 0:HALF], W.qk[:], xt[g % 2][:], start=True, stop=True).then_inc(q_done, 1)
                    wait(pe, v_ready, g)
                    for j in range(NPAIR):
                        mm = pe.matmul(v_bank[0:L, 128 * j:128 * j + 128], xt[g % 2][:, L * j:L * j + L], W.vo[:], start=True, stop=True)
                    mm.then_inc(v_done, 1)

                def mix(g):
                    pe.wait_ge(v_ready, g + 1)
                    pe.wait_ge(weighed, 2 * g + 2)
                    wait(pe, added, g - 1)
                    for b in range(G):
                        mm = pe.matmul(o_bank[g % 2][0:L, D * b:D * b + D], pt[g % 2][:, b, :], v[g % 3][:, D * b:D * b + D], start=True, stop=True)
                    mm.then_inc(mixed, 1)

                turn(0)
                turn(1)
                project(0)

                def step(g):
                    pe.wait_ge(q_ready, 2 * g + 2)
                    for c in (0, 1):
                        wait(pe, weighed, 2 * g - 1 + c)
                        for j in (2 * c, 2 * c + 1):
                            mm = pe.matmul(s_bank[c][0:L, (j % 2) * 2 * L:(j % 2 + 1) * 2 * L], xt[g % 2][:, L * j:L * j + L],
                                           qz[g % 2][:, j, :, :], start=True, stop=True)
                        mm.then_inc(scored, 1)
                    if exists(g + 2):
                        turn(g + 2)
                    if exists(g + 1):
                        project(g + 1)
                    if exists(g - 1):
                        mix(g - 1)

                in_groups(step)
                mix(NG - 1)

            @block.vector
            def _(dve):
                for i, t in enumerate(pt):
                    dve.memset(t[:], 0.0).then_inc(Z.dve_cleared, 1)
                dve.wait_ge(Z.dve_cleared, 2)

                def add(g):
                    dve.wait_ge(mixed, g + 1)
                    dve.tensor_tensor(slots(h, g), o_bank[g % 2][0:L, :].rearrange("p (b d) -> p b d", d=D), slots(h, g), ALU.add).then_inc(added, 1)

                def statistics(g):
                    dve.wait_ge(added, g + 1)
                    for b in range(G):
                        dve.bn_stats(slot(stats, g, b), slot(h, g, b))

                def step(g):
                    for c in (0, 1):
                        dve.wait_ge(scored, 2 * g + 1 + c)
                        wait(dve, mixed, g - 1)
                        dve.scalar_tensor_tensor(
                            pt[g % 2][0:L, NPAIR * c:NPAIR * c + NPAIR, :], s_bank[c][0:L, 0:HALF].rearrange("p (b l) -> p b l", l=L), 0.0,
                            W.mask[:].unsqueeze(1).broadcast_to([L, NPAIR, L]), ALU.max, ALU.mult).then_inc(weighed, 1)
                    if exists(g - 2):
                        statistics(g - 2)
                    if exists(g - 1):
                        add(g - 1)
                    LayerNorm.after_dve(dve, g, mine, following)

                in_groups(step)
                statistics(NG - 2)
                add(NG - 1)


def stage_rope_attention(nc, banks, h, stats, ident, W, mine, following, Z):
    with ExitStack() as ctx:
        def sb(name, shape, dt=F32):
            return ctx.enter_context(nc.sbuf_tensor(name, shape, dt))

        def sem(name):
            return ctx.enter_context(nc.semaphore("sa_" + name))

        w, rope, bias = W.w, W.rope, W.bias
        xt = [sb(f"sa_xt{p}", [128, HALF]) for p in (0, 1)]
        turn_c = sb("sa_turn_c", [128, 2, NPAIR, L])
        turn_s = sb("sa_turn_s", [128, 2, NPAIR, L])
        q = [sb(f"sa_q{p}", [128, NPAIR, L]) for p in (0, 1)]
        masked = [sb(f"sa_masked{p}", [L, G, L]) for p in (0, 1)]
        top = sb("sa_top", [L, G])
        low = [sb(f"sa_low{p}", [L, G]) for p in (0, 1)]
        prob = [sb(f"sa_prob{p}", [L, G, L]) for p in (0, 1)]
        total = [sb(f"sa_total{p}", [L, G]) for p in (0, 1)]
        share = sb("sa_share", [L, G])
        mixed_sb = sb("sa_mixed", [L, G, D])
        unused = sb("sa_unused", [L, 1])
        xo_bank, v_bank = banks[0], banks[1]
        qk_bank, sw_bank, s_bank = banks[2:4], banks[4:6], banks[6:8]
        p_bank = sw_bank

        normed = mine.normed
        kz, v, pt = Z.z, Z.v, Z.pt
        x_turned = sem("x_turned")
        x_ready = sem("x_ready")
        qk_done = sem("qk_done")
        sw_done = sem("sw_done")
        v_done = sem("v_done")
        v_ready = sem("v_ready")
        cos_done = sem("cos_done")
        sin_done = sem("sin_done")
        rotated = sem("rotated")
        scored = sem("scored")
        biased = sem("biased")
        topped = sem("topped")
        shifted = sem("shifted")
        raised = sem("raised")
        p_turned = sem("p_turned")
        p_ready = sem("p_ready")
        mixed = sem("mixed")
        shared = sem("shared")
        scaled = sem("scaled")
        added = sem("added")
        SCALE = float(D) ** -0.5

        with nc.Block() as block:
            @block.gpsimd
            def _(pool):
                def normal(f):
                    wait(pool, rotated, 3 * (f - 2))
                    wait(pool, x_turned, f - 2)
                    mine.normalise(pool, f)

                def rotate(g):
                    p = g % 2
                    pool.wait_ge(normed, min(g + 3, NG))
                    pool.wait_ge(cos_done, g + 1)
                    pool.wait_ge(sin_done, g + 1)
                    wait(pool, scored, 2 * g - 2)
                    pool.tensor_tensor(q[p][:], turn_c[:, 0], turn_s[:, 0], ALU.add).then_inc(rotated, 1)
                    pool.wait_ge(rotated, 3 * g + 1)
                    for s in (0, 1):
                        ins = pool.tensor_tensor(kz[p][s * D:(s + 1) * D, :, s, :], turn_c[s * D:(s + 1) * D, 1],
                                                 turn_s[s * D:(s + 1) * D, 1], ALU.add)
                        ins.then_inc(rotated, 1)

                def step(g):
                    rotate(g)
                    if exists(g + 3):
                        normal(g + 3)
                    else:
                        f = g + 3 - NG
                        pool.wait_ge(rotated, 3 * g + 3)
                        following.normalise(pool, f)
                        pool.wait_ge(following.normed, f + 1)

                in_groups(step)

            @block.scalar
            def _(act):
                def copy_x(g):
                    act.wait_ge(x_turned, g + 1)
                    act.activation(xt[g % 2][:], xo_bank[:, 0:HALF], ACT.Copy).then_inc(x_ready, 1)

                def copy_v(g):
                    act.wait_ge(v_done, g + 1)
                    wait(act, mixed, g - 3)
                    act.activation(v[g % 4][0:L, :], v_bank[0:L, :], ACT.Copy).then_inc(v_ready, 1)

                def copy_p(g):
                    act.wait_ge(p_turned, g + 1)
                    wait(act, mixed, g - 1)
                    for c in (0, 1):
                        act.activation(pt[g % 2][0:L, NPAIR * c:NPAIR * c + NPAIR, :], p_bank[c][0:L, 0:HALF].rearrange("p (b l) -> p b l", l=L),
                                       ACT.Copy).then_inc(p_ready, 1)

                def raise_(g):
                    act.wait_ge(shifted, g + 1)
                    wait(act, p_turned, g - 1)
                    wait(act, shared, g - 1)
                    for b in range(G):
                        act.activation(prob[g % 2][:, b, :], masked[g % 2][:, b, :], ACT.Exp, bias=low[g % 2][:, b:b + 1], scale=SCALE,
                                       accum_out=total[g % 2][:, b:b + 1]).then_inc(raised, 1)

                copy_x(0)
                copy_x(1)
                act.activation(unused[:], W.bias[:, 0:1], ACT.Exp)
                copy_v(0)
                copy_x(2)
                copy_v(1)

                def step(g):
                    if exists(g - 1):
                        copy_p(g - 1)
                    if exists(g + 3):
                        copy_x(g + 3)
                    raise_(g)
                    if exists(g + 2):
                        copy_v(g + 2)
                    LayerNorm.after_act(act, g, mine, following)

                in_groups(step)
                copy_p(NG - 1)

            @block.tensor
            def _(pe):
                def turn(g):
                    pe.wait_ge(normed, g + 1)
                    wait(pe, x_ready, g)
                    wait(pe, scaled, g - 4)
                    for j in range(NPAIR):
                        mm = pe.transpose(xo_bank[:, L * j:L * j + L], mine.rows(g)[:, 2 * j:2 * j + 2, :], ident[0:L, 0:L])
                    mm.then_inc(x_turned, 1)

                def project(g):
                    x = xt[g % 2][:]
                    pe.wait_ge(x_ready, g + 1)
                    wait(pe, cos_done, g)
                    for i in (0, 1):
                        mm = pe.matmul(qk_bank[i][:, 0:HALF], w[:, i, :], x, start=True, stop=True)
                    mm.then_inc(qk_done, 1)
                    wait(pe, sin_done, g)
                    wait(pe, p_ready, 2 * g - 4)
                    for i in (0, 1):
                        mm = pe.matmul(sw_bank[i][:, 0:HALF], w[:, 2 + i, :], x, start=True, stop=True)
                    mm.then_inc(sw_done, 1)

                def project_v(g):
                    wait(pe, v_ready, g)
                    for j in range(NPAIR):
                        mm = pe.matmul(v_bank[0:L, 128 * j:128 * j + 128], xt[g % 2][:, L * j:L * j + L], w[:, 4, :], start=True, stop=True)
                    mm.then_inc(v_done, 1)

                def score(g):
                    pe.wait_ge(rotated, 3 * g + 3)
                    for c in (0, 1):
                        wait(pe, biased, 2 * g - 1 + c)
                        for j in (2 * c, 2 * c + 1):
                            mm = pe.matmul(s_bank[c][0:L, (j % 2) * 2 * L:(j % 2 + 1) * 2 * L], q[g % 2][:, j, :],
                                           kz[g % 2][:, j, :, :], start=True, stop=True)
                        mm.then_inc(scored, 1)

                def turn_p(g):
                    pe.wait_ge(sin_done, min(g + 3, NG))
                    pe.wait_ge(raised, G * g + G)
                    for b in range(G):
                        mm = pe.transpose(p_bank[b // NPAIR][0:L, L * (b % NPAIR):L * (b % NPAIR) + L], prob[g % 2][:, b, :], ident[0:L, 0:L])
                    mm.then_inc(p_turned, 1)

                def mix(g):
                    pe.wait_ge(v_ready, g + 1)
                    pe.wait_ge(p_ready, 2 * g + 2)
                    pe.wait_ge(x_ready, min(g + 5, NG))
                    wait(pe, scaled, g)
                    for b in range(G):
                        mm = pe.matmul(xo_bank[0:L, D * b:D * b + D], pt[g % 2][:, b, :], v[g % 4][:, D * b:D * b + D], start=True, stop=True)
                    mm.then_inc(mixed, 1)

                turn(0)
                turn(1)
                project(0)
                project_v(0)
                turn(2)
                project(1)
                project_v(1)

                def step(g):
                    if exists(g + 1):
                        score(g)
                    if exists(g - 1):
                        turn_p(g - 1)
                    if g == NG - 2:
                        score(NG - 1)
                    if exists(g + 3):
                        turn(g + 3)
                    if exists(g + 2):
                        project(g + 2)
                    if exists(g - 1):
                        mix(g - 1)
                    if exists(g + 2):
                        project_v(g + 2)

                in_groups(step)
                turn_p(NG - 1)
                mix(NG - 1)

            @block.vector
            def _(dve):
                def rope_parts(g):
                    dve.wait_ge(qk_done, g + 1)
                    wait(dve, rotated, 3 * g)
                    for i in (0, 1):
                        ins = dve.tensor_tensor(turn_c[:, i], qk_bank[i][:, 0:HALF].rearrange("p (j l) -> p j l", l=L),
                                                rope[:, 0, :].unsqueeze(1).broadcast_to([128, NPAIR, L]), ALU.mult)
                    ins.then_inc(cos_done, 1)
                    dve.wait_ge(sw_done, g + 1)
                    for i in (0, 1):
                        ins = dve.tensor_tensor(turn_s[:, i], sw_bank[i][:, 0:HALF].rearrange("p (j l) -> p j l", l=L),
                                                rope[:, 1, :].unsqueeze(1).broadcast_to([128, NPAIR, L]), ALU.mult)
                    ins.then_inc(sin_done, 1)

                def mask(g):
                    for c in (0, 1):
                        dve.wait_ge(scored, 2 * g + 1 + c)
                        dve.tensor_tensor(masked[g % 2][:, NPAIR * c:NPAIR * c + NPAIR, :], s_bank[c][0:L, 0:HALF].rearrange("p (b l) -> p b l", l=L),
                                          bias[:].unsqueeze(1).broadcast_to([L, NPAIR, L]), ALU.add).then_inc(biased, 1)
                    dve.wait_ge(biased, 2 * g + 2)
                    dve.tensor_reduce(top[:], masked[g % 2][:], AX_X, ALU.max).then_inc(topped, 1)
                    dve.wait_ge(topped, g + 1)
                    dve.tensor_scalar(low[g % 2][:], top[:], -SCALE, None, ALU.mult).then_inc(shifted, 1)

                def add(g):
                    dve.wait_ge(raised, G * g + G)
                    dve.reciprocal(share[:], total[g % 2][:]).then_inc(shared, 1)
                    dve.wait_ge(shared, g + 1)
                    dve.wait_ge(mixed, g + 1)
                    dve.tensor_tensor(mixed_sb[:], xo_bank[0:L, :].rearrange("p (b d) -> p b d", d=D),
                                      share[:].unsqueeze(2).broadcast_to([L, G, D]), ALU.mult).then_inc(scaled, 1)
                    dve.wait_ge(scaled, g + 1)
                    dve.tensor_tensor(slots(h, g), mixed_sb[:], slots(h, g), ALU.add).then_inc(added, 1)

                def statistics(g):
                    dve.wait_ge(added, g + 1)
                    for b in range(G):
                        dve.bn_stats(slot(stats, g, b), slot(h, g, b))

                rope_parts(0)
                rope_parts(1)

                def step(g):
                    if exists(g + 1):
                        mask(g)
                    if g == NG - 2:
                        mask(NG - 1)
                    if exists(g + 2):
                        rope_parts(g + 2)
                    if exists(g - 2):
                        statistics(g - 2)
                    if exists(g - 1):
                        add(g - 1)
                    LayerNorm.after_dve(dve, g, mine, following)

                in_groups(step)
                statistics(NG - 2)
                add(NG - 1)


def moe_weights(nc, A, sb, sem, layer):
    last = layer == 1
    E = E1 if last else E0
    NP = E // 2
    tag = f"m{layer}_"
    W = Tiles()
    W.w1_raw = sb(tag + "w1_raw", [128, E, D])
    W.w1_hi, W.w1_lo = sb(tag + "w1_hi", [128, E, D], F32R), sb(tag + "w1_lo", [128, E, D], F32R)
    W.b1 = sb(tag + "b1", [128, NP])
    RC = D if last else 128
    W.wr_raw = sb(tag + "wr_raw", [128, RC])
    if last:
        W.wr = sb(tag + "wr", [128, RC], F32R)
    else:
        W.wr_hi, W.wr_lo = sb(tag + "wr_hi", [128, RC], F32R), sb(tag + "wr_lo", [128, RC], F32R)
    W.wo = sb(tag + "wo", [128, NP, D])
    W.bo_raw, W.bo_rest = sb(tag + "bo_raw", [NR, D]), sb(tag + "bo_rest", [NR, D])
    W.bo_part = sb(tag + "bo_part", [NR, D], BF16)
    W.bo_sum = sb(tag + "bo_sum", [NR, D])
    W.bo = sb(tag + "bo", [128, D], BF16)
    W.part = sb(tag + "part", [NR, 3])
    W.sel_raw = sb(tag + "sel_raw", [NR, NP * 128])
    W.sel = sb(tag + "sel", [128, NP * 128], BF16)
    W.first = sb(tag + "first", [L, E])
    if not last:
        W.w2 = sb(tag + "w2", [128, NP, 128])
        W.b2 = sb(tag + "b2", [128, NP])
        W.br1 = sb(tag + "br1", [RH, 1])
        W.wr2 = sb(tag + "wr2", [128, D])
    W.loaded, W.cleared, W.prepared = sem(tag + "loaded"), sem(tag + "cleared"), sem(tag + "prepared")
    zeroed = (W.wr_raw, W.bo, W.bo_raw, W.sel) + (() if last else (W.w2, W.wr2))
    W.n_loads, W.n_prepared = 0, 14

    def clear(pool):
        for i, t in enumerate(zeroed):
            pool.memset(t[:], 0.0).then_inc(W.cleared, 1)
            pool.wait_ge(W.cleared, i + 1)

    def load(eng):
        def get(dst, src):
            W.n_loads += 1
            eng.dma_start(dst, src).then_inc(W.loaded, 16)

        w_in, b_in = A["L1_ffn_w1" if last else "L0_ffn_expert_w1"], A["L1_ffn_b1" if last else "L0_ffn_expert_b1"]
        w_out, b_out = A["L1_ffn_w2" if last else "L0_ffn_expert_w3"], A["L1_ffn_b2" if last else "L0_ffn_expert_b3"]
        eng.wait_ge(W.cleared, len(zeroed))
        with nc.allow_non_contiguous_dma(reason="small biases"):
            for s in (0, 1):
                get(W.w1_raw[s * D:(s + 1) * D, :, :], w_in.rearrange("e d h -> d e h"))
                get(W.b1[s * D:(s + 1) * D, :], b_in.rearrange("(k e) h -> e h k", e=2)[s])
                get(W.wo[s * D:(s + 1) * D, :, :], w_out.rearrange("(k e) h d -> e h k d", e=2)[s])
            for i in range(9):
                get(W.bo_raw[i * EP:i * EP + E, :], b_out)
            get(W.part[:], A[f"c_part{layer}"])
            get(W.sel_raw[:], A[f"c_sel{layer}"])
            get(W.first[:], A[f"c_first{layer}"])
            for s in (0, 1):
                if last:
                    get(W.wr_raw[s * D:(s + 1) * D, 0:E], A["L1_ffn_router_w"].rearrange("e d -> d e"))
                else:
                    get(W.wr_raw[s * D:(s + 1) * D, 0:RH], A["L0_ffn_router_w1"])
                    get(W.b2[s * D:(s + 1) * D, :], A["L0_ffn_expert_b2"].rearrange("(k e) h -> e h k", e=2)[s])
            if not last:
                for e in range(E):
                    s = e % 2
                    get(W.w2[s * D:(s + 1) * D, e // 2, s * D:(s + 1) * D], A["L0_ffn_expert_w2"][e])
                get(W.br1[:], A["L0_ffn_router_b1"].rearrange("(r a) -> r a", a=1))
                get(W.wr2[0:RH, 0:E], A["L0_ffn_router_w2"])
                get(W.wr2[RH:RH + 1, 0:E], A["L0_ffn_router_b2"].rearrange("(a e) -> a e", a=1))

    def prepare(dve):
        done = 0

        def link(ins):
            nonlocal done
            done += 1
            ins.then_inc(W.prepared, 1)
            dve.wait_ge(W.prepared, done)

        dve.wait_ge(W.loaded, W.n_loads * 16)
        for raw, hi, lo in ((W.w1_raw, W.w1_hi, W.w1_lo),) + (() if last else ((W.wr_raw, W.wr_hi, W.wr_lo),)):
            link(dve.tensor_copy(hi[:], raw[:]))
            link(dve.tensor_tensor(lo[:], raw[:], hi[:].bitcast(F32), ALU.subtract))
        if last:
            link(dve.tensor_copy(W.wr[:], W.wr_raw[:]))
            link(dve.tensor_tensor(W.wr[:, E:2 * E], W.wr_raw[:, 0:E], W.wr[:, 0:E].bitcast(F32), ALU.subtract))
        link(dve.tensor_copy(W.sel[0:NR, :], W.sel_raw[:]))
        for j in range(3):
            src = W.bo_raw if j == 0 else W.bo_rest
            link(dve.tensor_copy(W.bo_part[:], src[:]))
            if j == 0:
                link(dve.tensor_scalar(W.bo_sum[:], W.bo_part[:], W.part[:, j:j + 1], None, ALU.mult))
            else:
                link(dve.scalar_tensor_tensor(W.bo_sum[:], W.bo_part[:], W.part[:, j:j + 1], W.bo_sum[:], ALU.mult, ALU.add))
            if j < 2:
                link(dve.tensor_tensor(W.bo_rest[:], src[:], W.bo_part[:], ALU.subtract))
        link(dve.tensor_copy(W.bo[0:NR, :], W.bo_sum[:]))
        assert done == W.n_prepared, done

    W.clear, W.load, W.prepare = clear, load, prepare
    return W


def stage_moe(nc, banks, h, stats, ident, ident16, layer, W, mine, following, Z, out):
    last = layer == 1
    E = E1 if last else E0
    NP = E // 2
    U = 2 * NP
    LAST = U - 1
    if last:
        FRONT, RESIDUAL, TAKE, TURN, STATISTICS, SECOND = 4, 4, 3, (6, 6), (), (0, 4)
        ROUTE = {(0, 1): (0,), (0, 3): (1,), (0, 5): (2,), (0, 6): (3,), (0, 7): (4,), (1, 0): (5,), (1, 1): (6,), (1, 3): (7,)}
        FIRST_ROUTE = {4: (0,), 5: (1,), 6: (2,), 7: (3, 4)}
    else:
        FRONT, RESIDUAL, TAKE, TURN, STATISTICS, SECOND = 3, 4, 3, (4, 5), (0, 1, 2, 4), (1, 1)
        ROUTE = {(0, 4): (0,), (0, 5): (1,), (1, 0): (2,), (1, 1): (3, 4), (1, 2): (5, 6), (1, 3): (7,)}

    def ahead(g, u, at):
        if g == 0 and FRONT > AHEAD:
            return {at: FRONT - 1, at + 4: FRONT}.get(u)
        return g + FRONT if u == at and exists(g + FRONT) else None

    with ExitStack() as ctx:
        def sb(name, shape, dt=F32):
            return ctx.enter_context(nc.sbuf_tensor(f"m{layer}_{name}", shape, dt))

        def sem(name):
            return ctx.enter_context(nc.semaphore(f"m{layer}_{name}"))

        xs = [sb(f"xs{p}", [128, G, L], F32R) for p in range(FRONT + 1)]
        h1 = [sb(f"h1_{n}", [128, HALF]) for n in range(RING)]
        h2 = None if last else [sb(f"h2_{n}", [128, HALF]) for n in range(RING)]
        hm = [sb(f"hm{u}", [128, HALF]) for u in range(U)]
        osb = sb("osb", [128, HALF])
        unused = sb("unused", [L, 1])
        lg = [sb(f"lg{p}", [L, 2 * G, E]) for p in (0, 1)]
        top = sb("top", [L, 2, G])
        ev, idx = sb("ev", [L, 2 * G, E]), sb("idx", [L, 2 * G, E])
        s1, s2 = sb("s1", [L, 2 * G, E]), sb("s2", [L, 2 * G, E])
        cw, rest = sb("cw", [L, 2 * G, E]), sb("rest", [L, 2 * G, E])
        small = sb("small", [L, 8, 2 * G])
        fin = [sb(f"fin{p}", [L, G, D]) for p in (0, 1)] if last else None

        a_bank, o_bank = banks[0:2], banks[2]
        h1_bank = [banks[3], banks[4]] if last else [banks[3]] * 2
        h2_bank = None if last else [banks[4], banks[7]]
        cb_bank = banks[5:8] if last else banks[5:7]

        normed = mine.normed
        cp, ct, rh = Z.cp, Z.ct, Z.rh
        carried = sem("carried")
        x_turned = sem("x_turned")
        x_high = sem("x_high")
        x_ready = sem("x_ready")
        r_done = sem("r_done")
        r_ready = sem("r_ready")
        routed = sem("routed")
        lg_read = sem("lg_read")
        exp_a, exp_in, exp_b = sem("exp_a"), sem("exp_in"), sem("exp_b")
        cp_ready = sem("cp_ready")
        c_turned = sem("c_turned")
        c_ready = sem("c_ready")
        h1_done, h1_ready = sem("h1_done"), sem("h1_ready")
        h2_done, h2_ready = sem("h2_done"), sem("h2_ready")
        cb_done = sem("cb_done")
        hm_ready = sem("hm_ready")
        o_pairs = sem("o_pairs")
        o_done = sem("o_done")
        o_ready = sem("o_ready")
        o_turned = sem("o_turned")
        added = sem("added")
        chain = sem("chain")
        sent = [sem(f"sent{p}") for p in (0, 1)] if last else None

        def front(f):
            return cb_bank if f == 1 else a_bank

        with nc.Block() as block:
            @block.sync
            def _(sp):
                if last:
                    dst = out.rearrange("b l d -> l b d")

                    def step(g):
                        sp.wait_ge(added, g + 1)
                        sp.dma_start(dst[:, G * g:G * g + G, :], fin[g % 2][:]).then_inc(sent[g % 2], 16)

                    in_groups(step)
                    for p in (0, 1):
                        sp.wait_ge(sent[p], NG // 2 * 16)

            @block.gpsimd
            def _(pool):
                def carry(f):
                    pool.wait_ge(normed, f + 1)
                    pool.tensor_tensor(slots(h, f), mine.rows(f)[:, :, 0, :], slots(h, f), ALU.add).then_inc(carried, 1)

                if last:
                    for f in range(AHEAD):
                        carry(f)

                def step(f):
                    wait(pool, x_turned, 2 * (f - 2))
                    mine.normalise(pool, f)
                    if last:
                        carry(f)

                in_groups(step, AHEAD)
                if following is not None:
                    pool.wait_ge(normed, NG)
                    for f in range(AHEAD):
                        following.normalise(pool, f)

            @block.scalar
            def _(act):

                def high(f):
                    for c in (0, 1):
                        act.wait_ge(x_turned, 2 * f + 1 + c)
                        if c == 0:
                            wait(act, h1_done, (f - FRONT) * U)
                        act.activation(xs[f % len(xs)][:, NPAIR * c:NPAIR * c + NPAIR, :], front(f)[c][:, 0:HALF].rearrange("p (b l) -> p b l", l=L),
                                       ACT.Copy).then_inc(x_high, 1)

                def router_hidden(f):
                    for c in (0, 1):
                        act.wait_ge(r_done, 2 * f + 1 + c)
                        wait(act, routed, f)
                        act.activation(rh[0:RH, NPAIR * c:NPAIR * c + NPAIR, :], front(f)[c][0:RH, 0:HALF].rearrange("p (b l) -> p b l", l=L),
                                       ACT.Relu, bias=W.br1[:]).then_inc(r_ready, 1)

                def exponents(n):
                    act.wait_ge(lg_read, 2 * n + 2)
                    act.activation(ev[:], lg[n % 2][:], ACT.Exp).then_inc(exp_a, 1)

                def weight_of_second(n):
                    act.wait_ge(exp_in, n + 1)
                    if last:
                        act.activation(small[:, 3, :], small[:, 2, :], ACT.Tanh, scale=-0.5).then_inc(exp_b, 1)
                    else:
                        act.activation(small[:, 4, :], small[:, 3, :], ACT.Exp).then_inc(exp_b, 1)

                def combine(g):
                    act.wait_ge(c_turned, g + 1)
                    wait(act, o_done, g - 1)
                    act.activation(ct[g % 2][0:NR, :, :], a_bank[1][0:NR, 0:G * L // 2].bitcast(BF16).rearrange("p (b l) -> p b l", l=L),
                                   ACT.Copy).then_inc(c_ready, 1)

                def hidden1(g, u):
                    n = g * U + u
                    act.wait_ge(h1_done, n + 1)
                    wait(act, hm_ready if last else h2_done, n + 1 - RING)
                    act.activation(h1[n % RING][:], h1_bank[u % 2][:, 0:HALF], ACT.Gelu if last else ACT.Relu,
                                   bias=W.b1[:, u // 2:u // 2 + 1]).then_inc(h1_ready, 1)

                def hidden2(g, u):
                    n = g * U + u
                    act.wait_ge(h2_done, n + 1)
                    wait(act, hm_ready, n + 1 - RING)
                    act.activation(h2[n % RING][:], h2_bank[u % 2][:, 0:HALF], ACT.Relu, bias=W.b2[:, u // 2:u // 2 + 1]).then_inc(h2_ready, 1)

                def output(g):
                    act.wait_ge(o_done, g + 1)
                    wait(act, o_turned, g)
                    act.activation(osb[:], o_bank[:, 0:HALF], ACT.Copy).then_inc(o_ready, 1)

                high(0)
                high(1)
                act.activation(unused[:], W.first[:, 0:1], ACT.Gelu if last else ACT.Exp)
                if not last:
                    router_hidden(0)
                    router_hidden(1)
                    exponents(0)
                high(2)
                weight_of_second(0)
                if not last:
                    router_hidden(2)
                combine(0)
                hidden1(0, 0)

                def step(g):
                    f = g + FRONT
                    for u in range(U):
                        if g % 2 == 0 and u == 4 and exists(g + 2) and not last:
                            exponents(g // 2 + 1)
                        if (g % 2, u) == ((0, 6) if last and g == 0 else SECOND) and exists(g // 2 * 2 + 2):
                            weight_of_second(g // 2 + 1)
                        if u == LAST and TURN[g % 2] < LAST and exists(g + 1):
                            combine(g + 1)
                        if u < LAST:
                            hidden1(g, u + 1)
                        elif exists(g + 1):
                            hidden1(g + 1, 0)
                        if not last:
                            hidden2(g, u)
                        if ahead(g, u, 0):
                            high(ahead(g, u, 0))
                        if ahead(g, u, 1) and not last:
                            router_hidden(ahead(g, u, 1))
                        if u == 1 and exists(g - 1):
                            output(g - 1)
                        if u == LAST and TURN[g % 2] == LAST and exists(g + 1):
                            combine(g + 1)
                    LayerNorm.after_act(act, g, mine, following)

                in_groups(step)
                output(NG - 1)

            @block.tensor
            def _(pe):
                def turn(f):
                    pe.wait_ge(normed, f + 1)
                    if f > 1:
                        pe.wait_ge(lg_read, f if f > 2 else 1)
                    wait(pe, c_ready, max(f + 1 - FRONT, 1 if f >= AHEAD else 0))
                    for c in (0, 1):
                        for j in range(NPAIR):
                            b = NPAIR * c + j
                            mm = pe.transpose(front(f)[c][:, L * j:L * j + L], mine.rows(f)[:, b].rearrange("p a d -> p (a d)"), ident[0:L, 0:L])
                        mm.then_inc(x_turned, 1)

                def router(f):
                    for c in (0, 1):
                        pe.wait_ge(x_ready, 2 * f + 1 + c)
                        x = xs[f % len(xs)][:, NPAIR * c:NPAIR * c + NPAIR, :]
                        pe.matmul(front(f)[c][:, 0:HALF], W.wr_hi[:], x, start=True, stop=False)
                        pe.matmul(front(f)[c][:, 0:HALF], W.wr_lo[:], x, start=False, stop=True).then_inc(r_done, 1)

                def logits(f):
                    if last:
                        pe.wait_ge(x_ready, 2 * f + 2)
                    else:
                        pe.wait_ge(r_ready, 2 * f + 2)
                    for b in range(G):
                        o = front(f)[0][0:L, D * b:D * b + D]
                        if last:
                            mm = pe.matmul(o, xs[f % len(xs)][:, b, :], W.wr[:], start=True, stop=True)
                        else:
                            mm = pe.matmul(o, rh[:, b, :], W.wr2[:], start=True, stop=True)
                    mm.then_inc(routed, 1)

                def turn_combine(g):
                    pe.wait_ge(cp_ready, g // 2 + 1)
                    for b in range(G):
                        mm = pe.transpose(a_bank[1][0:NR, b * L // 2:(b + 1) * L // 2].bitcast(BF16),
                                          cp[:, G * (g % 2) + b].rearrange("p i j e -> p (i j e)"), ident16[0:L, 0:L])
                    mm.then_inc(c_turned, 1)

                def layer1(g, u):
                    n = g * U + u
                    k, c = u // 2, u % 2
                    wait(pe, h1_ready, n - 1 if last else n)
                    x = xs[g % len(xs)][:, NPAIR * c:NPAIR * c + NPAIR, :]
                    o = h1_bank[u % 2][:, 0:HALF]
                    pe.matmul(o, W.w1_hi[:, 2 * k:2 * k + 2, :], x, start=True, stop=False)
                    pe.matmul(o, W.w1_lo[:, 2 * k:2 * k + 2, :], x, start=False, stop=True).then_inc(h1_done, 1)

                def spread(g, u):
                    n = g * U + u
                    k, c = u // 2, u % 2
                    pe.wait_ge(c_ready, g + 1)
                    wait(pe, hm_ready, n + 1 - len(cb_bank))
                    pe.matmul(cb_bank[n % len(cb_bank)][:, 0:HALF], W.sel[:, 128 * k:128 * k + 128], ct[g % 2][:, NPAIR * c:NPAIR * c + NPAIR, :],
                              start=True, stop=True).then_inc(cb_done, 1)

                def layer2(g, u):
                    n = g * U + u
                    pe.wait_ge(h1_ready, n + 1)
                    wait(pe, h2_ready, n - 1)
                    pe.matmul(h2_bank[u % 2][:, 0:HALF], W.w2[:, u // 2, :], h1[n % RING][:], start=True, stop=True).then_inc(h2_done, 1)

                def sum_pair(g, k):
                    pe.wait_ge(hm_ready, g * U + 2 * k + 2)
                    if k == 0:
                        wait(pe, o_ready, g)
                    for c in (0, 1):
                        mm = pe.matmul(o_bank[c * D:(c + 1) * D, 0:HALF], W.wo[:, k, :], hm[2 * k + c][:], start=(k == 0), stop=False)
                    mm.then_inc(o_pairs, 1)

                def finish_sum(g):
                    sum_pair(g, NP - 1)
                    for c in (0, 1):
                        mm = pe.matmul(o_bank[c * D:(c + 1) * D, 0:HALF], W.bo[:], ct[g % 2][:, NPAIR * c:NPAIR * c + NPAIR, :],
                                       start=False, stop=True)
                    mm.then_inc(o_done, 1)

                def turn_output(g):
                    pe.wait_ge(o_ready, g + 1)
                    f = g + 1 + FRONT
                    if g == NG - 1:
                        pe.wait_ge(added, g)
                    if exists(f):
                        pe.wait_ge(x_ready if last else r_ready, 2 * f + 2)
                    else:
                        pe.wait_ge(c_ready, min(g + 2, NG))
                    for j in range(NPAIR):
                        mm = pe.transpose(a_bank[1][0:L, 128 * j:128 * j + 128], osb[:, L * j:L * j + L], ident[:])
                    mm.then_inc(o_turned, 1)

                turn(0)
                turn(1)
                if not last:
                    router(0)
                    router(1)
                logits(0)
                logits(1)
                turn(2)
                if not last:
                    router(2)
                logits(2)
                pe.wait_ge(x_ready if last else r_ready, 2 * AHEAD)
                turn_combine(0)
                layer1(0, 0)

                def step(g):
                    f = g + FRONT
                    for u in range(U):
                        if u < LAST:
                            layer1(g, u + 1)
                        elif exists(g + 1):
                            layer1(g + 1, 0)
                        if not last:
                            layer2(g, u)
                        if ahead(g, u, 0):
                            turn(ahead(g, u, 0))
                        spread(g, u)
                        if ahead(g, u, 1) and not last:
                            router(ahead(g, u, 1))
                        if ahead(g, u, 2):
                            logits(ahead(g, u, 2))
                        if u == 1 and exists(g - 1):
                            finish_sum(g - 1)
                        if u == 3 and exists(g - 1):
                            turn_output(g - 1)
                        if u % 2 == 1 and u >= 3:
                            sum_pair(g, (u - 3) // 2)
                        if u == TURN[g % 2] and exists(g + 1):
                            wait(pe, added, g)
                            if exists(f):
                                pe.wait_ge(x_ready if last else r_ready, 2 * f + 2)
                            turn_combine(g + 1)

                in_groups(step)
                finish_sum(NG - 1)
                turn_output(NG - 1)

            @block.vector
            def _(dve):
                ch = Chain(dve, chain)

                def low(f):
                    for c in (0, 1):
                        dve.wait_ge(x_high, 2 * f + 1 + c)
                        x = xs[f % len(xs)][D:128, NPAIR * c:NPAIR * c + NPAIR, :]
                        dve.tensor_tensor(x, front(f)[c][D:128, 0:HALF].rearrange("p (b l) -> p b l", l=L), x.bitcast(F32),
                                          ALU.subtract).then_inc(x_ready, 1)

                def wide(t, n=2 * G):
                    return t.unsqueeze(2).broadcast_to([L, n, E])

                firsts = W.first[:].unsqueeze(1).broadcast_to([L, 2 * G, E])

                def take_logits(f):
                    dve.wait_ge(routed, f + 1)
                    columns = front(f)[0][0:L, :].rearrange("p (b d) -> p b d", d=D)
                    here = lg[f // 2 % 2][:, G * (f % 2):G * (f % 2) + G, :]
                    if last:
                        ch(dve.tensor_copy(here, columns[:, :, 0:E]))
                        dve.tensor_tensor(here, columns[:, :, E:2 * E], here, ALU.add).then_inc(lg_read, 1)
                        return
                    bank = columns[:, :, 0:E]
                    ch(dve.tensor_reduce(top[:, f % 2, :], bank, AX_X, ALU.max))
                    dve.tensor_tensor(here, bank, wide(top[:, f % 2, :], G), ALU.subtract).then_inc(lg_read, 1)

                def route(n, k):
                    src = lg[n % 2] if last else ev
                    second = small[:, 2, :]
                    ch.settle()
                    if k == 0:
                        dve.wait_ge(lg_read, 2 * n + 2)
                        if last:
                            ch(dve.tensor_reduce(small[:, 0, :], src[:], AX_X, ALU.max))
                            ch(dve.tensor_tensor(src[:], src[:], wide(small[:, 0, :]), ALU.subtract))
                            ch(dve.scalar_tensor_tensor(idx[:], src[:], 0.0, firsts, ALU.is_ge, ALU.mult))
                        else:
                            dve.wait_ge(exp_a, n + 1)
                            ch.mark(dve.tensor_reduce(small[:, 5, :], ev[:], AX_X, ALU.add))
                            ch(dve.scalar_tensor_tensor(idx[:], ev[:], 1.0, firsts, ALU.is_ge, ALU.mult))
                        ch(dve.tensor_reduce(small[:, 1, :], idx[:], AX_X, ALU.max))
                        ch.mark(dve.tensor_tensor(s1[:], idx[:], wide(small[:, 1, :]), ALU.is_equal))
                    if k == 1:
                        off = -BIG if last else -4.0
                        if not last:
                            ch.mark(dve.reciprocal(small[:, 6, :], small[:, 5, :]))
                        ch(dve.scalar_tensor_tensor(rest[:], s1[:], off, src[:], ALU.mult, ALU.add))
                        ins = dve.tensor_reduce(second, rest[:], AX_X, ALU.max)
                        if last:
                            ins.then_inc(exp_in, 1)
                            dve.wait_ge(exp_in, n + 1)
                        else:
                            ch(ins)
                            dve.scalar_tensor_tensor(small[:, 3, :], second, -1.0, small[:, 6, :], ALU.add, ALU.mult).then_inc(exp_in, 1)
                        ch.mark(dve.tensor_tensor(idx[:], rest[:], wide(second), ALU.subtract))
                    if k == 2:
                        ch(dve.scalar_tensor_tensor(rest[:], idx[:], 0.0, firsts, ALU.is_ge, ALU.mult))
                        ch(dve.tensor_reduce(small[:, 1, :], rest[:], AX_X, ALU.max))
                        ch.mark(dve.tensor_tensor(s2[:], rest[:], wide(small[:, 1, :]), ALU.is_equal))
                    if k == 3:
                        dve.wait_ge(exp_b, n + 1)
                        if last:
                            ch.mark(dve.tensor_scalar(small[:, 6, :], small[:, 3, :], 0.5, 0.5, ALU.mult, ALU.add))
                            ch.mark(dve.tensor_scalar(small[:, 7, :], small[:, 3, :], -0.5, 0.5, ALU.mult, ALU.add))
                        else:
                            ch(dve.tensor_scalar(small[:, 5, :], small[:, 4, :], 1.0, None, ALU.add))
                            ch(dve.reciprocal(small[:, 6, :], small[:, 5, :]))
                            ch.mark(dve.tensor_tensor(small[:, 7, :], small[:, 4, :], small[:, 6, :], ALU.mult))
                    if k == 4:
                        ch.mark(dve.tensor_tensor(s1[:], s1[:], wide(small[:, 6, :]), ALU.mult))
                        ch(dve.tensor_tensor(s2[:], s2[:], wide(small[:, 7, :]), ALU.mult))
                        ch.mark(dve.tensor_tensor(cw[:], s1[:], s2[:], ALU.add))
                    if k >= 5:
                        i = k - 5
                        wait(dve, c_turned, 2 * n)
                        ins = dve.tensor_copy(cp[:, :, i, :, 0:E], (cw if i == 0 else rest)[:].unsqueeze(2).broadcast_to([L, 2 * G, 3, E]))
                        if i == 2:
                            ins.then_inc(cp_ready, 1)
                        else:
                            ch(ins)
                            ch.mark(dve.tensor_tensor(rest[:], (rest if i else cw)[:], cp[:, :, i, 0, 0:E], ALU.subtract))

                def weigh(g, u):
                    n = g * U + u
                    dve.wait_ge(cb_done, n + 1)
                    dve.wait_ge(h1_ready if last else h2_ready, n + 1)
                    if g > 0:
                        dve.wait_ge(o_pairs, (g - 1) * NP + u // 2 + 1)
                    src = h1 if last else h2
                    dve.tensor_tensor(hm[u][:], cb_bank[n % len(cb_bank)][:, 0:HALF], src[n % RING][:], ALU.mult).then_inc(hm_ready, 1)

                def residual(g):
                    p = g % 2
                    dve.wait_ge(o_turned, g + 1)
                    src = a_bank[1][0:L, :].rearrange("p (j c d) -> p c j d", c=2, d=D)
                    for c in (0, 1):
                        here = h[:, G * g + NPAIR * c:G * g + NPAIR * c + NPAIR, :]
                        dst = here
                        if last:
                            if c == 0:
                                dve.wait_ge(carried, g + 1)
                                if g >= 2:
                                    dve.wait_ge(sent[p], g // 2 * 16)
                            dst = fin[p][:, NPAIR * c:NPAIR * c + NPAIR, :]
                        ins = dve.tensor_tensor(dst, src[:, c], here, ALU.add)
                        if c == 1:
                            ins.then_inc(added, 1)

                def statistics(g, b0, b1):
                    dve.wait_ge(added, g + 1)
                    for b in range(b0, b1):
                        dve.bn_stats(slot(stats, g, b), slot(h, g, b))

                low(0)
                low(1)
                take_logits(0)
                take_logits(1)
                for k in range(8):
                    route(0, k)
                    if k == 1:
                        low(2)
                    if k == 4:
                        take_logits(2)

                def step(g):
                    n = g // 2 + 1
                    for u in range(U):
                        if ahead(g, u, 0) and not last:
                            low(ahead(g, u, 0))
                        if ahead(g, u, TAKE):
                            take_logits(ahead(g, u, TAKE))
                        if u == RESIDUAL and exists(g - 1):
                            residual(g - 1)
                        weigh(g, u)
                        if ahead(g, u, 0) and last:
                            low(ahead(g, u, 0))
                        if u in STATISTICS:
                            i = STATISTICS.index(u)
                            k = g - 3 + i // 2 if g % 2 == 0 else g - 2
                            if exists(k) and (g % 2 == 0 or (g == NG - 1 and i < 2)):
                                statistics(k, 4 * (i % 2), 4 * (i % 2) + 4)
                        if exists(2 * n):
                            for k in FIRST_ROUTE.get(u, ()) if last and g == 0 else ROUTE.get((g % 2, u), ()):
                                route(n, k)
                    LayerNorm.after_dve(dve, g, mine, following)

                in_groups(step)
                if not last:
                    statistics(NG - 2, 0, G)
                residual(NG - 1)


_INS = [
    "x", "L0_tok_weight", "L0_tok_bias", "L0_attn_Wq", "L0_attn_Wk", "L0_attn_Wv", "L0_attn_Wo",
    "L0_ffn_router_w1", "L0_ffn_router_b1", "L0_ffn_router_w2", "L0_ffn_router_b2",
    "L0_ffn_expert_w1", "L0_ffn_expert_b1", "L0_ffn_expert_w2", "L0_ffn_expert_b2", "L0_ffn_expert_w3", "L0_ffn_expert_b3",
    "L1_attn_Wq_comp", "L1_attn_Wkv_comp", "L1_attn_Wqc", "L1_attn_Wqr", "L1_attn_Wkc", "L1_attn_Wkr", "L1_attn_Wv",
    "L1_ffn_router_w", "L1_ffn_w1", "L1_ffn_b1", "L1_ffn_w2", "L1_ffn_b2",
]


def kernel(**inputs):
    import concourse.bacc as _bacc
    from concourse.bass_utils import run_bass_kernel_spmd as _run

    nc = _bacc.Bacc("TRN2", target_bir_lowering=False, num_devices=1)
    arrays, A = {}, {}
    for name in _INS:
        a = np.ascontiguousarray(inputs[name])
        arrays[f"in_{name}_dram"] = a
        A[name] = nc.dram_tensor(f"in_{name}_dram", a.shape, mybir.dt.from_np(a.dtype), kind="ExternalInput").ap()
    for name, a in constants().items():
        arrays[f"{name}_dram"] = np.ascontiguousarray(a)
        A[name] = nc.dram_tensor(f"{name}_dram", a.shape, mybir.dt.from_np(a.dtype), kind="ExternalInput").ap()
    out = nc.dram_tensor("out_0_dram", (B, L, D), F32, kind="ExternalOutput").ap()
    build(nc, A, out)
    r = _run(nc, [arrays], core_ids=[0])
    return r.results[0]["out_0_dram"]
```
